# Optimizing a Trainium2 kernel written in Bass

```python
import numpy as np
import jax
import jax.numpy as jnp

def _softmax(x, axis=-1):
    return jax.nn.softmax(x, axis=axis)

def _gelu(x):
    return jax.nn.gelu(x, approximate=True)

def _silu(x):
    return jax.nn.silu(x)

def _sigmoid(x):
    return jax.nn.sigmoid(x)

def _layernorm(x, axis=-1, eps=1e-05):
    m = jnp.mean(x, axis=axis, keepdims=True)
    v = jnp.var(x, axis=axis, keepdims=True)
    return (x - m) / jnp.sqrt(v + eps)

def _scatter_add(tgt, idx, src, axis=0):
    return tgt.at[idx].add(src)

def _segment_sum(src, seg, n):
    return jax.ops.segment_sum(src, seg, n)
kernel_name = 'mk_perceiver_d4_seqx_r8_e424c1'

def setup_inputs(seed: int=0):
    np.random.seed(seed)
    _w = jnp.asarray

    def _rec_inputs():
        import jax
        import jax.numpy as jnp
        _rk = jax.random.key(seed)
        x = -0.000125 + 0.9999 * jax.random.normal(jax.random.fold_in(_rk, 1), (2, 128, 256), jnp.float32)
        _lenS = 128 - jax.random.randint(jax.random.fold_in(_rk, 7), (2,), 0, max(1, 128 // 4) + 1, jnp.int32)
        _lenS2 = 2048 - jax.random.randint(jax.random.fold_in(_rk, 8), (2,), 0, max(1, 2048 // 4) + 1, jnp.int32)
        _ctx_2048P = jax.random.normal(jax.random.fold_in(_rk, 11), (2, 16, 256), jnp.float32)
        _ctx_2048c = jax.random.dirichlet(jax.random.fold_in(_rk, 511), 0.3 * jnp.ones((16,), jnp.float32), (2, 2048))
        _ctx_2048t = jnp.einsum('bsk,bkd->bsd', _ctx_2048c, _ctx_2048P)
        _ctx_2048t = _ctx_2048t * jax.lax.rsqrt(jnp.mean(jnp.square(_ctx_2048t)) + 1e-12) * 0.953939
        ctx_2048 = -1.52775e-05 + 0.999936 * (_ctx_2048t + 0.3 * jax.random.normal(jax.random.fold_in(_rk, 611), (2, 2048, 256), jnp.float32))
        _validS = jnp.arange(128)[None, :] < _lenS[:, None]
        _validS2 = jnp.arange(2048)[None, :] < _lenS2[:, None]
        _causal = jnp.tril(jnp.ones((128, 128), dtype=bool))
        mask_BxS2_ik0 = jnp.where(jnp.broadcast_to(_validS2[:, :], (2, 2048)), 0, 1).astype(jnp.int32)
        mask_Bx1xSxS_fk0 = jnp.where(jnp.broadcast_to(_validS[:, None, None, :], (2, 1, 128, 128)), -1000000000.0, 0.0).astype(jnp.float32)
        mask_BxS2_ff1 = jnp.where(jnp.ones((2, 2048), dtype=bool), 1.0, 0.0).astype(jnp.float32)
        return (x, ctx_2048, mask_BxS2_ik0, mask_Bx1xSxS_fk0, mask_BxS2_ff1)
    x, ctx_2048, mask_BxS2_ik0, mask_Bx1xSxS_fk0, mask_BxS2_ff1 = _rec_inputs()

    def _L0_xattn_setup():
        import jax, jax.numpy as jnp
        import numpy as np
        EPS = 1e-06
        NUM_HEADS = 16

        def _feature_map(x):
            return jnp.where(x > 0, x + 1.0, jnp.exp(x))
        key = jax.random.key(seed)
        ks = jax.random.split(key, 7)
        B, L, S, D = (4, 512, 512, 256)
        sc = 1.0 / np.sqrt(D)
        return {'query': jax.random.normal(ks[0], (B, L, D), jnp.float32), 'kv': jax.random.normal(ks[1], (B, S, D), jnp.float32), 'Wq': jax.random.normal(ks[2], (D, D), jnp.float32) * sc, 'Wg': jax.random.normal(ks[3], (D, D), jnp.float32) * sc, 'bg': jnp.ones((D,), jnp.float32), 'Wkv': jax.random.normal(ks[4], (2 * D, D), jnp.float32) * sc, 'Wo': jax.random.normal(ks[5], (D, D), jnp.float32) * sc}
    _L0_xattn_all = _L0_xattn_setup()
    _L0_xattn_in = {k: v for k, v in _L0_xattn_all.items() if k in ('Wq', 'Wg', 'bg', 'Wkv', 'Wo')}
    del _L0_xattn_all

    def _L0_attn_setup():
        import jax, jax.numpy as jnp
        import numpy as np
        D_MODEL = 256
        N_HEADS = 16
        D_K = D_MODEL // N_HEADS
        EPS = 1e-06
        key = jax.random.key(seed)
        ks = jax.random.split(key, 9)
        s = 1.0 / np.sqrt(D_MODEL)
        return {'x': jax.random.normal(ks[0], (4, 512, D_MODEL), dtype=jnp.float32), 'Wq': jax.random.normal(ks[1], (D_MODEL, D_MODEL), dtype=jnp.float32) * s, 'bq': jnp.zeros((D_MODEL,), dtype=jnp.float32), 'Wk': jax.random.normal(ks[2], (D_MODEL, D_MODEL), dtype=jnp.float32) * s, 'bk': jnp.zeros((D_MODEL,), dtype=jnp.float32), 'Wv': jax.random.normal(ks[3], (D_MODEL, D_MODEL), dtype=jnp.float32) * s, 'bv': jnp.zeros((D_MODEL,), dtype=jnp.float32), 'Wo': jax.random.normal(ks[4], (D_MODEL, D_MODEL), dtype=jnp.float32) * s, 'bo': jnp.zeros((D_MODEL,), dtype=jnp.float32)}
    _L0_attn_all = _L0_attn_setup()
    _L0_attn_in = {k: v for k, v in _L0_attn_all.items() if k in ('Wq', 'bq', 'Wk', 'bk', 'Wv', 'bv', 'Wo', 'bo')}
    del _L0_attn_all

    def _L0_ffn_setup():
        import jax, jax.numpy as jnp
        import numpy as np
        B, S, D, H = (4, 256, 256, 1024)

        def fwht(x):
            orig_shape = x.shape
            n = orig_shape[-1]
            x = x.reshape(-1, n)
            h = 1
            while h < n:
                xb = x.reshape(-1, n // (2 * h), 2, h)
                a = xb[:, :, 0, :]
                b = xb[:, :, 1, :]
                x = jnp.stack([a + b, a - b], axis=2).reshape(-1, n)
                h *= 2
            scale = jnp.asarray(1.0 / np.sqrt(n), dtype=x.dtype)
            return (x * scale).reshape(orig_shape)
        key = jax.random.key(seed)
        kx, k1, k2, k3 = jax.random.split(key, 4)
        x = jax.random.normal(kx, (B, S, D), dtype=jnp.float32)
        W1 = jax.random.normal(k1, (H, D), dtype=jnp.float32) * (1.0 / np.sqrt(D))
        W2 = jax.random.normal(k2, (D, H), dtype=jnp.float32) * (1.0 / np.sqrt(H))
        W3 = jax.random.normal(k3, (H, D), dtype=jnp.float32) * (1.0 / np.sqrt(D))
        return {'x': x, 'W1': W1, 'W2': W2, 'W3': W3}
    _L0_ffn_all = _L0_ffn_setup()
    _L0_ffn_in = {k: v for k, v in _L0_ffn_all.items() if k in ('W1', 'W2', 'W3')}
    del _L0_ffn_all

    def _L1_xattn_setup():
        import jax, jax.numpy as jnp
        import numpy as np
        import math
        H = 256
        NH = 16
        HD = H // NH
        EPS_LN = 1e-05
        RES_SCALE_MAX = 0.3

        def _nan_clean(x, lim=10000.0):
            return jnp.nan_to_num(x, nan=0.0, posinf=lim, neginf=-lim)
        key = jax.random.key(seed)
        ks = jax.random.split(key, 12)
        B, S, T = (4, 256, 32)
        std = 1.0 / math.sqrt(H)
        return {'hidden_states': jax.random.normal(ks[0], (B, S, H), jnp.float32), 'audio_tokens': jax.random.normal(ks[1], (B, T, H), jnp.float32), 'attention_mask': jax.random.randint(ks[2], (B, T), 0, 2, jnp.int32), 'Wq': jax.random.normal(ks[3], (H, H), jnp.float32) * std, 'bq': jnp.zeros((H,), jnp.float32), 'Wk': jax.random.normal(ks[4], (H, H), jnp.float32) * std, 'bk': jnp.zeros((H,), jnp.float32), 'Wv': jax.random.normal(ks[5], (H, H), jnp.float32) * std, 'bv': jnp.zeros((H,), jnp.float32), 'Wo': jax.random.normal(ks[6], (H, H), jnp.float32) * std, 'bo': jnp.zeros((H,), jnp.float32), 'ln_gamma': jnp.ones((H,), jnp.float32), 'ln_beta': jnp.zeros((H,), jnp.float32), 'residual_scale': jnp.float32(0.05)}
    _L1_xattn_all = _L1_xattn_setup()
    _L1_xattn_in = {k: v for k, v in _L1_xattn_all.items() if k in ('Wq', 'bq', 'Wk', 'bk', 'Wv', 'bv', 'Wo', 'bo', 'ln_gamma', 'ln_beta', 'residual_scale')}
    del _L1_xattn_all

    def _L1_attn_setup():
        import jax, jax.numpy as jnp
        import numpy as np
        B, S, H_DIM = (2, 256, 256)
        N_HEADS, D_HEAD = (16, 128)
        key = jax.random.key(seed)
        k1, k2, k3 = jax.random.split(key, 3)
        x = jax.random.normal(k1, (B, S, H_DIM), dtype=jnp.float32)
        w_qkv = jax.random.normal(k2, (H_DIM, 3 * N_HEADS * D_HEAD), dtype=jnp.float32) * 0.02
        w_o = jax.random.normal(k3, (N_HEADS * D_HEAD, H_DIM), dtype=jnp.float32) * 0.02
        return {'x': x, 'w_qkv': w_qkv, 'w_o': w_o}
    _L1_attn_all = _L1_attn_setup()
    _L1_attn_in = {k: v for k, v in _L1_attn_all.items() if k in ('w_qkv', 'w_o')}
    del _L1_attn_all

    def _L1_ffn_setup():
        import jax, jax.numpy as jnp
        import numpy as np
        EPS_NORM = 1e-06
        EPS_SCALE = 1e-05
        NUM_BITS = 8
        QP = 2 ** (NUM_BITS - 1) - 1
        QN = -2 ** (NUM_BITS - 1)

        def rms_norm(x, gamma):
            rms = jnp.sqrt(jnp.mean(x * x, axis=-1, keepdims=True) + EPS_NORM)
            return x / rms * gamma

        def activation_quant_8bit(x):
            scale = jnp.maximum(jnp.max(jnp.abs(x)), EPS_SCALE)
            x_scaled = x / scale * QP
            rounded = jnp.round(jnp.clip(x_scaled, QN, QP))
            x_quant = jax.lax.stop_gradient(rounded - x_scaled) + x_scaled
            return x_quant / QP * scale

        def weight_quant_ternary(w):
            scale = jnp.maximum(jnp.mean(jnp.abs(w)), EPS_SCALE)
            w_norm = w / scale
            w_q = jnp.round(jnp.clip(w_norm, -1.0, 1.0))
            return (jax.lax.stop_gradient(w_q - w_norm) + w_norm, scale)
        key = jax.random.key(seed)
        k1, k2 = jax.random.split(key)
        B, S, D_IN, D_OUT = (4, 512, 256, 256)
        x = jax.random.normal(k1, (B, S, D_IN), dtype=jnp.float32)
        bound = 1.0 / np.sqrt(D_IN)
        weight = jax.random.uniform(k2, (D_OUT, D_IN), dtype=jnp.float32, minval=-bound, maxval=bound)
        norm_weight = jnp.ones((D_IN,), dtype=jnp.float32)
        return {'x': x, 'weight': weight, 'norm_weight': norm_weight}
    _L1_ffn_all = _L1_ffn_setup()
    _L1_ffn_in = {k: v for k, v in _L1_ffn_all.items() if k in ('weight', 'norm_weight')}
    del _L1_ffn_all

    def _L2_xattn_setup():
        import jax, jax.numpy as jnp
        import numpy as np
        import math
        B, S, HID, H = (2, 256, 256, 32)
        D = HID // H
        AL = 10

        def _rope_tables(seq_len, dim, dtype):
            inv_freq = 1.0 / 10000.0 ** (np.arange(0, dim, 2, dtype=np.float32) / dim)
            t = np.arange(seq_len, dtype=np.float32)
            freqs = np.outer(t, inv_freq)
            emb = np.concatenate([freqs, freqs], -1)
            return (jnp.asarray(np.cos(emb), dtype), jnp.asarray(np.sin(emb), dtype))

        def _rotate_half(x):
            x1, x2 = jnp.split(x, 2, axis=-1)
            return jnp.concatenate([-x2, x1], axis=-1)
        key = jax.random.key(seed)
        ks = jax.random.split(key, 8)
        hidden_states = jax.random.normal(ks[0], (B, S, HID), dtype=jnp.float32)
        adapter = jax.random.normal(ks[1], (B, AL, HID), dtype=jnp.float32)
        causal = jnp.tril(jnp.ones((S, S), dtype=bool))
        attention_mask = jnp.broadcast_to(jnp.where(causal, 0.0, -1000000000.0).astype(jnp.float32)[None, None], (B, 1, S, S))
        scale = 0.02
        Wq = jax.random.normal(ks[2], (HID, HID), dtype=jnp.float32) * scale
        Wk = jax.random.normal(ks[3], (HID, HID), dtype=jnp.float32) * scale
        Wv = jax.random.normal(ks[4], (HID, HID), dtype=jnp.float32) * scale
        Wo = jax.random.normal(ks[5], (HID, HID), dtype=jnp.float32) * scale
        gate = jax.random.normal(ks[6], (1, H, 1, 1), dtype=jnp.float32) * 0.1
        return {'hidden_states': hidden_states, 'attention_mask': attention_mask, 'adapter': adapter, 'Wq': Wq, 'Wk': Wk, 'Wv': Wv, 'Wo': Wo, 'gate': gate}
    _L2_xattn_all = _L2_xattn_setup()
    _L2_xattn_in = {k: v for k, v in _L2_xattn_all.items() if k in ('Wq', 'Wk', 'Wv', 'Wo', 'gate')}
    del _L2_xattn_all

    def _L2_attn_setup():
        import jax, jax.numpy as jnp
        import numpy as np
        import math
        B, S, HID = (2, 256, 256)
        NH = 16
        QK_NOPE, QK_ROPE, KV_RANK, Q_RANK, V_DIM = (64, 64, 64, 64, 64)
        Q_HEAD = QK_NOPE + QK_ROPE
        ROPE_BASE = 10000.0
        FACTOR = 40.0
        BETA_FAST, BETA_SLOW = (32.0, 1.0)
        ORIG_MAX = 512
        MSCALE = 0.707
        SOFTMAX_SCALE = Q_HEAD ** (-0.5)

        def yarn_get_mscale(scale, mscale=1.0):
            if scale <= 1:
                return 1.0
            return 0.1 * mscale * math.log(scale) + 1.0

        def yarn_cos_sin(seq_len, dim):
            exponents = np.arange(0, dim, 2, dtype=np.float64) / dim
            freq_extra = 1.0 / ROPE_BASE ** exponents
            freq_inter = 1.0 / (FACTOR * ROPE_BASE ** exponents)

            def corr_dim(num_rot):
                return dim * math.log(ORIG_MAX / (num_rot * 2 * math.pi)) / (2 * math.log(ROPE_BASE))
            low = max(math.floor(corr_dim(BETA_FAST)), 0)
            high = min(math.ceil(corr_dim(BETA_SLOW)), dim - 1)
            if low == high:
                high = high + 0.001
            ramp = np.clip((np.arange(dim // 2, dtype=np.float64) - low) / (high - low), 0.0, 1.0)
            inv_freq_mask = 1.0 - ramp
            inv_freq = freq_inter * (1.0 - inv_freq_mask) + freq_extra * inv_freq_mask
            t = np.arange(seq_len, dtype=np.float64)
            freqs = np.outer(t, inv_freq)
            msc = yarn_get_mscale(FACTOR, MSCALE) / yarn_get_mscale(FACTOR, 0.0)
            emb = np.concatenate([freqs, freqs], axis=-1)
            return (jnp.asarray(np.cos(emb) * msc, jnp.float32), jnp.asarray(np.sin(emb) * msc, jnp.float32))

        def rms_norm(x, w, eps=1e-06):
            xf = x.astype(jnp.float32)
            var = jnp.mean(xf * xf, axis=-1, keepdims=True)
            return (xf * jax.lax.rsqrt(var + eps)).astype(x.dtype) * w

        def rotate_half(x):
            x1, x2 = jnp.split(x, 2, axis=-1)
            return jnp.concatenate([-x2, x1], axis=-1)

        def apply_rope(x, cos, sin):
            b, h, s, d = x.shape
            x = x.reshape(b, h, s, d // 2, 2).transpose(0, 1, 2, 4, 3).reshape(b, h, s, d)
            return x * cos + rotate_half(x) * sin
        key = jax.random.key(seed)
        ks = jax.random.split(key, 8)
        sc = 0.02
        return {'hidden_states': jax.random.normal(ks[0], (B, S, HID), jnp.float32), 'wq_a': jax.random.normal(ks[1], (HID, Q_RANK), jnp.float32) * sc, 'q_a_norm_w': jnp.ones((Q_RANK,), jnp.float32), 'wq_b': jax.random.normal(ks[2], (Q_RANK, NH * Q_HEAD), jnp.float32) * sc, 'wkv_a': jax.random.normal(ks[3], (HID, KV_RANK + QK_ROPE), jnp.float32) * sc, 'kv_a_norm_w': jnp.ones((KV_RANK,), jnp.float32), 'wkv_b': jax.random.normal(ks[4], (KV_RANK, NH * (QK_NOPE + V_DIM)), jnp.float32) * sc, 'wo': jax.random.normal(ks[5], (NH * V_DIM, HID), jnp.float32) * sc}
    _L2_attn_all = _L2_attn_setup()
    _L2_attn_in = {k: v for k, v in _L2_attn_all.items() if k in ('wq_a', 'q_a_norm_w', 'wq_b', 'wkv_a', 'kv_a_norm_w', 'wkv_b', 'wo')}
    del _L2_attn_all

    def _L2_ffn_setup():
        import jax, jax.numpy as jnp
        import numpy as np
        from jax import lax
        D_MODEL = 256
        D_CROSS = 1024
        D_RETR = 128
        D_PRIV = 128
        N_EXPERTS = 2048
        N_HEADS = 8
        K_PER_HEAD = 8
        NUM_KEYS = int(np.sqrt(N_EXPERTS))
        BATCH, SEQ = (2, 256)
        key = jax.random.key(seed)
        ks = jax.random.split(key, 10)
        s = 0.02
        return {'hidden_states': jax.random.normal(ks[0], (BATCH, SEQ, D_MODEL), jnp.float32), 'W_up': jax.random.normal(ks[1], (D_CROSS, D_MODEL), jnp.float32) * s, 'b_up': jnp.zeros((D_CROSS,), jnp.float32), 'W_down': jax.random.normal(ks[2], (D_PRIV, D_CROSS), jnp.float32) * s, 'b_down': jnp.zeros((D_PRIV,), jnp.float32), 'W_q': jax.random.normal(ks[3], (D_RETR * N_HEADS, D_PRIV), jnp.float32) * s, 'keys': jax.random.normal(ks[4], (N_HEADS, NUM_KEYS, 2, D_RETR // 2), jnp.float32) * s, 'down_embed': jax.random.normal(ks[5], (N_EXPERTS, D_PRIV), jnp.float32) * s, 'up_embed': jax.random.normal(ks[6], (N_EXPERTS, D_MODEL), jnp.float32) * s}
    _L2_ffn_all = _L2_ffn_setup()
    _L2_ffn_in = {k: v for k, v in _L2_ffn_all.items() if k in ('W_up', 'b_up', 'W_down', 'b_down', 'W_q', 'keys', 'down_embed', 'up_embed')}
    del _L2_ffn_all

    def _L3_xattn_setup():
        import jax, jax.numpy as jnp
        import numpy as np
        H = 256
        NH = 16
        HD = H // NH
        FD = 64
        key = jax.random.key(seed)
        ks = jax.random.split(key, 12)
        B, S = (4, 512)
        s = 1.0 / np.sqrt(H)
        sf = 1.0 / np.sqrt(HD)
        return {'query': jax.random.normal(ks[0], (B, S, H), jnp.float32), 'key': jax.random.normal(ks[1], (B, S, H), jnp.float32), 'value': jax.random.normal(ks[2], (B, S, H), jnp.float32), 'attention_mask': jnp.ones((B, S), jnp.float32), 'Wq': jax.random.normal(ks[3], (H, H), jnp.float32) * s, 'bq': jnp.zeros((H,), jnp.float32), 'Wk': jax.random.normal(ks[4], (H, H), jnp.float32) * s, 'bk': jnp.zeros((H,), jnp.float32), 'Wv': jax.random.normal(ks[5], (H, H), jnp.float32) * s, 'bv': jnp.zeros((H,), jnp.float32), 'Wqf': jax.random.normal(ks[6], (FD, HD), jnp.float32) * sf, 'Wkf': jax.random.normal(ks[7], (FD, HD), jnp.float32) * sf, 'Wo': jax.random.normal(ks[8], (H, H), jnp.float32) * s, 'bo': jnp.zeros((H,), jnp.float32)}
    _L3_xattn_all = _L3_xattn_setup()
    _L3_xattn_in = {k: v for k, v in _L3_xattn_all.items() if k in ('Wq', 'bq', 'Wk', 'bk', 'Wv', 'bv', 'Wqf', 'Wkf', 'Wo', 'bo')}
    del _L3_xattn_all

    def _L3_attn_setup():
        import jax, jax.numpy as jnp
        import numpy as np
        B, T, D, H = (2, 256, 256, 16)
        DK = D // H
        NEG = -1e+30
        key = jax.random.key(seed)
        kx, kq, kk, kv, ko = jax.random.split(key, 5)
        s = 0.02
        return {'x': jax.random.normal(kx, (B, T, D), jnp.float32), 'Wq': jax.random.normal(kq, (D, D), jnp.float32) * s, 'Wk': jax.random.normal(kk, (D, D), jnp.float32) * s, 'Wv': jax.random.normal(kv, (D, D), jnp.float32) * s, 'Wo': jax.random.normal(ko, (D, D), jnp.float32) * s}
    _L3_attn_all = _L3_attn_setup()
    _L3_attn_in = {k: v for k, v in _L3_attn_all.items() if k in ('Wq', 'Wk', 'Wv', 'Wo')}
    del _L3_attn_all

    def _L3_ffn_setup():
        import jax, jax.numpy as jnp
        import numpy as np
        E, K, H, F = (64, 6, 256, 96)
        G, KG = (8, 4)
        SHARED_F = 96
        SCALE = 2.5
        T = 2 * 128
        CAP = 2 * (T * K // E)

        def _grouped_topk(logits, bias):
            scores = jax.nn.sigmoid(logits.astype(jnp.float32))
            scores_b = scores + bias[None, :]
            gs = scores_b.reshape(-1, G, E // G)
            group_scores = jnp.sum(jax.lax.top_k(gs, 2)[0], axis=-1)
            gidx = jax.lax.top_k(group_scores, KG)[1]
            rows = jnp.arange(group_scores.shape[0])[:, None]
            group_mask = jnp.zeros_like(group_scores).at[rows, gidx].set(1.0)
            score_mask = jnp.repeat(group_mask, E // G, axis=-1) > 0
            tmp = jnp.where(score_mask, scores_b, -jnp.inf)
            topk_ids = jax.lax.top_k(tmp, K)[1]
            topk_w = jnp.take_along_axis(scores, topk_ids, axis=-1)
            topk_w = topk_w / jnp.sum(topk_w, axis=-1, keepdims=True)
            return (topk_w * SCALE, topk_ids)

        def _routed_moe(x, topk_w, topk_ids, w_gate, w_up, w_down):
            Tn = x.shape[0]
            flat_e = topk_ids.reshape(-1)
            order = jnp.argsort(flat_e)
            se = flat_e[order]
            pos = jnp.arange(Tn * K) - jnp.searchsorted(se, se, side='left')
            tok = order // K
            valid = pos < CAP
            slot = jnp.where(valid, pos, CAP)
            buf = jnp.zeros((E, CAP + 1, H), x.dtype).at[se, slot].set(x[tok])[:, :CAP]
            h = jax.nn.silu(jnp.einsum('ech,ehf->ecf', buf, w_gate)) * jnp.einsum('ech,ehf->ecf', buf, w_up)
            out = jnp.einsum('ecf,efh->ech', h, w_down)
            gathered = out[se, jnp.minimum(pos, CAP - 1)] * valid.astype(x.dtype)[:, None]
            w = topk_w.reshape(-1)[order].astype(x.dtype)[:, None]
            return jax.ops.segment_sum(gathered * w, tok, num_segments=Tn)
        key = jax.random.key(seed)
        ks = jax.random.split(key, 9)
        s = 0.02
        return dict(hidden_states=jax.random.normal(ks[0], (2, 128, H), jnp.float32), gate_w=jax.random.normal(ks[1], (H, E), jnp.float32) * s, bias=jax.random.normal(ks[2], (E,), jnp.float32) * s, w_gate=jax.random.normal(ks[3], (E, H, F), jnp.float32) * s, w_up=jax.random.normal(ks[4], (E, H, F), jnp.float32) * s, w_down=jax.random.normal(ks[5], (E, F, H), jnp.float32) * s, ws_gate=jax.random.normal(ks[6], (H, SHARED_F), jnp.float32) * s, ws_up=jax.random.normal(ks[7], (H, SHARED_F), jnp.float32) * s, ws_down=jax.random.normal(ks[8], (SHARED_F, H), jnp.float32) * s)
    _L3_ffn_all = _L3_ffn_setup()
    _L3_ffn_in = {k: v for k, v in _L3_ffn_all.items() if k in ('gate_w', 'bias', 'w_gate', 'w_up', 'w_down', 'ws_gate', 'ws_up', 'ws_down')}
    del _L3_ffn_all
    return {'x': x, 'ctx_2048': ctx_2048, 'mask_BxS2_ik0': mask_BxS2_ik0, 'mask_Bx1xSxS_fk0': mask_Bx1xSxS_fk0, 'mask_BxS2_ff1': mask_BxS2_ff1, 'L0_xattn_Wq': _L0_xattn_in['Wq'], 'L0_xattn_Wg': _L0_xattn_in['Wg'], 'L0_xattn_bg': _L0_xattn_in['bg'], 'L0_xattn_Wkv': _L0_xattn_in['Wkv'], 'L0_xattn_Wo': _L0_xattn_in['Wo'], 'L0_attn_Wq': _L0_attn_in['Wq'], 'L0_attn_bq': _L0_attn_in['bq'], 'L0_attn_Wk': _L0_attn_in['Wk'], 'L0_attn_bk': _L0_attn_in['bk'], 'L0_attn_Wv': _L0_attn_in['Wv'], 'L0_attn_bv': _L0_attn_in['bv'], 'L0_attn_Wo': _L0_attn_in['Wo'], 'L0_attn_bo': _L0_attn_in['bo'], 'L0_ffn_W1': _L0_ffn_in['W1'], 'L0_ffn_W2': _L0_ffn_in['W2'], 'L0_ffn_W3': _L0_ffn_in['W3'], 'L1_xattn_Wq': _L1_xattn_in['Wq'], 'L1_xattn_bq': _L1_xattn_in['bq'], 'L1_xattn_Wk': _L1_xattn_in['Wk'], 'L1_xattn_bk': _L1_xattn_in['bk'], 'L1_xattn_Wv': _L1_xattn_in['Wv'], 'L1_xattn_bv': _L1_xattn_in['bv'], 'L1_xattn_Wo': _L1_xattn_in['Wo'], 'L1_xattn_bo': _L1_xattn_in['bo'], 'L1_xattn_ln_gamma': _L1_xattn_in['ln_gamma'], 'L1_xattn_ln_beta': _L1_xattn_in['ln_beta'], 'L1_xattn_residual_scale': _L1_xattn_in['residual_scale'], 'L1_attn_w_qkv': _L1_attn_in['w_qkv'], 'L1_attn_w_o': _L1_attn_in['w_o'], 'L1_ffn_weight': _L1_ffn_in['weight'], 'L1_ffn_norm_weight': _L1_ffn_in['norm_weight'], 'L2_xattn_Wq': _L2_xattn_in['Wq'], 'L2_xattn_Wk': _L2_xattn_in['Wk'], 'L2_xattn_Wv': _L2_xattn_in['Wv'], 'L2_xattn_Wo': _L2_xattn_in['Wo'], 'L2_xattn_gate': _L2_xattn_in['gate'], 'L2_attn_wq_a': _L2_attn_in['wq_a'], 'L2_attn_q_a_norm_w': _L2_attn_in['q_a_norm_w'], 'L2_attn_wq_b': _L2_attn_in['wq_b'], 'L2_attn_wkv_a': _L2_attn_in['wkv_a'], 'L2_attn_kv_a_norm_w': _L2_attn_in['kv_a_norm_w'], 'L2_attn_wkv_b': _L2_attn_in['wkv_b'], 'L2_attn_wo': _L2_attn_in['wo'], 'L2_ffn_W_up': _L2_ffn_in['W_up'], 'L2_ffn_b_up': _L2_ffn_in['b_up'], 'L2_ffn_W_down': _L2_ffn_in['W_down'], 'L2_ffn_b_down': _L2_ffn_in['b_down'], 'L2_ffn_W_q': _L2_ffn_in['W_q'], 'L2_ffn_keys': _L2_ffn_in['keys'], 'L2_ffn_down_embed': _L2_ffn_in['down_embed'], 'L2_ffn_up_embed': _L2_ffn_in['up_embed'], 'L3_xattn_Wq': _L3_xattn_in['Wq'], 'L3_xattn_bq': _L3_xattn_in['bq'], 'L3_xattn_Wk': _L3_xattn_in['Wk'], 'L3_xattn_bk': _L3_xattn_in['bk'], 'L3_xattn_Wv': _L3_xattn_in['Wv'], 'L3_xattn_bv': _L3_xattn_in['bv'], 'L3_xattn_Wqf': _L3_xattn_in['Wqf'], 'L3_xattn_Wkf': _L3_xattn_in['Wkf'], 'L3_xattn_Wo': _L3_xattn_in['Wo'], 'L3_xattn_bo': _L3_xattn_in['bo'], 'L3_attn_Wq': _L3_attn_in['Wq'], 'L3_attn_Wk': _L3_attn_in['Wk'], 'L3_attn_Wv': _L3_attn_in['Wv'], 'L3_attn_Wo': _L3_attn_in['Wo'], 'L3_ffn_gate_w': _L3_ffn_in['gate_w'], 'L3_ffn_bias': _L3_ffn_in['bias'], 'L3_ffn_w_gate': _L3_ffn_in['w_gate'], 'L3_ffn_w_up': _L3_ffn_in['w_up'], 'L3_ffn_w_down': _L3_ffn_in['w_down'], 'L3_ffn_ws_gate': _L3_ffn_in['ws_gate'], 'L3_ffn_ws_up': _L3_ffn_in['ws_up'], 'L3_ffn_ws_down': _L3_ffn_in['ws_down']}

def reference(x, ctx_2048, mask_BxS2_ik0, mask_Bx1xSxS_fk0, mask_BxS2_ff1, L0_xattn_Wq, L0_xattn_Wg, L0_xattn_bg, L0_xattn_Wkv, L0_xattn_Wo, L0_attn_Wq, L0_attn_bq, L0_attn_Wk, L0_attn_bk, L0_attn_Wv, L0_attn_bv, L0_attn_Wo, L0_attn_bo, L0_ffn_W1, L0_ffn_W2, L0_ffn_W3, L1_xattn_Wq, L1_xattn_bq, L1_xattn_Wk, L1_xattn_bk, L1_xattn_Wv, L1_xattn_bv, L1_xattn_Wo, L1_xattn_bo, L1_xattn_ln_gamma, L1_xattn_ln_beta, L1_xattn_residual_scale, L1_attn_w_qkv, L1_attn_w_o, L1_ffn_weight, L1_ffn_norm_weight, L2_xattn_Wq, L2_xattn_Wk, L2_xattn_Wv, L2_xattn_Wo, L2_xattn_gate, L2_attn_wq_a, L2_attn_q_a_norm_w, L2_attn_wq_b, L2_attn_wkv_a, L2_attn_kv_a_norm_w, L2_attn_wkv_b, L2_attn_wo, L2_ffn_W_up, L2_ffn_b_up, L2_ffn_W_down, L2_ffn_b_down, L2_ffn_W_q, L2_ffn_keys, L2_ffn_down_embed, L2_ffn_up_embed, L3_xattn_Wq, L3_xattn_bq, L3_xattn_Wk, L3_xattn_bk, L3_xattn_Wv, L3_xattn_bv, L3_xattn_Wqf, L3_xattn_Wkf, L3_xattn_Wo, L3_xattn_bo, L3_attn_Wq, L3_attn_Wk, L3_attn_Wv, L3_attn_Wo, L3_ffn_gate_w, L3_ffn_bias, L3_ffn_w_gate, L3_ffn_w_up, L3_ffn_w_down, L3_ffn_ws_gate, L3_ffn_ws_up, L3_ffn_ws_down):
    import jax
    import jax.numpy as jnp

    def _L0_xattn_ref(query, kv, Wq, Wg, bg, Wkv, Wo):
        import jax, jax.numpy as jnp
        import numpy as np
        EPS = 1e-06
        NUM_HEADS = 16

        def _feature_map(x):
            return jnp.where(x > 0, x + 1.0, jnp.exp(x))
        B, L, D = query.shape
        S = kv.shape[1]
        H = NUM_HEADS
        hd = D // H
        q = query @ Wq.T
        gate = jax.nn.sigmoid(query @ Wg.T + bg)
        kvp = kv @ Wkv.T
        k, v = jnp.split(kvp, 2, axis=-1)
        q = _feature_map(q.reshape(B, L, H, hd).transpose(0, 2, 1, 3))
        k = _feature_map(k.reshape(B, S, H, hd).transpose(0, 2, 1, 3))
        v = v.reshape(B, S, H, hd).transpose(0, 2, 1, 3)
        kv_summary = jnp.einsum('bhsd,bhse->bhde', k, v)
        k_sum = k.sum(axis=-2)
        z = 1.0 / (jnp.einsum('bhld,bhd->bhl', q, k_sum)[..., None] + EPS)
        attn = jnp.einsum('bhld,bhde->bhle', q, kv_summary) * z
        attn = attn.transpose(0, 2, 1, 3).reshape(B, L, D)
        out = attn * gate @ Wo.T
        return out

    def _L0_attn_ref(x, Wq, bq, Wk, bk, Wv, bv, Wo, bo):
        import jax, jax.numpy as jnp
        import numpy as np
        D_MODEL = 256
        N_HEADS = 16
        D_K = D_MODEL // N_HEADS
        EPS = 1e-06
        b, n, _ = x.shape
        h, d = (N_HEADS, D_K)

        def proj(W, bias):
            y = jnp.einsum('bnm,dm->bnd', x, W) + bias
            return y.reshape(b, n, h, d).transpose(0, 2, 1, 3)
        Q = jax.nn.relu(proj(Wq, bq))
        K = jax.nn.relu(proj(Wk, bk))
        V = proj(Wv, bv)
        pos = jnp.arange(n, dtype=x.dtype)
        decay = jnp.exp(-pos / n)[None, None, :, None]
        Q = Q * decay
        K = K * decay
        KV = jnp.einsum('bhnd,bhne->bhde', K, V)
        Ksum = K.sum(axis=2)
        Z = 1.0 / (jnp.einsum('bhnd,bhd->bhn', Q, Ksum)[..., None] + EPS)
        out = jnp.einsum('bhnd,bhde->bhne', Q, KV) * Z
        out = out.transpose(0, 2, 1, 3).reshape(b, n, h * d)
        return jnp.einsum('bnm,dm->bnd', out, Wo) + bo

    def _L0_ffn_ref(x, W1, W2, W3):
        import jax, jax.numpy as jnp
        import numpy as np
        B, S, D, H = (4, 256, 256, 1024)

        def fwht(x):
            orig_shape = x.shape
            n = orig_shape[-1]
            x = x.reshape(-1, n)
            h = 1
            while h < n:
                xb = x.reshape(-1, n // (2 * h), 2, h)
                a = xb[:, :, 0, :]
                b = xb[:, :, 1, :]
                x = jnp.stack([a + b, a - b], axis=2).reshape(-1, n)
                h *= 2
            scale = jnp.asarray(1.0 / np.sqrt(n), dtype=x.dtype)
            return (x * scale).reshape(orig_shape)
        up_gate = jnp.einsum('bsd,hd->bsh', x, W1)
        up_lin = jnp.einsum('bsd,hd->bsh', x, W3)
        hidden = jax.nn.silu(up_gate) * up_lin
        hidden = fwht(hidden)
        out = jnp.einsum('bsh,dh->bsd', hidden, W2)
        return out

    def _L1_xattn_ref(hidden_states, audio_tokens, attention_mask, Wq, bq, Wk, bk, Wv, bv, Wo, bo, ln_gamma, ln_beta, residual_scale):
        import jax, jax.numpy as jnp
        import numpy as np
        import math
        H = 256
        NH = 16
        HD = H // NH
        EPS_LN = 1e-05
        RES_SCALE_MAX = 0.3

        def _nan_clean(x, lim=10000.0):
            return jnp.nan_to_num(x, nan=0.0, posinf=lim, neginf=-lim)
        B, S, _ = hidden_states.shape
        T = audio_tokens.shape[1]
        hs = _nan_clean(hidden_states).astype(jnp.float32)
        at = _nan_clean(audio_tokens).astype(jnp.float32)

        def proj(x, W, b, L):
            y = x @ W.T + b
            return y.reshape(B, L, NH, HD).transpose(0, 2, 1, 3)
        q = _nan_clean(proj(hs, Wq, bq, S))
        k = _nan_clean(proj(at, Wk, bk, T))
        v = _nan_clean(proj(at, Wv, bv, T))
        scale = max(math.sqrt(HD), 1e-08)
        scores = jnp.einsum('bhsd,bhtd->bhst', q, k) / scale
        scores = jnp.clip(scores, -50.0, 50.0)
        scores = jnp.nan_to_num(scores, nan=0.0, posinf=50.0, neginf=-50.0)
        attend = (attention_mask.astype(jnp.float32) > 0.5)[:, None, None, :]
        scores = jnp.where(attend, scores, -10000.0)
        scores = jnp.clip(scores, -50.0, 50.0)
        probs = jax.nn.softmax(scores, axis=-1)
        probs = jnp.nan_to_num(probs, nan=0.0, posinf=1.0, neginf=0.0)
        probs = probs / (probs.sum(axis=-1, keepdims=True) + 1e-08)
        ctx = jnp.einsum('bhst,bhtd->bhsd', probs, v)
        ctx = ctx.transpose(0, 2, 1, 3).reshape(B, S, H)
        delta = _nan_clean(ctx @ Wo.T + bo)
        rs = jnp.clip(residual_scale, 0.0, RES_SCALE_MAX)
        delta = rs * delta
        mu = delta.mean(axis=-1, keepdims=True)
        var = jnp.mean((delta - mu) ** 2, axis=-1, keepdims=True)
        delta = (delta - mu) / jnp.sqrt(var + EPS_LN) * ln_gamma + ln_beta
        return delta

    def _L1_attn_ref(x, w_qkv, w_o):
        import jax, jax.numpy as jnp
        import numpy as np
        B, S, H_DIM = (2, 256, 256)
        N_HEADS, D_HEAD = (16, 128)
        b, s, _ = x.shape
        qkv = jnp.einsum('bsh,hf->bsf', x, w_qkv)
        qkv = qkv.reshape(b, s, 3, N_HEADS, D_HEAD)
        q, k, v = (qkv[:, :, 0], qkv[:, :, 1], qkv[:, :, 2])
        q = q.transpose(0, 2, 1, 3)
        k = k.transpose(0, 2, 1, 3)
        v = v.transpose(0, 2, 1, 3)
        scores = jnp.einsum('bhqd,bhkd->bhqk', q, k) / jnp.sqrt(jnp.float32(D_HEAD))
        probs = jax.nn.softmax(scores, axis=-1)
        values = jnp.einsum('bhqk,bhkd->bhkd', probs, v)
        values = values.transpose(0, 2, 1, 3).reshape(b, s, N_HEADS * D_HEAD)
        out = jnp.einsum('bsf,fh->bsh', values, w_o)
        return out

    def _L1_ffn_ref(x, weight, norm_weight):
        import jax, jax.numpy as jnp
        import numpy as np
        EPS_NORM = 1e-06
        EPS_SCALE = 1e-05
        NUM_BITS = 8
        QP = 2 ** (NUM_BITS - 1) - 1
        QN = -2 ** (NUM_BITS - 1)

        def rms_norm(x, gamma):
            rms = jnp.sqrt(jnp.mean(x * x, axis=-1, keepdims=True) + EPS_NORM)
            return x / rms * gamma

        def activation_quant_8bit(x):
            scale = jnp.maximum(jnp.max(jnp.abs(x)), EPS_SCALE)
            x_scaled = x / scale * QP
            rounded = jnp.round(jnp.clip(x_scaled, QN, QP))
            x_quant = jax.lax.stop_gradient(rounded - x_scaled) + x_scaled
            return x_quant / QP * scale

        def weight_quant_ternary(w):
            scale = jnp.maximum(jnp.mean(jnp.abs(w)), EPS_SCALE)
            w_norm = w / scale
            w_q = jnp.round(jnp.clip(w_norm, -1.0, 1.0))
            return (jax.lax.stop_gradient(w_q - w_norm) + w_norm, scale)
        xn = rms_norm(x, norm_weight)
        xq = activation_quant_8bit(xn)
        wq, w_scale = weight_quant_ternary(weight)
        out = jnp.einsum('bsi,oi->bso', xq, wq)
        return out * w_scale

    def _L2_xattn_ref(hidden_states, attention_mask, adapter, Wq, Wk, Wv, Wo, gate):
        import jax, jax.numpy as jnp
        import numpy as np
        import math
        B, S, HID, H = (2, 256, 256, 32)
        D = HID // H
        AL = 10

        def _rope_tables(seq_len, dim, dtype):
            inv_freq = 1.0 / 10000.0 ** (np.arange(0, dim, 2, dtype=np.float32) / dim)
            t = np.arange(seq_len, dtype=np.float32)
            freqs = np.outer(t, inv_freq)
            emb = np.concatenate([freqs, freqs], -1)
            return (jnp.asarray(np.cos(emb), dtype), jnp.asarray(np.sin(emb), dtype))

        def _rotate_half(x):
            x1, x2 = jnp.split(x, 2, axis=-1)
            return jnp.concatenate([-x2, x1], axis=-1)
        bsz, q_len, hid = hidden_states.shape
        n_heads = gate.shape[1]
        head_dim = hid // n_heads
        inv_sqrt_d = 1.0 / math.sqrt(head_dim)

        def split_heads(x, length):
            return x.reshape(bsz, length, n_heads, head_dim).transpose(0, 2, 1, 3)
        q = split_heads(hidden_states @ Wq, q_len)
        k = split_heads(hidden_states @ Wk, q_len)
        v = split_heads(hidden_states @ Wv, q_len)
        cos, sin = _rope_tables(q_len, head_dim, q.dtype)
        q = q * cos + _rotate_half(q) * sin
        k = k * cos + _rotate_half(k) * sin
        scores = jnp.einsum('bhqd,bhkd->bhqk', q, k) * inv_sqrt_d
        scores = scores + attention_mask
        scores = jnp.maximum(scores, jnp.finfo(scores.dtype).min)
        w = jax.nn.softmax(scores.astype(jnp.float32), axis=-1).astype(q.dtype)
        attn_output = jnp.einsum('bhqk,bhkd->bhqd', w, v)
        adapter_len = adapter.shape[1]
        a_k = split_heads(adapter @ Wk, adapter_len)
        a_v = split_heads(adapter @ Wv, adapter_len)
        a_scores = jnp.einsum('bhqd,bhkd->bhqk', q, a_k) * inv_sqrt_d
        a_scores = jnp.tanh(gate) * jax.nn.softmax(a_scores.astype(jnp.float32), axis=-1).astype(q.dtype)
        attn_output = attn_output + jnp.einsum('bhqk,bhkd->bhqd', a_scores, a_v)
        attn_output = attn_output.transpose(0, 2, 1, 3).reshape(bsz, q_len, hid)
        return attn_output @ Wo

    def _L2_attn_ref(hidden_states, wq_a, q_a_norm_w, wq_b, wkv_a, kv_a_norm_w, wkv_b, wo):
        import jax, jax.numpy as jnp
        import numpy as np
        import math
        B, S, HID = (2, 256, 256)
        NH = 16
        QK_NOPE, QK_ROPE, KV_RANK, Q_RANK, V_DIM = (64, 64, 64, 64, 64)
        Q_HEAD = QK_NOPE + QK_ROPE
        ROPE_BASE = 10000.0
        FACTOR = 40.0
        BETA_FAST, BETA_SLOW = (32.0, 1.0)
        ORIG_MAX = 512
        MSCALE = 0.707
        SOFTMAX_SCALE = Q_HEAD ** (-0.5)

        def yarn_get_mscale(scale, mscale=1.0):
            if scale <= 1:
                return 1.0
            return 0.1 * mscale * math.log(scale) + 1.0

        def yarn_cos_sin(seq_len, dim):
            exponents = np.arange(0, dim, 2, dtype=np.float64) / dim
            freq_extra = 1.0 / ROPE_BASE ** exponents
            freq_inter = 1.0 / (FACTOR * ROPE_BASE ** exponents)

            def corr_dim(num_rot):
                return dim * math.log(ORIG_MAX / (num_rot * 2 * math.pi)) / (2 * math.log(ROPE_BASE))
            low = max(math.floor(corr_dim(BETA_FAST)), 0)
            high = min(math.ceil(corr_dim(BETA_SLOW)), dim - 1)
            if low == high:
                high = high + 0.001
            ramp = np.clip((np.arange(dim // 2, dtype=np.float64) - low) / (high - low), 0.0, 1.0)
            inv_freq_mask = 1.0 - ramp
            inv_freq = freq_inter * (1.0 - inv_freq_mask) + freq_extra * inv_freq_mask
            t = np.arange(seq_len, dtype=np.float64)
            freqs = np.outer(t, inv_freq)
            msc = yarn_get_mscale(FACTOR, MSCALE) / yarn_get_mscale(FACTOR, 0.0)
            emb = np.concatenate([freqs, freqs], axis=-1)
            return (jnp.asarray(np.cos(emb) * msc, jnp.float32), jnp.asarray(np.sin(emb) * msc, jnp.float32))

        def rms_norm(x, w, eps=1e-06):
            xf = x.astype(jnp.float32)
            var = jnp.mean(xf * xf, axis=-1, keepdims=True)
            return (xf * jax.lax.rsqrt(var + eps)).astype(x.dtype) * w

        def rotate_half(x):
            x1, x2 = jnp.split(x, 2, axis=-1)
            return jnp.concatenate([-x2, x1], axis=-1)

        def apply_rope(x, cos, sin):
            b, h, s, d = x.shape
            x = x.reshape(b, h, s, d // 2, 2).transpose(0, 1, 2, 4, 3).reshape(b, h, s, d)
            return x * cos + rotate_half(x) * sin
        b, s, _ = hidden_states.shape
        q = rms_norm(hidden_states @ wq_a, q_a_norm_w) @ wq_b
        q = q.reshape(b, s, NH, Q_HEAD).transpose(0, 2, 1, 3)
        q_nope, q_pe = (q[..., :QK_NOPE], q[..., QK_NOPE:])
        ckv = hidden_states @ wkv_a
        compressed_kv, k_pe = (ckv[..., :KV_RANK], ckv[..., KV_RANK:])
        k_pe = k_pe.reshape(b, s, 1, QK_ROPE).transpose(0, 2, 1, 3)
        kv = rms_norm(compressed_kv, kv_a_norm_w) @ wkv_b
        kv = kv.reshape(b, s, NH, QK_NOPE + V_DIM).transpose(0, 2, 1, 3)
        k_nope, value_states = (kv[..., :QK_NOPE], kv[..., QK_NOPE:])
        cos, sin = yarn_cos_sin(s, QK_ROPE)
        cos, sin = (cos[None, None], sin[None, None])
        k_pe = jnp.broadcast_to(k_pe, (b, NH, s, QK_ROPE))
        q_pe = apply_rope(q_pe, cos, sin)
        k_pe = apply_rope(k_pe, cos, sin)
        query_states = jnp.concatenate([q_nope, q_pe], axis=-1)
        key_states = jnp.concatenate([k_nope, k_pe], axis=-1)
        attn = jnp.einsum('bhqd,bhkd->bhqk', query_states, key_states) * SOFTMAX_SCALE
        attn = jax.nn.softmax(attn.astype(jnp.float32), axis=-1).astype(query_states.dtype)
        out = jnp.einsum('bhqk,bhkd->bhqd', attn, value_states)
        out = out.transpose(0, 2, 1, 3).reshape(b, s, NH * V_DIM)
        return out @ wo

    def _L2_ffn_ref(hidden_states, W_up, b_up, W_down, b_down, W_q, keys, down_embed, up_embed):
        import jax, jax.numpy as jnp
        import numpy as np
        from jax import lax
        D_MODEL = 256
        D_CROSS = 1024
        D_RETR = 128
        D_PRIV = 128
        N_EXPERTS = 2048
        N_HEADS = 8
        K_PER_HEAD = 8
        NUM_KEYS = int(np.sqrt(N_EXPERTS))
        BATCH, SEQ = (2, 256)
        b, t, _ = hidden_states.shape
        act = jax.nn.silu
        h = act(jnp.einsum('btd,cd->btc', hidden_states, W_up) + b_up)
        h = jnp.einsum('btc,pc->btp', h, W_down) + b_down
        q = jnp.einsum('btp,rp->btr', h, W_q)
        q = q.reshape(b, t, 2, N_HEADS, D_RETR // 2).transpose(2, 0, 1, 3, 4)
        sim = jnp.einsum('pbthn,hkpn->pbthk', q, keys)
        scores, idx = lax.top_k(sim, K_PER_HEAD)
        sx, sy = (scores[0], scores[1])
        ix, iy = (idx[0], idx[1])
        all_scores = (sx[..., :, None] + sy[..., None, :]).reshape(b, t, N_HEADS, K_PER_HEAD * K_PER_HEAD)
        all_indices = (ix[..., :, None] * NUM_KEYS + iy[..., None, :]).reshape(b, t, N_HEADS, K_PER_HEAD * K_PER_HEAD)
        sc, pk = lax.top_k(all_scores, K_PER_HEAD)
        indices = jnp.take_along_axis(all_indices, pk, axis=-1)
        de = down_embed[indices]
        ue = up_embed[indices]
        z = jnp.einsum('btd,bthkd->bthk', h, de)
        z = act(z * jax.nn.softmax(sc, axis=-1))
        out = jnp.einsum('bthk,bthkd->btd', z, ue)
        return out

    def _L3_xattn_ref(query, key, value, attention_mask, Wq, bq, Wk, bk, Wv, bv, Wqf, Wkf, Wo, bo):
        import jax, jax.numpy as jnp
        import numpy as np
        H = 256
        NH = 16
        HD = H // NH
        FD = 64
        B, Sq, _ = query.shape
        Sk = key.shape[1]

        def heads(x, W, b, S):
            return (x @ W.T + b).reshape(B, S, NH, HD).transpose(0, 2, 1, 3)
        q = heads(query, Wq, bq, Sq)
        k = heads(key, Wk, bk, Sk)
        v = heads(value, Wv, bv, Sk)
        q_prime = jax.nn.relu(jnp.einsum('bhnd,fd->bhnf', q, Wqf))
        k_prime = jax.nn.relu(jnp.einsum('bhnd,fd->bhnf', k, Wkf))
        k_prime = k_prime * attention_mask[:, None, :, None]
        kv = jnp.einsum('bhnf,bhne->bhfe', k_prime, v)
        qkv = jnp.einsum('bhmf,bhfe->bhme', q_prime, kv)
        k_sum = jnp.sum(k_prime, axis=2)
        qk_sum = jnp.einsum('bhmf,bhf->bhm', q_prime, k_sum)[..., None]
        out = qkv / (qk_sum + 1e-08)
        out = out.transpose(0, 2, 1, 3).reshape(B, Sq, H)
        return out @ Wo.T + bo

    def _L3_attn_ref(x, Wq, Wk, Wv, Wo):
        import jax, jax.numpy as jnp
        import numpy as np
        B, T, D, H = (2, 256, 256, 16)
        DK = D // H
        NEG = -1e+30
        b, t, _ = x.shape
        scale = 1.0 / np.sqrt(DK).astype(np.float32)

        def split_heads(y):
            return y.reshape(b, t, H, DK).transpose(0, 2, 1, 3)
        Q = split_heads(x @ Wq.T)
        K = split_heads(x @ Wk.T)
        V = split_heads(x @ Wv.T)
        S = jnp.einsum('bhqd,bhkd->bhqk', Q, K) * scale
        causal = jnp.tril(jnp.ones((t, t), dtype=bool))
        S = jnp.where(causal, S, NEG)
        P = jax.nn.softmax(S, axis=-1)
        O = jnp.einsum('bhqk,bhkd->bhqd', P, V)
        out = O.transpose(0, 2, 1, 3).reshape(b, t, D) @ Wo.T
        return out

    def _L3_ffn_ref(hidden_states, gate_w, bias, w_gate, w_up, w_down, ws_gate, ws_up, ws_down):
        import jax, jax.numpy as jnp
        import numpy as np
        E, K, H, F = (64, 6, 256, 96)
        G, KG = (8, 4)
        SHARED_F = 96
        SCALE = 2.5
        T = 2 * 128
        CAP = 2 * (T * K // E)

        def _grouped_topk(logits, bias):
            scores = jax.nn.sigmoid(logits.astype(jnp.float32))
            scores_b = scores + bias[None, :]
            gs = scores_b.reshape(-1, G, E // G)
            group_scores = jnp.sum(jax.lax.top_k(gs, 2)[0], axis=-1)
            gidx = jax.lax.top_k(group_scores, KG)[1]
            rows = jnp.arange(group_scores.shape[0])[:, None]
            group_mask = jnp.zeros_like(group_scores).at[rows, gidx].set(1.0)
            score_mask = jnp.repeat(group_mask, E // G, axis=-1) > 0
            tmp = jnp.where(score_mask, scores_b, -jnp.inf)
            topk_ids = jax.lax.top_k(tmp, K)[1]
            topk_w = jnp.take_along_axis(scores, topk_ids, axis=-1)
            topk_w = topk_w / jnp.sum(topk_w, axis=-1, keepdims=True)
            return (topk_w * SCALE, topk_ids)

        def _routed_moe(x, topk_w, topk_ids, w_gate, w_up, w_down):
            Tn = x.shape[0]
            flat_e = topk_ids.reshape(-1)
            order = jnp.argsort(flat_e)
            se = flat_e[order]
            pos = jnp.arange(Tn * K) - jnp.searchsorted(se, se, side='left')
            tok = order // K
            valid = pos < CAP
            slot = jnp.where(valid, pos, CAP)
            buf = jnp.zeros((E, CAP + 1, H), x.dtype).at[se, slot].set(x[tok])[:, :CAP]
            h = jax.nn.silu(jnp.einsum('ech,ehf->ecf', buf, w_gate)) * jnp.einsum('ech,ehf->ecf', buf, w_up)
            out = jnp.einsum('ecf,efh->ech', h, w_down)
            gathered = out[se, jnp.minimum(pos, CAP - 1)] * valid.astype(x.dtype)[:, None]
            w = topk_w.reshape(-1)[order].astype(x.dtype)[:, None]
            return jax.ops.segment_sum(gathered * w, tok, num_segments=Tn)
        orig_shape = hidden_states.shape
        x = hidden_states.reshape(-1, H)
        router_logits = x @ gate_w
        topk_w, topk_ids = _grouped_topk(router_logits, bias)
        y = _routed_moe(x, topk_w, topk_ids, w_gate, w_up, w_down)
        shared = jax.nn.silu(x @ ws_gate) * (x @ ws_up) @ ws_down
        return (y + shared).reshape(orig_shape)
    x = x + _L0_xattn_ref(_layernorm(x, axis=-1), ctx_2048, L0_xattn_Wq, L0_xattn_Wg, L0_xattn_bg, L0_xattn_Wkv, L0_xattn_Wo)
    x = x + _L0_attn_ref(_layernorm(x, axis=-1), L0_attn_Wq, L0_attn_bq, L0_attn_Wk, L0_attn_bk, L0_attn_Wv, L0_attn_bv, L0_attn_Wo, L0_attn_bo)
    x = x + _L0_ffn_ref(_layernorm(x, axis=-1), L0_ffn_W1, L0_ffn_W2, L0_ffn_W3)
    x = x + _L1_xattn_ref(_layernorm(x, axis=-1), ctx_2048, mask_BxS2_ik0, L1_xattn_Wq, L1_xattn_bq, L1_xattn_Wk, L1_xattn_bk, L1_xattn_Wv, L1_xattn_bv, L1_xattn_Wo, L1_xattn_bo, L1_xattn_ln_gamma, L1_xattn_ln_beta, L1_xattn_residual_scale)
    x = x + _L1_attn_ref(_layernorm(x, axis=-1), L1_attn_w_qkv, L1_attn_w_o)
    x = x + _L1_ffn_ref(_layernorm(x, axis=-1), L1_ffn_weight, L1_ffn_norm_weight)
    x = x + _L2_xattn_ref(_layernorm(x, axis=-1), mask_Bx1xSxS_fk0, ctx_2048, L2_xattn_Wq, L2_xattn_Wk, L2_xattn_Wv, L2_xattn_Wo, L2_xattn_gate)
    x = x + _L2_attn_ref(_layernorm(x, axis=-1), L2_attn_wq_a, L2_attn_q_a_norm_w, L2_attn_wq_b, L2_attn_wkv_a, L2_attn_kv_a_norm_w, L2_attn_wkv_b, L2_attn_wo)
    x = x + _L2_ffn_ref(_layernorm(x, axis=-1), L2_ffn_W_up, L2_ffn_b_up, L2_ffn_W_down, L2_ffn_b_down, L2_ffn_W_q, L2_ffn_keys, L2_ffn_down_embed, L2_ffn_up_embed)
    x = x + _L3_xattn_ref(_layernorm(x, axis=-1), ctx_2048, ctx_2048, mask_BxS2_ff1, L3_xattn_Wq, L3_xattn_bq, L3_xattn_Wk, L3_xattn_bk, L3_xattn_Wv, L3_xattn_bv, L3_xattn_Wqf, L3_xattn_Wkf, L3_xattn_Wo, L3_xattn_bo)
    x = x + _L3_attn_ref(_layernorm(x, axis=-1), L3_attn_Wq, L3_attn_Wk, L3_attn_Wv, L3_attn_Wo)
    x = x + _L3_ffn_ref(_layernorm(x, axis=-1), L3_ffn_gate_w, L3_ffn_bias, L3_ffn_w_gate, L3_ffn_w_up, L3_ffn_w_down, L3_ffn_ws_gate, L3_ffn_ws_up, L3_ffn_ws_down)
    return x

_drawn_inputs = setup_inputs


def setup_inputs(seed=0):
    import zlib

    import numpy as np

    out = dict(_drawn_inputs(seed))
    spreads = {'L0_xattn_bg': (1.0, 0.6),
     'L0_attn_bq': (0.0, 0.8),
     'L0_attn_bk': (0.0, 0.8),
     'L0_attn_bv': (0.0, 0.1),
     'L0_attn_bo': (0.0, 0.1),
     'L1_xattn_bq': (0.0, 0.353),
     'L1_xattn_bk': (0.0, 0.8),
     'L1_xattn_bv': (0.0, 0.1),
     'L1_xattn_bo': (0.0, 0.1),
     'L1_xattn_ln_gamma': (1.0, 0.2),
     'L1_xattn_ln_beta': (0.0, 0.1),
     'L1_ffn_norm_weight': (1.0, 0.2),
     'L2_attn_q_a_norm_w': (1.0, 0.6),
     'L2_attn_kv_a_norm_w': (1.0, 0.6),
     'L2_ffn_b_up': (0.0, 0.8),
     'L2_ffn_b_down': (0.0, 0.8),
     'L3_xattn_bq': (0.0, 0.8),
     'L3_xattn_bk': (0.0, 0.8),
     'L3_xattn_bv': (0.0, 0.1),
     'L3_xattn_bo': (0.0, 0.1)}
    factors = {'L0_xattn_Wq': 5.072,
     'L2_xattn_Wq': 8.0,
     'L2_xattn_Wk': 8.0,
     'L2_xattn_gate': 8.0,
     'L2_attn_wq_a': 8.0,
     'L2_attn_wq_b': 8.0,
     'L2_ffn_W_up': 8.0,
     'L2_ffn_W_down': 8.0,
     'L2_ffn_W_q': 8.0,
     'L2_ffn_keys': 8.0,
     'L2_ffn_down_embed': 8.0,
     'L2_ffn_up_embed': 8.0,
     'L3_attn_Wq': 8.0,
     'L3_attn_Wk': 8.0,
     'L3_ffn_gate_w': 8.0,
     'L3_ffn_bias': 8.0,
     'L3_ffn_w_gate': 8.0,
     'L3_ffn_w_up': 8.0,
     'L3_ffn_w_down': 8.0,
     'L3_ffn_ws_gate': 8.0,
     'L3_ffn_ws_up': 8.0,
     'L3_ffn_ws_down': 8.0}
    for name, (base, spread) in spreads.items():
        noise = np.random.default_rng([zlib.crc32(name.encode()), seed]).standard_normal(out[name].shape)
        drawn = base * np.exp(spread * noise) if base else spread * noise
        out[name] = jnp.asarray(drawn.astype(out[name].dtype))
    for name, factor in factors.items():
        out[name] = (out[name] * factor).astype(out[name].dtype)
    return out
```

```python
from contextlib import ExitStack

import numpy as np

import concourse.bass as bass
from concourse import mybir

ALU = mybir.AluOpType
ACT = mybir.ActivationFunctionType
AX = mybir.AxisListType.X
F32 = mybir.dt.float32
BF16 = mybir.dt.bfloat16
I32 = mybir.dt.int32
U32 = mybir.dt.uint32

P = 128
B = 2
D = 256
KC = D // P
T = B * P
S2 = 2048
NT = S2 // P
LN_EPS = 1e-5
NEG_LARGE = -1e30


def hadamard(n):
    h = np.ones((1, 1), np.float32)
    while h.shape[0] < n:
        h = np.block([[h, h], [h, -h]]).astype(np.float32)
    return h


def rope_small():
    inv = 1.0 / 10000.0 ** (np.arange(0, 8, 2, dtype=np.float32) / 8)
    f = np.outer(np.arange(P, dtype=np.float32), inv)
    emb = np.concatenate([f, f], -1)
    sin = np.sin(emb).astype(np.float32)
    sin[:, :4] *= -1
    return np.cos(emb).astype(np.float32), sin


def rope_yarn():
    import math
    dim, base, factor, orig = 64, 10000.0, 40.0, 512
    ex = np.arange(0, dim, 2, dtype=np.float64) / dim
    extra = 1.0 / base ** ex
    inter = 1.0 / (factor * base ** ex)

    def corr(rot):
        return dim * math.log(orig / (rot * 2 * math.pi)) / (2 * math.log(base))
    low, high = max(math.floor(corr(32.0)), 0), min(math.ceil(corr(1.0)), dim - 1)
    if low == high:
        high = high + 0.001
    ramp = np.clip((np.arange(dim // 2, dtype=np.float64) - low) / (high - low), 0.0, 1.0)
    keep = 1.0 - ramp
    inv = inter * (1.0 - keep) + extra * keep
    f = np.outer(np.arange(P, dtype=np.float64), inv)

    def mscale(m):
        return 0.1 * m * math.log(factor) + 1.0
    msc = mscale(0.707) / mscale(0.0)
    return (np.cos(f) * msc).astype(np.float32), (np.sin(f) * msc).astype(np.float32)


def constants():
    i = np.arange(P)
    eye = np.eye(P, dtype=np.float32)
    cos8, sin8 = rope_small()
    cy, sy = rope_yarn()
    cos_rows = np.concatenate([np.ones((64, P), np.float32), cy.T, cy.T], 0)
    sin_rows = np.concatenate([np.zeros((64, P), np.float32), -sy.T, sy.T], 0)
    return {
        "ident": eye,
        "minus_half": np.full((P, B), -0.5, np.float32),
        "ones": np.ones((P, P), np.float32),
        "block16": (i[:, None] // 16 == i[None, :] // 16).astype(np.float32),
        "head16": (i[:, None] // 16 == np.arange(8)[None, :]).astype(np.float32),
        "head8": (i[:, None] // 8 == np.arange(16)[None, :]).astype(np.float32),
        "pair64": (i[:, None] // 64 == np.arange(34)[None, :] // 17).astype(np.float32),
        "causal": np.where(i[:, None] >= i[None, :], 0.0, NEG_LARGE).astype(np.float32),
        "before": (i[:, None] < i[None, :]).astype(np.float32),
        "hadamard": hadamard(P),
        "decay": np.exp(-np.arange(P, dtype=np.float32) / P)[:, None].astype(np.float32),
        "decay_row": np.broadcast_to(np.exp(-np.arange(P, dtype=np.float32) / P), (P, P)),
        "cos8": cos8, "sin8": sin8,
        "cos_rows": cos_rows, "sin_rows": sin_rows,
        "cos_tok": np.concatenate([cy, cy], 1), "sin_tok": np.concatenate([-sy, sy], 1),
        "eight": np.broadcast_to(np.arange(8, dtype=np.float32), (P, 8)),
    }


def tiles(w):
    k, n = w.shape[0] // P, w.shape[1]
    return w.reshape(k, P, n).transpose(1, 0, 2).reshape(P, k * n)


def every_row(v):
    v = np.asarray(v).reshape(1, -1)
    return np.broadcast_to(v, (P, v.shape[1]))


def per_channel(v):
    return np.asarray(v).reshape(-1, P).T


def full(a):
    return np.concatenate([a, np.zeros((P - a.shape[0], a.shape[1]), a.dtype)], 0)


def block_diag(w, n):
    r, c = w.shape
    out = np.zeros((n * r, n * c), w.dtype)
    for j in range(n):
        out[j * r:(j + 1) * r, j * c:(j + 1) * c] = w
    return out


class Fields:

    def __init__(self, widths):
        self.at, n = {}, 0
        for name, w in widths:
            self.at[name] = (n, w)
            n += w
        self.n = n

    def view(self, buffer, name):
        a, w = self.at[name]
        return buffer[:, a:a + w]


class Layer:

    def __init__(self, env, name):
        self.env, self.nc, self.name = env, env.nc, name
        self.stack, self.sems = ExitStack(), []

    def sb(self, name, shape, dt=F32):
        return self.stack.enter_context(self.nc.sbuf_tensor(f"{self.name}_{name}", shape, dt))

    def bank(self, name):
        return self.stack.enter_context(self.nc.psum_tensor(f"{self.name}_bank_{name}", [P, 512], F32))

    def sem(self, name):
        s = self.nc.alloc_semaphore(f"{self.name}_{name}")
        self.sems.append(s)
        return s

    def block(self):
        return self.nc.Block(f"{self.name}_block")

    def close(self):
        self.stack.close()
        self.nc.clear_and_free_semaphores(self.sems)
        self.nc.all_engine_barrier()


class Chain:

    def __init__(self, eng, sem):
        self.eng, self.sem, self.n = eng, sem, 0

    def __call__(self, ins):
        self.n += 1
        ins.then_inc(self.sem, 1)
        self.eng.wait_ge(self.sem, self.n)


class InvSqrt:

    def __init__(self, L, name):
        self.L = L
        self.sum, self.out = L.sb(f"{name}_plus_eps", [P, B]), L.sb(f"{name}_inv_sqrt", [P, B])
        self.s_sum, self.s_out = L.sem(f"{name}_plus_eps_ready"), L.sem(f"{name}_inv_sqrt_ready")

    def vector(self, dve, value, eps):
        self.L.nc.vector.tensor_scalar(self.sum[:, :], value, eps, None, ALU.add).then_inc(self.s_sum, 1)
        dve.wait_ge(self.s_out, 1)

    def gpsimd(self, pool):
        pool.wait_ge(self.s_sum, 1)
        self.L.nc.gpsimd.tensor_tensor(self.out[:, :], self.sum[:, :], self.L.env.const("minus_half"),
                                       ALU.pow).then_inc(self.s_out, 1)


class Head:

    def __init__(self, L, bank):
        self.L, self.bank = L, bank
        self.xn = L.sb("xn", [P, B, D])
        self.xT = L.sb("xT", [P, KC, T])
        self.stats = L.sb("ln_stats", [P, B, 6])
        self.mv = L.sb("ln_mv", [P, B, 2])
        self.rstd = InvSqrt(L, "ln_var")
        self.s_norm = L.sem("normed")
        self.s_turn = L.sem("xn_turned")
        self.s_xT = L.sem("xT_ready")

    def vector(self, dve, chain):
        nc, x = self.L.nc, self.L.env.x
        for b in range(B):
            i = nc.vector.bn_stats(self.stats[:, b, :], x[:, b, :])
        chain(i)
        for b in range(B):
            i = nc.vector.bn_aggr(self.mv[:, b, :], self.stats[:, b, :])
        chain(i)
        self.rstd.vector(dve, self.mv[:, :, 1], LN_EPS)
        for b in range(B):
            nc.vector.tensor_scalar(self.xn[:, b, :], x[:, b, :], self.mv[:, b, 0:1], self.rstd.out[:, b:b + 1],
                                    ALU.subtract, ALU.mult).then_inc(self.s_norm, 1)

    def gpsimd(self, pool):
        self.rstd.gpsimd(pool)

    def tensor(self, pe):
        turn(self.L, pe, self.bank, self.xn, self.s_norm, B, self.s_turn)

    def scalar(self, act):
        act.wait_ge(self.s_turn, 1)
        self.L.nc.scalar.activation(self.xT[:, :, :].rearrange("p k t -> p (k t)"), self.bank[:, :],
                                    ACT.Copy).then_inc(self.s_xT, 1)


def turn(L, pe, bank, src, s_src, count, s_done):
    nc, ident = L.nc, L.env.const("ident")
    pe.wait_ge(s_src, count)
    for k in range(KC):
        for b in range(B):
            at = k * T + b * P
            i = nc.tensor.transpose(bank[:, at:at + P], src[:, b, k * P:(k + 1) * P], ident)
    i.then_inc(s_done, 1)


class Tail:

    def __init__(self, L, y, bank_t, bank_o, wo, bias=None, ys=B):
        self.L, self.y, self.bank_t, self.bank_o, self.wo, self.bias, self.ys = L, y, bank_t, bank_o, wo, bias, ys
        self.yT = L.sb("yT", [P, KC, T])
        self.s_y = L.sem("y_ready")
        self.s_turn = L.sem("y_turned")
        self.s_yT = L.sem("yT_ready")
        self.s_out = L.sem("out_ready")

    def tensor(self, pe):
        nc = self.L.nc
        turn(self.L, pe, self.bank_t, self.y, self.s_y, self.ys, self.s_turn)
        pe.wait_ge(self.s_yT, 1)
        for b in range(B):
            for k in range(KC):
                i = nc.tensor.matmul(self.bank_o[:, b * D:(b + 1) * D], self.yT[:, k, b * P:(b + 1) * P],
                                     self.wo[:, k * D:(k + 1) * D], start=(k == 0), stop=(k == KC - 1))
        i.then_inc(self.s_out, 1)

    def scalar(self, act):
        act.wait_ge(self.s_turn, 1)
        self.L.nc.scalar.activation(self.yT[:, :, :].rearrange("p k t -> p (k t)"), self.bank_t[:, :],
                                    ACT.Copy).then_inc(self.s_yT, 1)

    def vector(self, dve, chain):
        nc, x = self.L.nc, self.L.env.x[:, :, :].rearrange("p b d -> p (b d)")
        dve.wait_ge(self.s_out, 1)
        if self.bias is not None:
            xb = self.L.env.x
            chain(nc.vector.tensor_tensor(xb[:, :, :], xb[:, :, :],
                                          self.bias.unsqueeze(1).to_broadcast([P, B, D]), ALU.add))
        chain(nc.vector.tensor_tensor(x, x, self.bank_o[:, :], ALU.add))


def project_T(L, bank, w, xT, n_out=KC, cols=T):
    for m in range(n_out):
        for k in range(KC):
            i = L.nc.tensor.matmul(bank[:, m * cols:(m + 1) * cols], w[:, k, m * P:(m + 1) * P], xT[:, k, :],
                                   start=(k == 0), stop=(k == KC - 1))
    return i


def project(L, bank, w, xT):
    n = w.shape[2]
    for b in range(B):
        for k in range(KC):
            i = L.nc.tensor.matmul(bank[:, b * n:(b + 1) * n], xT[:, k, b * P:(b + 1) * P], w[:, k, :],
                                   start=(k == 0), stop=(k == KC - 1))
    return i


class LinearRead:

    VW = P + 1

    def __init__(self, L, banks, qf, y, ys_scale=None):
        self.L, self.banks, self.qf, self.y = L, banks, qf, y
        self.kvd = L.sb("kv_blocks", [P, B, KC, P + 8])
        self.ksum = L.sb("k_sum", [P, B, KC, 1])
        self.z = L.sb("z", [P, B, D // 16])
        self.s_kvd, self.s_att = L.sem("kv_blocks_ready"), L.sem("attended")

    def blocks(self, dve, chain, b):
        nc, const = self.L.nc, self.L.env.const
        for c in range(KC):
            at = c * self.VW
            nc.vector.tensor_tensor(self.kvd[:, b, c, 0:P], self.banks[b][:, at:at + P], const("block16"), ALU.mult)
            i = nc.vector.tensor_copy(self.ksum[:, b, c, :], self.banks[b][:, at + P:at + self.VW])
        chain(i)
        for c in range(KC):
            i = nc.vector.tensor_scalar(self.kvd[:, b, c, P:P + 8], const("head16"), self.ksum[:, b, c, :], None, ALU.mult)
        i.then_inc(self.s_kvd, 1)

    def tensor(self, pe):
        for b in range(B):
            pe.wait_ge(self.s_kvd, b + 1)
            for c in range(KC):
                i = self.L.nc.tensor.matmul(self.banks[b][:, c * (P + 8):(c + 1) * (P + 8)],
                                            self.qf[:, c, b * P:(b + 1) * P], self.kvd[:, b, c, :], start=True, stop=True)
            i.then_inc(self.s_att, 1)

    def divide(self, dve, chain, b, eps):
        nc = self.L.nc
        dve.wait_ge(self.s_att, b + 1)
        o = self.banks[b][:, 0:KC * (P + 8)].rearrange("p (c n) -> p c n", c=KC)
        chain(nc.vector.tensor_scalar(self.z[:, b, :].rearrange("p (c h) -> p c h", c=KC), o[:, :, P:P + 8], eps, None, ALU.add))
        chain(nc.vector.reciprocal(self.z[:, b, :], self.z[:, b, :]))
        yb = self.y[:, b, :].rearrange("p (h e) -> p h e", e=16)
        for c in range(KC):
            i = nc.vector.tensor_tensor(yb[:, c * 8:(c + 1) * 8, :], o[:, c, 0:P].rearrange("p (h e) -> p h e", e=16),
                                        self.z[:, b, c * 8:(c + 1) * 8].unsqueeze(2).to_broadcast([P, 8, 16]), ALU.mult)
        return i


L0X = Fields([("Wq", KC * D), ("Wg", KC * D), ("Wkv", KC * 2 * D), ("Wo", KC * D), ("bg", D)])


def pack_L0X(i):
    return [tiles(i["L0_xattn_Wq"].T), tiles(i["L0_xattn_Wg"].T), tiles(i["L0_xattn_Wkv"].T),
            tiles(i["L0_xattn_Wo"].T), every_row(i["L0_xattn_bg"])]


def layer_L0X(env):
    L = Layer(env, "L0X")
    nc, w = env.nc, env.weights("L0X")
    wq = w("Wq").rearrange("p (k n) -> p k n", k=KC)
    wg = w("Wg").rearrange("p (k n) -> p k n", k=KC)
    wkv = w("Wkv").rearrange("p (k n) -> p k n", k=KC)
    VW = LinearRead.VW
    bank_x, bank_q, bank_g = L.bank("xT"), L.bank("q"), L.bank("g")
    bank_kv = [L.bank(f"kv{j}") for j in range(3)]
    bank_s = [L.bank(f"summary{b}") for b in range(B)]
    head = Head(L, bank_x)
    y = L.sb("y", [P, B, D])
    tail = Tail(L, y, bank_q, bank_g, w("Wo"))
    qmin, qexp, qf = L.sb("qmin", [P, KC * T]), L.sb("qexp", [P, KC * T]), L.sb("qf", [P, KC, T])
    gate, gexp = L.sb("gate", [P, B, D]), L.sb("gexp", [P, B, D])
    NB = 3
    ks = L.sb("k_raw", [P, NB, D])
    kmin = L.sb("k_min", [P, NB, D])
    kexp = L.sb("k_exp", [P, NB, D])
    kf = L.sb("k_feature", [P, NB, D])
    vo = L.sb("v_ones", [P, NB, KC, VW])
    read = LinearRead(L, bank_s, qf, y)
    s_chain = L.sem("dve_chain")
    s_q, s_g, s_qmin, s_qexp, s_gexp, s_gp = (L.sem(n) for n in
                                              ("q_done", "g_done", "qmin_ready", "qexp_ready", "gexp_ready", "gpre_ready"))
    s_qf = L.sem("q_features")
    s_kv, s_raw, s_kmin, s_kexp, s_kf = (L.sem(n) for n in ("kv_done", "kv_copied", "kmin_ready", "kexp_ready", "k_features"))
    s_sum, s_ones = L.sem("summary_step"), L.sem("ones_set")
    steps = [(b, t) for b in range(B) for t in range(NT)]
    env.prefetch(L, "L0A")

    with L.block() as block:
        @block.sync
        def _(sp):
            env.issue_prefetch(sp)

        @block.tensor
        def _(pe):
            env.wait_weights(pe, "L0X")

            def context_kv(i):
                b, t = steps[i]
                env.wait_context(pe, b, t)
                if i >= 3:
                    pe.wait_ge(s_raw, i - 2)
                for k in range(KC):
                    m = nc.tensor.matmul(bank_kv[i % 3][:, :], env.ctx(k, b, t), wkv[:, k, :],
                                         start=(k == 0), stop=(k == KC - 1))
                m.then_inc(s_kv, 1)

            def summary(i):
                b, t = steps[i]
                pe.wait_ge(s_kf, i + 1)
                for c in range(KC):
                    m = nc.tensor.matmul(bank_s[b][:, c * VW:(c + 1) * VW], kf[:, i % NB, c * P:(c + 1) * P],
                                         vo[:, i % NB, c, :], start=(t == 0 and c == 0), stop=(t == NT - 1),
                                         skip_group_check=True)
                m.then_inc(s_sum, 1)

            context_kv(0)
            context_kv(1)
            head.tensor(pe)
            pe.wait_ge(head.s_xT, 1)
            project_T(L, bank_q, wq, head.xT).then_inc(s_q, 1)
            project(L, bank_g, wg, head.xT).then_inc(s_g, 1)
            pe.wait_ge(s_ones, 1)
            for i in range(2, len(steps)):
                context_kv(i)
                summary(i - 2)
            summary(len(steps) - 2)
            summary(len(steps) - 1)
            pe.wait_ge(s_qf, 1)
            read.tensor(pe)
            tail.tensor(pe)

        @block.gpsimd
        def _(pool):
            head.gpsimd(pool)

        @block.scalar
        def _(act):
            def copy_kv(i):
                act.wait_ge(s_kv, i + 1)
                if i >= NB:
                    act.wait_ge(s_sum, i - NB + 1)
                nc.scalar.activation(ks[:, i % NB, :], bank_kv[i % 3][:, 0:D], ACT.Copy)
                nc.scalar.activation(vo[:, i % NB, :, 0:P],
                                     bank_kv[i % 3][:, D:2 * D].rearrange("p (c n) -> p c n", c=KC),
                                     ACT.Copy).then_inc(s_raw, 1)

            def exp_k(i):
                act.wait_ge(s_kmin, i + 1)
                nc.scalar.activation(kexp[:, i % NB, :], kmin[:, i % NB, :], ACT.Exp).then_inc(s_kexp, 1)

            copy_kv(0)
            head.scalar(act)
            act.wait_ge(s_qmin, 1)
            nc.scalar.activation(qexp[:, :], qmin[:, :], ACT.Exp).then_inc(s_qexp, 1)
            act.wait_ge(s_gp, 1)
            nc.scalar.activation(gexp[:, :, :], gate[:, :, :], ACT.Exp, scale=-1.0).then_inc(s_gexp, 1)
            for i in range(1, len(steps)):
                copy_kv(i)
                exp_k(i - 1)
            exp_k(len(steps) - 1)
            tail.scalar(act)

        @block.vector
        def _(dve):
            chain = Chain(dve, s_chain)
            nc.vector.memset(vo[:, :, :, P:VW], 1.0).then_inc(s_ones, 1)
            head.vector(dve, chain)
            dve.wait_ge(s_q, 1)
            nc.vector.tensor_scalar(qmin[:, :], bank_q[:, :], 0.0, None, ALU.min).then_inc(s_qmin, 1)
            dve.wait_ge(s_g, 1)
            nc.vector.tensor_tensor(gate[:, :, :], bank_g[:, :].rearrange("p (b n) -> p b n", b=B),
                                    w("bg").unsqueeze(1).to_broadcast([P, B, D]), ALU.add).then_inc(s_gp, 1)
            dve.wait_ge(s_qexp, 1)
            nc.vector.scalar_tensor_tensor(out=qf[:, :, :].rearrange("p c t -> p (c t)"), in0=bank_q[:, :], scalar=0.0,
                                           in1=qexp[:, :], op0=ALU.max, op1=ALU.add).then_inc(s_qf, 1)
            dve.wait_ge(s_gexp, 1)
            chain(nc.vector.tensor_scalar(gexp[:, :, :], gexp[:, :, :], 1.0, None, ALU.add))
            chain(nc.vector.reciprocal(gate[:, :, :], gexp[:, :, :]))

            def k_min(i):
                dve.wait_ge(s_raw, i + 1)
                if i >= NB:
                    dve.wait_ge(s_kexp, i - NB + 1)
                nc.vector.tensor_scalar(kmin[:, i % NB, :], ks[:, i % NB, :], 0.0, None, ALU.min).then_inc(s_kmin, 1)

            def k_feature(i):
                dve.wait_ge(s_kexp, i + 1)
                nc.vector.scalar_tensor_tensor(out=kf[:, i % NB, :], in0=ks[:, i % NB, :], scalar=0.0,
                                               in1=kexp[:, i % NB, :], op0=ALU.max, op1=ALU.add).then_inc(s_kf, 1)

            def blocks(b):
                dve.wait_ge(s_sum, NT * (b + 1))
                read.blocks(dve, chain, b)

            k_min(0)
            for i in range(1, len(steps)):
                k_min(i)
                k_feature(i - 1)
                if i == NT + 2:
                    blocks(0)
            k_feature(len(steps) - 1)
            blocks(1)
            for b in range(B):
                chain(read.divide(dve, chain, b, 1e-6))
                nc.vector.tensor_tensor(y[:, b, :], y[:, b, :], gate[:, b, :], ALU.mult).then_inc(tail.s_y, 1)
            tail.vector(dve, chain)
    L.close()


L0A = Fields([("Wq", KC * D), ("Wk", KC * D), ("Wv", KC * D), ("Wo", KC * D), ("bq", KC), ("bk", D), ("bv", D), ("bo", D)])


def pack_L0A(i):
    return [tiles(i[f"L0_attn_W{n}"].T) for n in "qkvo"] + \
        [per_channel(i["L0_attn_bq"])] + [every_row(i[f"L0_attn_b{n}"]) for n in "kvo"]


def layer_L0A(env):
    L = Layer(env, "L0A")
    nc, w = env.nc, env.weights("L0A")
    wq, wk, wv = (w(n).rearrange("p (k n) -> p k n", k=KC) for n in ("Wq", "Wk", "Wv"))
    VW = LinearRead.VW
    bank_x, bank_q, bank_k, bank_v = L.bank("xT"), L.bank("q"), L.bank("k"), L.bank("v")
    bank_s = [L.bank(f"summary{b}") for b in range(B)]
    head = Head(L, bank_x)
    y = L.sb("y", [P, B, D])
    tail = Tail(L, y, bank_q, bank_k, w("Wo"), bias=w("bo"))
    qf, kf = L.sb("q_feature", [P, KC, T]), L.sb("k_feature", [P, B, D])
    vo = L.sb("v_ones", [P, B, KC, VW])
    read = LinearRead(L, bank_s, qf, y)
    s_chain, s_q, s_k, s_v, s_kv, s_sum = (L.sem(n) for n in
                                           ("dve_chain", "q_done", "k_done", "v_done", "k_and_v_ready", "summary_done"))
    env.prefetch(L, "L0F")

    with L.block() as block:
        @block.sync
        def _(sp):
            env.issue_prefetch(sp)

        @block.tensor
        def _(pe):
            env.wait_weights(pe, "L0A")
            head.tensor(pe)
            pe.wait_ge(head.s_xT, 1)
            project(L, bank_k, wk, head.xT).then_inc(s_k, 1)
            project(L, bank_v, wv, head.xT).then_inc(s_v, 1)
            project_T(L, bank_q, wq, head.xT).then_inc(s_q, 1)
            pe.wait_ge(s_kv, 1)
            for b in range(B):
                for c in range(KC):
                    m = nc.tensor.matmul(bank_s[b][:, c * VW:(c + 1) * VW], kf[:, b, c * P:(c + 1) * P], vo[:, b, c, :],
                                         start=True, stop=True)
                m.then_inc(s_sum, 1)
            read.tensor(pe)
            tail.tensor(pe)

        @block.gpsimd
        def _(pool):
            head.gpsimd(pool)

        @block.scalar
        def _(act):
            head.scalar(act)
            tail.scalar(act)

        @block.vector
        def _(dve):
            chain = Chain(dve, s_chain)
            nc.vector.memset(vo[:, :, :, P:VW], 1.0)
            head.vector(dve, chain)
            dve.wait_ge(s_k, 1)
            env.wait_weights(dve, "L0A")
            chain(nc.vector.tensor_tensor(kf[:, :, :], bank_k[:, :].rearrange("p (b n) -> p b n", b=B),
                                          w("bk").unsqueeze(1).to_broadcast([P, B, D]), ALU.add))
            nc.vector.tensor_scalar(kf[:, :, :], kf[:, :, :], 0.0, env.const("decay"), ALU.max, ALU.mult)
            dve.wait_ge(s_v, 1)
            for b in range(B):
                i = nc.vector.tensor_tensor(vo[:, b, :, 0:P], bank_v[:, b * D:(b + 1) * D].rearrange("p (c n) -> p c n", c=KC),
                                            w("bv").rearrange("p (c n) -> p c n", c=KC), ALU.add)
            i.then_inc(s_kv, 1)
            dve.wait_ge(s_q, 1)
            for c in range(KC):
                i = nc.vector.tensor_scalar(qf[:, c, :], bank_q[:, c * T:(c + 1) * T], w("bq")[:, c:c + 1], 0.0,
                                            ALU.add, ALU.max)
            chain(i)
            qd = qf[:, :, :].rearrange("p c (b t) -> p (c b) t", b=B)
            chain(nc.vector.tensor_tensor(qd, qd, env.const("decay_row").unsqueeze(1).to_broadcast([P, KC * B, P]), ALU.mult))
            for b in range(B):
                dve.wait_ge(s_sum, b + 1)
                read.blocks(dve, chain, b)
            for b in range(B):
                read.divide(dve, chain, b, 1e-6).then_inc(tail.s_y, 1)
            tail.vector(dve, chain)
    L.close()


HID = 1024
HC = HID // P
L0F = Fields([("W1", KC * HID), ("W3", KC * HID), ("W2", HC * D)])


def pack_L0F(i):
    return [tiles(i["L0_ffn_W1"].T), tiles(i["L0_ffn_W3"].T), tiles(i["L0_ffn_W2"].T)]


def layer_L0F(env):
    L = Layer(env, "L0F")
    nc, w = env.nc, env.weights("L0F")
    w1, w3 = (w(n).rearrange("p (k n) -> p k n", k=KC) for n in ("W1", "W3"))
    bank_x, bank_o = L.bank("xT"), L.bank("out")
    bank_g, bank_u = ([L.bank(f"{n}{j}") for j in range(2)] for n in ("gate", "up"))
    bank_w = [L.bank(f"w2_{j}") for j in range(2)]
    head = Head(L, bank_x)
    e, r, h = L.sb("tanh", [P, 2, 512]), L.sb("sig", [P, 2, 512]), L.sb("hidden", [P, HC, T])
    wa, wb = L.sb("w2_a", [P, HC, D]), L.sb("w2_b", [P, HC, D])
    s_chain, s_w, s_wc, s_fly, s_g, s_u, s_e, s_h, s_o = (L.sem(n) for n in (
        "dve_chain", "w2_rows_done", "w2_copied", "butterfly_step", "gate_done", "up_done", "tanh_ready", "hidden_ready", "out_done"))
    JOBS = HC // 2
    env.prefetch(L, "L1X")

    with L.block() as block:
        @block.sync
        def _(sp):
            env.issue_prefetch(sp)

        @block.tensor
        def _(pe):
            env.wait_weights(pe, "L0F")
            for j in range(JOBS):
                if j >= 2:
                    pe.wait_ge(s_wc, j - 1)
                nc.tensor.matmul(bank_w[j % 2][:, :], env.const("hadamard"), w("W2")[:, j * 512:(j + 1) * 512],
                                 start=True, stop=True).then_inc(s_w, 1)
            head.tensor(pe)
            pe.wait_ge(head.s_xT, 1)
            for j in range(JOBS):
                if j >= 2:
                    pe.wait_ge(s_h, j - 1)
                for wt, bank, s in ((w1, bank_g, s_g), (w3, bank_u, s_u)):
                    for m in range(2):
                        for k in range(KC):
                            at = (2 * j + m) * P
                            i = nc.tensor.matmul(bank[j % 2][:, m * T:(m + 1) * T], wt[:, k, at:at + P], head.xT[:, k, :],
                                                 start=(k == 0), stop=(k == KC - 1))
                    i.then_inc(s, 1)
            pe.wait_ge(s_fly, 3)
            pe.wait_ge(s_h, JOBS)
            for b in range(B):
                for m in range(HC):
                    i = nc.tensor.matmul(bank_o[:, b * D:(b + 1) * D], h[:, m, b * P:(b + 1) * P], wb[:, m, :],
                                         start=(m == 0), stop=(m == HC - 1))
            i.then_inc(s_o, 1)

        @block.gpsimd
        def _(pool):
            head.gpsimd(pool)
            pool.wait_ge(s_wc, JOBS)
            src, dst = wa, wb
            for n, half in enumerate((1, 2, 4)):
                if n:
                    pool.wait_ge(s_fly, n)
                s = src[:, :, :].rearrange("p (a two h) d -> p a two h d", two=2, h=half)
                d = dst[:, :, :].rearrange("p (a two h) d -> p a two h d", two=2, h=half)
                for a in range(HC // (2 * half)):
                    nc.gpsimd.tensor_tensor(d[:, a, 0], s[:, a, 0], s[:, a, 1], ALU.add)
                    i = nc.gpsimd.tensor_tensor(d[:, a, 1], s[:, a, 0], s[:, a, 1], ALU.subtract)
                i.then_inc(s_fly, 1)
                src, dst = dst, src

        @block.scalar
        def _(act):
            for j in range(JOBS):
                act.wait_ge(s_w, j + 1)
                nc.scalar.activation(wa[:, 2 * j:2 * j + 2, :].rearrange("p a d -> p (a d)"), bank_w[j % 2][:, :], ACT.Copy,
                                     scale=0.5 * HID ** -0.5).then_inc(s_wc, 1)
                if j == 1:
                    head.scalar(act)
            for j in range(JOBS):
                act.wait_ge(s_g, j + 1)
                if j >= 2:
                    act.wait_ge(s_h, j - 1)
                nc.scalar.activation(e[:, j % 2, :], bank_g[j % 2][:, :], ACT.Tanh, scale=0.5).then_inc(s_e, 1)

        @block.vector
        def _(dve):
            chain = Chain(dve, s_chain)
            head.vector(dve, chain)
            for j in range(JOBS):
                dve.wait_ge(s_e, j + 1)
                chain(nc.vector.scalar_tensor_tensor(out=r[:, j % 2, :], in0=e[:, j % 2, :], scalar=1.0, in1=bank_g[j % 2][:, :],
                                                     op0=ALU.add, op1=ALU.mult))
                dve.wait_ge(s_u, j + 1)
                nc.vector.tensor_tensor(h[:, 2 * j:2 * j + 2, :].rearrange("p a t -> p (a t)"), r[:, j % 2, :],
                                        bank_u[j % 2][:, :], ALU.mult).then_inc(s_h, 1)
            dve.wait_ge(s_o, 1)
            x = env.x[:, :, :].rearrange("p b d -> p (b d)")
            chain(nc.vector.tensor_tensor(x, x, bank_o[:, :], ALU.add))
    L.close()


L1X = Fields([("Wq", KC * D), ("Wk", KC * D), ("Wv", KC * D), ("Wo", KC * D), ("bq", KC), ("bk", KC), ("bv", D),
              ("bo", D), ("gamma", D), ("beta", D), ("rs", 1)])


def pack_L1X(i):
    p = "L1_xattn_"
    return [tiles(i[f"{p}W{n}"].T) for n in "qkvo"] + [per_channel(i[p + "bq"]), per_channel(i[p + "bk"])] + \
        [every_row(i[p + n]) for n in ("bv", "bo", "ln_gamma", "ln_beta", "residual_scale")]


EXTRA_L1X = {"L1X_mask": lambda i: i["mask_BxS2_ik0"].reshape(B * NT, P).T}


def layer_L1X(env):
    L = Layer(env, "L1X")
    nc, w = env.nc, env.weights("L1X")
    wq, wk, wv = (w(n).rearrange("p (k n) -> p k n", k=KC) for n in ("Wq", "Wk", "Wv"))
    NH, HD, CLIP = 16, 16, 50.0
    VW = HD + 1
    bank_x = L.bank("xT")
    bank_p = [L.bank(f"proj{j}") for j in range(2)]
    NS = 3
    bank_s = [L.bank(f"scores{j}") for j in range(NS)]
    bank_o = [L.bank(f"read{b}") for b in range(B)]
    head = Head(L, bank_x)
    y = L.sb("y", [P, B, D])
    tail = Tail(L, y, bank_x, bank_p[0], w("Wo"))
    qT = L.sb("qT", [P, KC, T])
    qd = L.sb("q_blocks", [P, KC, B, 8, P])
    kT = L.sb("kT", [P, 2, KC, S2])
    vo = L.sb("v_ones", [P, NT, NH, VW])
    mask_i, keep, drop = L.sb("mask_int", [P, B * NT], I32), L.sb("keep", [P, B * NT]), L.sb("drop", [P, B * NT])
    NP = 3
    sc, pr = L.sb("clipped", [P, NP, 512]), L.sb("probs", [P, NP, 512])
    rden = L.sb("inv_den", [P, B, NH])
    delta, dsq = L.sb("delta", [P, B, D]), L.sb("delta_stats", [P, B, 6])
    dmv, rs = L.sb("delta_mv", [P, B, 2]), L.sb("res_scale", [P, 1])
    dinv = InvSqrt(L, "delta_var")
    (s_chain, s_mask, s_q, s_qd, s_k, s_kc, s_v, s_vc, s_vfree, s_s, s_cl, s_p, s_o, s_keep) = (L.sem(n) for n in (
        "dve_chain", "mask_loaded", "q_done", "q_blocks_ready", "k_done", "k_copied", "v_done", "v_copied", "values_read",
        "scores_done", "clipped_ready", "probs_ready", "read_step", "mask_ready"))
    units = [(b, t, g) for b in range(B) for t in range(NT) for g in range(4)]
    NJ = 4 * KC
    NV = NT // 2
    per_b = NJ + NV
    env.prefetch(L, "L1A")

    with L.block() as block:
        @block.sync
        def _(sp):
            sp.dma_start(mask_i[:, :], env.dram["L1X_mask"]).then_inc(s_mask, 16)
            env.issue_prefetch(sp)

        @block.tensor
        def _(pe):
            def projections(b):
                for j in range(NJ):
                    q, c = j // KC, j % KC
                    env.wait_context(pe, b, 4 * q)
                    n = b * NJ + j
                    if n >= 1:
                        pe.wait_ge(s_kc, n)
                    for k in range(KC):
                        i = nc.tensor.matmul(bank_p[0][:, :], wk[:, k, c * P:(c + 1) * P], env.ctx4(k, b, q),
                                             start=(k == 0), stop=(k == KC - 1))
                    i.then_inc(s_k, 1)
                    n = b * NV + j
                    if n >= 1:
                        pe.wait_ge(s_vc, n)
                    for u in range(2):
                        for k in range(KC):
                            i = nc.tensor.matmul(bank_p[1][:, u * D:(u + 1) * D], env.ctx(k, b, 2 * j + u), wv[:, k, :],
                                                 start=(k == 0), stop=(k == KC - 1))
                    i.then_inc(s_v, 1)

            def scores(n):
                b, t, g = units[n]
                c, half = g // 2, g % 2
                if n >= NS:
                    pe.wait_ge(s_cl, n - NS + 1)
                rhs = qd[:, c, b, 4 * half:4 * half + 4, :].rearrange("p h t -> p (h t)")
                nc.tensor.matmul(bank_s[n % NS][:, :], kT[:, b % 2, c, t * P:(t + 1) * P], rhs,
                                 start=True, stop=True).then_inc(s_s, 1)

            def read(n):
                b, t, g = units[n]
                pe.wait_ge(s_p, n + 1)
                for h in range(4):
                    at = (4 * g + h) * VW
                    i = nc.tensor.matmul(bank_o[b][:, at:at + VW], pr[:, n % NP, h * P:(h + 1) * P], vo[:, t, 4 * g + h, :],
                                         start=(t == 0 and g == 0 and h == 0), stop=(t == NT - 1), skip_group_check=True)
                i.then_inc(s_o, 1)

            env.wait_weights(pe, "L1X")
            head.tensor(pe)
            pe.wait_ge(head.s_xT, 1)
            project_T(L, bank_s[0], wq, head.xT).then_inc(s_q, 1)
            projections(0)
            pe.wait_ge(s_qd, 1)
            per = len(units) // B
            for b in range(B):
                if b:
                    projections(b)
                pe.wait_ge(s_kc, (b + 1) * NJ)
                pe.wait_ge(s_vc, (b + 1) * NV)
                first = b * per
                for n in range(first, first + per):
                    scores(n)
                    if n >= first + 2:
                        read(n - 2)
                read(first + per - 2)
                read(first + per - 1)
            tail.tensor(pe)

        @block.gpsimd
        def _(pool):
            head.gpsimd(pool)
            dinv.gpsimd(pool)

        @block.scalar
        def _(act):
            head.scalar(act)
            env.wait_weights(act, "L1X")
            per = len(units) // B
            for b in range(B):
                for j in range(NJ):
                    q, c = j // KC, j % KC
                    act.wait_ge(s_k, b * NJ + j + 1)
                    nc.scalar.activation(kT[:, b % 2, c, q * 512:(q + 1) * 512], bank_p[0][:, :], ACT.Identity,
                                         bias=w("bk")[:, c:c + 1]).then_inc(s_kc, 1)
                if b == 0:
                    act.wait_ge(s_keep, 1)
                for n in range(b * per, (b + 1) * per):
                    _, t, g = units[n]
                    act.wait_ge(s_cl, n + 1)
                    if n >= NP:
                        act.wait_ge(s_o, n - NP + 1)
                    col = b * NT + t
                    nc.scalar.activation(pr[:, n % NP, :], sc[:, n % NP, :], ACT.Exp, bias=drop[:, col:col + 1],
                                         scale=keep[:, col:col + 1]).then_inc(s_p, 1)
            tail.scalar(act)

        @block.vector
        def _(dve):
            chain = Chain(dve, s_chain)
            chain(nc.vector.memset(vo[:, :, :, HD:VW], 1.0))
            dve.wait_ge(s_mask, 16)
            chain(nc.vector.tensor_copy(drop[:, :], mask_i[:, :]))
            chain(nc.vector.tensor_scalar(keep[:, :], drop[:, :], 0.5, None, ALU.is_gt))
            nc.vector.tensor_scalar(drop[:, :], keep[:, :], -1.0, CLIP, ALU.add, ALU.mult).then_inc(s_keep, 1)
            head.vector(dve, chain)
            env.wait_weights(dve, "L1X")
            dve.wait_ge(s_q, 1)
            for c in range(KC):
                i = nc.vector.tensor_scalar(qT[:, c, :], bank_s[0][:, c * T:(c + 1) * T], w("bq")[:, c:c + 1], HD ** -0.5,
                                            ALU.add, ALU.mult)
            chain(i)
            for c in range(KC):
                for b in range(B):
                    i = nc.vector.tensor_tensor(qd[:, c, b, :, :], qT[:, c, b * P:(b + 1) * P].unsqueeze(1).to_broadcast([P, 8, P]),
                                                env.const("head16").unsqueeze(2).to_broadcast([P, 8, P]), ALU.mult)
            i.then_inc(s_qd, 1)
            per = len(units) // B
            bv = w("bv").rearrange("p (h e) -> p h e", h=NH).unsqueeze(1).to_broadcast([P, 2, NH, HD])
            for b in range(B):
                for j in range(NV):
                    dve.wait_ge(s_v, b * NV + j + 1)
                    if b and j == 0:
                        dve.wait_ge(s_o, b * per)
                    nc.vector.tensor_tensor(vo[:, 2 * j:2 * j + 2, :, 0:HD],
                                            bank_p[1][:, :].rearrange("p (t h e) -> p t h e", t=2, h=NH), bv,
                                            ALU.add).then_inc(s_vc, 1)
                for n in range(b * per, (b + 1) * per):
                    dve.wait_ge(s_s, n + 1)
                    if n >= NP:
                        dve.wait_ge(s_p, n - NP + 1)
                    nc.vector.tensor_scalar(sc[:, n % NP, :], bank_s[n % NS][:, :], CLIP, -CLIP, ALU.min,
                                            ALU.max).then_inc(s_cl, 1)
            dve.wait_ge(s_o, len(units))
            for b in range(B):
                o = bank_o[b][:, 0:NH * VW].rearrange("p (h e) -> p h e", h=NH)
                chain(nc.vector.tensor_scalar(rden[:, b, :], o[:, :, HD], 1e-8, None, ALU.add))
                chain(nc.vector.reciprocal(rden[:, b, :], rden[:, b, :]))
                nc.vector.tensor_tensor(y[:, b, :].rearrange("p (h e) -> p h e", h=NH), o[:, :, 0:HD],
                                        rden[:, b, :].unsqueeze(2).to_broadcast([P, NH, HD]), ALU.mult).then_inc(tail.s_y, 1)
            chain(nc.vector.tensor_scalar(rs[:, :], w("rs"), 0.0, 0.3, ALU.max, ALU.min))
            dve.wait_ge(tail.s_out, 1)
            chain(nc.vector.tensor_tensor(delta[:, :, :], tail.bank_o[:, :].rearrange("p (b n) -> p b n", b=B),
                                          w("bo").unsqueeze(1).to_broadcast([P, B, D]), ALU.add))
            chain(nc.vector.tensor_scalar(delta[:, :, :], delta[:, :, :], rs[:, 0:1], None, ALU.mult))
            for b in range(B):
                i = nc.vector.bn_stats(dsq[:, b, :], delta[:, b, :])
            chain(i)
            for b in range(B):
                i = nc.vector.bn_aggr(dmv[:, b, :], dsq[:, b, :])
            chain(i)
            dinv.vector(dve, dmv[:, :, 1], LN_EPS)
            for b in range(B):
                i = nc.vector.tensor_scalar(delta[:, b, :], delta[:, b, :], dmv[:, b, 0:1], dinv.out[:, b:b + 1],
                                            ALU.subtract, ALU.mult)
            chain(i)
            chain(nc.vector.tensor_tensor(delta[:, :, :], delta[:, :, :], w("gamma").unsqueeze(1).to_broadcast([P, B, D]), ALU.mult))
            chain(nc.vector.tensor_tensor(delta[:, :, :], delta[:, :, :], w("beta").unsqueeze(1).to_broadcast([P, B, D]), ALU.add))
            chain(nc.vector.tensor_tensor(env.x[:, :, :], env.x[:, :, :], delta[:, :, :], ALU.add))
    L.close()


HG = 4
NG = 16 // HG
L1A = Fields([("group0", 3 * HG * KC * P), ("w_o", 16 * D)])


def head_group(i, g):
    wt = i["L1_attn_w_qkv"].reshape(KC, P, 3, 16, P)[:, :, :, g * HG:(g + 1) * HG]
    return wt.transpose(1, 2, 3, 0, 4).reshape(P, 3 * HG * KC * P)


def pack_L1A(i):
    return [head_group(i, 0), tiles(i["L1_attn_w_o"])]


EXTRA_L1A = {"L1A_groups": lambda i: np.stack([head_group(i, g) for g in range(1, NG)])}


def layer_L1A(env):
    L = Layer(env, "L1A")
    nc, w = env.nc, env.weights("L1A")
    SCALE = P ** -0.5
    bank_x, bank_o = L.bank("xT"), L.bank("out")
    bank_qk = [L.bank(f"qk{j}") for j in range(2)]
    bank_v, bank_c = L.bank("v"), L.bank("colsum")
    bank_s = [L.bank(f"scores{j}") for j in range(2)]
    head = Head(L, bank_x)
    more = L.sb("groups", [P, NG - 1, 3 * HG * KC * P])
    qk = L.sb("qkT", [P, 2, HG, 2 * T])
    vT = L.sb("vT", [P, 2, HG, T])
    val = L.sb("scaled_vT", [P, 16, T])
    ex, pn = L.sb("exp", [P, 2, HG, P]), L.sb("probs", [P, 2, HG, P])
    mx, nmx, rsum, rinv = (L.sb(n, [P, 2, HG]) for n in ("max", "neg_max", "row_sum", "inv_sum"))
    s_load = [L.sem(f"group{g}_loaded") for g in range(1, NG)]
    s_chain, s_qk, s_qkc, s_v, s_vc, s_s, s_nm, s_e, s_pn, s_c, s_val, s_out = (L.sem(n) for n in (
        "dve_chain", "qk_done", "qk_copied", "v_done", "v_copied", "scores_done", "neg_max_ready", "exp_ready",
        "probs_ready", "colsum_done", "values_scaled", "out_done"))
    units = [(g, b) for g in range(NG) for b in range(B)]
    env.prefetch(L, "L1F")

    def wt(g, part, h, k):
        src = w("group0") if g == 0 else more[:, g - 1, :]
        at = ((part * HG + h) * KC + k) * P
        return src[:, at:at + P]

    with L.block() as block:
        @block.sync
        def _(sp):
            for g in range(1, NG):
                sp.dma_start(more[:, g - 1, :], env.dram["L1A_groups"][g - 1]).then_inc(s_load[g - 1], 16)
            env.issue_prefetch(sp)

        @block.tensor
        def _(pe):
            def project_group(g):
                if g:
                    pe.wait_ge(s_load[g - 1], 16)
                for h in range(HG):
                    n = g * HG + h
                    if n >= 2:
                        pe.wait_ge(s_qkc, n - 1)
                    for part in range(2):
                        for k in range(KC):
                            i = nc.tensor.matmul(bank_qk[n % 2][:, part * T:(part + 1) * T], wt(g, part, h, k), head.xT[:, k, :],
                                                 start=(k == 0), stop=(k == KC - 1))
                    i.then_inc(s_qk, 1)
                for j in range(HG // 2):
                    n = g * (HG // 2) + j
                    if n >= 1:
                        pe.wait_ge(s_vc, n)
                    for h in range(2):
                        for k in range(KC):
                            i = nc.tensor.matmul(bank_v[:, h * T:(h + 1) * T], wt(g, 2, 2 * j + h, k), head.xT[:, k, :],
                                                 start=(k == 0), stop=(k == KC - 1))
                    i.then_inc(s_v, 1)

            def scores(u):
                g, b = units[u]
                pe.wait_ge(s_qkc, (g + 1) * HG)
                if u >= 2:
                    pe.wait_ge(s_e, u - 1)
                for h in range(HG):
                    i = nc.tensor.matmul(bank_s[u % 2][:, h * P:(h + 1) * P], qk[:, g % 2, h, b * P:(b + 1) * P],
                                         qk[:, g % 2, h, T + b * P:T + (b + 1) * P], start=True, stop=True)
                i.then_inc(s_s, 1)

            def column_sums(u):
                pe.wait_ge(s_pn, u + 1)
                if u:
                    pe.wait_ge(s_val, u)
                nc.tensor.matmul(bank_c[:, :], env.const("ones"), pn[:, u % 2, :, :].rearrange("p h t -> p (h t)"),
                                 start=True, stop=True).then_inc(s_c, 1)

            env.wait_weights(pe, "L1A")
            head.tensor(pe)
            pe.wait_ge(head.s_xT, 1)
            project_group(0)
            for g in range(NG):
                for b in range(B):
                    scores(g * B + b)
                if g + 1 < NG:
                    project_group(g + 1)
                for b in range(B):
                    column_sums(g * B + b)
            pe.wait_ge(s_val, len(units))
            for b in range(B):
                for h in range(16):
                    i = nc.tensor.matmul(bank_o[:, b * D:(b + 1) * D], val[:, h, b * P:(b + 1) * P], w("w_o")[:, h * D:(h + 1) * D],
                                         start=(h == 0), stop=(h == 15))
            i.then_inc(s_out, 1)

        @block.gpsimd
        def _(pool):
            head.gpsimd(pool)

        @block.scalar
        def _(act):
            def copy_group(g):
                for h in range(HG):
                    n = g * HG + h
                    act.wait_ge(s_qk, n + 1)
                    if g >= 2 and h == 0:
                        act.wait_ge(s_s, (g - 1) * B)
                    nc.scalar.activation(qk[:, g % 2, h, :], bank_qk[n % 2][:, :], ACT.Copy).then_inc(s_qkc, 1)

            def exps(u):
                act.wait_ge(s_nm, u + 1)
                if u >= 2:
                    act.wait_ge(s_pn, u - 1)
                for h in range(HG):
                    i = nc.scalar.activation(ex[:, u % 2, h, :], bank_s[u % 2][:, h * P:(h + 1) * P], ACT.Exp,
                                             bias=nmx[:, u % 2, h:h + 1], scale=SCALE, accum_out=rsum[:, u % 2, h:h + 1])
                i.then_inc(s_e, 1)

            head.scalar(act)
            copy_group(0)
            for g in range(NG):
                for b in range(B):
                    exps(g * B + b)
                if g + 1 < NG:
                    copy_group(g + 1)

        @block.vector
        def _(dve):
            chain = Chain(dve, s_chain)
            head.vector(dve, chain)

            def copy_values(g):
                for j in range(HG // 2):
                    dve.wait_ge(s_v, g * (HG // 2) + j + 1)
                    nc.vector.tensor_copy(vT[:, g % 2, 2 * j:2 * j + 2, :].rearrange("p h t -> p (h t)"),
                                          bank_v[:, :]).then_inc(s_vc, 1)

            def maxima(u):
                dve.wait_ge(s_s, u + 1)
                if u >= 2:
                    dve.wait_ge(s_e, u - 1)
                chain(nc.vector.tensor_reduce(mx[:, u % 2, :], bank_s[u % 2][:, :].rearrange("p (h t) -> p h t", h=HG), AX, ALU.max))
                nc.vector.tensor_scalar(nmx[:, u % 2, :], mx[:, u % 2, :], -SCALE, None, ALU.mult).then_inc(s_nm, 1)

            def normalise(u):
                dve.wait_ge(s_e, u + 1)
                chain(nc.vector.reciprocal(rinv[:, u % 2, :], rsum[:, u % 2, :]))
                if u >= 2:
                    dve.wait_ge(s_c, u - 1)
                nc.vector.tensor_tensor(pn[:, u % 2, :, :], ex[:, u % 2, :, :],
                                        rinv[:, u % 2, :].unsqueeze(2).to_broadcast([P, HG, P]), ALU.mult).then_inc(s_pn, 1)

            def scale_values(u):
                g, b = units[u]
                dve.wait_ge(s_c, u + 1)
                nc.vector.tensor_tensor(val[:, g * HG:(g + 1) * HG, b * P:(b + 1) * P], vT[:, g % 2, :, b * P:(b + 1) * P],
                                        bank_c[:, :].rearrange("p (h t) -> p h t", h=HG), ALU.mult).then_inc(s_val, 1)

            copy_values(0)
            for g in range(NG):
                for b in range(B):
                    maxima(g * B + b)
                for b in range(B):
                    normalise(g * B + b)
                if g + 1 < NG:
                    copy_values(g + 1)
                for b in range(B):
                    scale_values(g * B + b)
            dve.wait_ge(s_out, 1)
            x = env.x[:, :, :].rearrange("p b d -> p (b d)")
            chain(nc.vector.tensor_tensor(x, x, bank_o[:, :], ALU.add))
    L.close()


L1F = Fields([("W", KC * D), ("norm", D)])
ROUND = 1.5 * 2.0 ** 23


def pack_L1F(i):
    return [tiles(i["L1_ffn_weight"].T), every_row(i["L1_ffn_norm_weight"])]


def layer_L1F(env):
    L = Layer(env, "L1F")
    nc, w = env.nc, env.weights("L1F")
    QP, QN, EPS_SCALE = 127.0, -128.0, 1e-5
    bank_x, bank_m, bank_w, bank_o = L.bank("xT"), L.bank("max"), L.bank("wsum"), L.bank("out")
    head = Head(L, bank_x)
    xr, sq = L.sb("x_rms", [P, B, D]), L.sb("squares", [P, B, D])
    ms = L.sb("mean_square", [P, B])
    inv = InvSqrt(L, "mean_square")
    ext = L.sb("extremes", [P, 2])
    amax, row, top = L.sb("abs_max", [P, 1]), L.sb("max_row", [1, 1]), L.sb("max_all", [P, 1])
    wabs, wsum, wsc, winv = L.sb("w_abs", [P, KC * D]), L.sb("w_sum", [P, 1]), L.sb("w_scale", [P, 1]), L.sb("w_inv", [P, 1])
    xinv, osc = L.sb("x_inv", [P, 1]), L.sb("out_scale", [P, 1])
    wt, wq = L.sb("w_scaled", [P, KC * D]), L.sb("w_ternary", [P, KC, D], BF16)
    xqT = L.sb("xqT", [P, KC, T], BF16)
    s_chain, s_wabs, s_wsum, s_ms, s_am, s_mT, s_row, s_top, s_xq, s_turn, s_xqT, s_wq, s_out = (L.sem(n) for n in (
        "dve_chain", "w_abs_ready", "w_sum_done", "mean_square_ready", "abs_max_ready", "max_turned", "row_max_ready", "max_spread",
        "x_quantised", "xq_turned", "xqT_ready", "w_quantised", "out_done"))
    env.prefetch(L, "L2X")

    with L.block() as block:
        @block.sync
        def _(sp):
            env.issue_prefetch(sp)

        @block.tensor
        def _(pe):
            pe.wait_ge(s_wabs, 1)
            nc.tensor.matmul(bank_w[:, 0:1], env.const("ones"), wsum[:, :], start=True, stop=True).then_inc(s_wsum, 1)
            pe.wait_ge(s_am, 1)
            nc.tensor.transpose(bank_m[0:1, 0:P], amax[:, :], env.const("ident")).then_inc(s_mT, 1)
            pe.wait_ge(s_row, 1)
            nc.tensor.matmul(bank_m[:, 0:1], env.const("ones")[0:1, :], row[:, :], start=True, stop=True).then_inc(s_top, 1)
            turn(L, pe, bank_x, xr, s_xq, 1, s_turn)
            pe.wait_ge(s_xqT, 1)
            pe.wait_ge(s_wq, 1)
            for b in range(B):
                for k in range(KC):
                    i = nc.tensor.matmul(bank_o[:, b * D:(b + 1) * D], xqT[:, k, b * P:(b + 1) * P], wq[:, k, :],
                                         start=(k == 0), stop=(k == KC - 1))
            i.then_inc(s_out, 1)

        @block.gpsimd
        def _(pool):
            head.gpsimd(pool)
            inv.gpsimd(pool)

        @block.scalar
        def _(act):
            env.wait_weights(act, "L1F")
            nc.scalar.activation(wabs[:, :], w("W"), ACT.Abs, accum_out=wsum[:, :]).then_inc(s_wabs, 1)
            act.wait_ge(s_turn, 1)
            nc.scalar.activation(xqT[:, :, :].rearrange("p k t -> p (k t)"), bank_x[:, :], ACT.Copy).then_inc(s_xqT, 1)

        @block.vector
        def _(dve):
            chain = Chain(dve, s_chain)
            head.vector(dve, chain)
            dve.wait_ge(head.s_norm, B)
            for b in range(B):
                i = nc.vector.tensor_tensor_reduce(out=sq[:, b, :], in0=head.xn[:, b, :], in1=head.xn[:, b, :], scale=1.0 / D,
                                                   scalar=0.0, op0=ALU.mult, op1=ALU.add, accum_out=ms[:, b:b + 1])
            chain(i)
            inv.vector(dve, ms[:, :], 1e-6)
            env.wait_weights(dve, "L1F")
            for b in range(B):
                i = nc.vector.scalar_tensor_tensor(out=xr[:, b, :], in0=head.xn[:, b, :], scalar=inv.out[:, b:b + 1],
                                                   in1=w("norm"), op0=ALU.mult, op1=ALU.mult)
            chain(i)
            flat = xr[:, :, :].rearrange("p b d -> p (b d)")
            nc.vector.tensor_reduce(ext[:, 0:1], flat, AX, ALU.max)
            chain(nc.vector.tensor_reduce(ext[:, 1:2], flat, AX, ALU.min))
            nc.vector.scalar_tensor_tensor(out=amax[:, :], in0=ext[:, 1:2], scalar=-1.0, in1=ext[:, 0:1], op0=ALU.mult,
                                           op1=ALU.max).then_inc(s_am, 1)
            dve.wait_ge(s_wsum, 1)
            chain(nc.vector.tensor_scalar(wsc[:, :], bank_w[:, 0:1], 1.0 / (D * D), EPS_SCALE, ALU.mult, ALU.max))
            chain(nc.vector.reciprocal(winv[:, :], wsc[:, :]))
            chain(nc.vector.tensor_scalar(wt[:, :], w("W"), winv[:, 0:1], 1.0, ALU.mult, ALU.min))
            chain(nc.vector.tensor_scalar(wt[:, :], wt[:, :], -1.0, ROUND, ALU.max, ALU.add))
            nc.vector.tensor_scalar(wq[:, :, :].rearrange("p k n -> p (k n)"), wt[:, :], ROUND, None,
                                    ALU.subtract).then_inc(s_wq, 1)
            dve.wait_ge(s_mT, 1)
            nc.vector.tensor_reduce(row[:, :], bank_m[0:1, 0:P], AX, ALU.max).then_inc(s_row, 1)
            dve.wait_ge(s_top, 1)
            chain(nc.vector.tensor_scalar(top[:, :], bank_m[:, 0:1], EPS_SCALE, None, ALU.max))
            chain(nc.vector.reciprocal(xinv[:, :], top[:, :]))
            chain(nc.vector.tensor_scalar(flat, flat, xinv[:, 0:1], QP, ALU.mult, ALU.mult))
            chain(nc.vector.tensor_scalar(flat, flat, QP, QN, ALU.min, ALU.max))
            nc.vector.tensor_scalar(flat, flat, ROUND, ROUND, ALU.add, ALU.subtract).then_inc(s_xq, 1)
            chain(nc.vector.tensor_scalar(osc[:, :], top[:, :], 1.0 / QP, wsc[:, 0:1], ALU.mult, ALU.mult))
            dve.wait_ge(s_out, 1)
            x = env.x[:, :, :].rearrange("p b d -> p (b d)")
            chain(nc.vector.scalar_tensor_tensor(out=x, in0=bank_o[:, :], scalar=osc[:, 0:1], in1=x, op0=ALU.mult, op1=ALU.add))
    L.close()


class SmallAttention:
    G = 4
    LOWEST = float(np.finfo(np.float32).min)

    def __init__(self, L, width, bank_s, bank_t, bank_o, mask):
        self.L, self.w, self.HT, self.NH = L, width, P // width, D // width
        self.bank_s, self.bank_t, self.bank_o, self.mask = bank_s, bank_t, bank_o, mask
        self.per = self.NH // self.G
        self.qT, self.kT = L.sb("self_qT", [P, KC, T]), L.sb("self_kT", [P, KC, T])
        self.qd = L.sb("self_q_blocks", [P, KC, self.HT, P])
        self.vo = L.sb("self_v_ones", [P, B, self.NH, width + 1])
        self.e, self.pT = L.sb("self_exp", [P, 2, self.G, P]), L.sb("self_probsT", [P, 2, self.G * P])
        self.mx, self.inv = L.sb("self_max", [P, 2, self.G]), L.sb("self_inv_den", [P, self.NH])
        self.s_qd, self.s_s, self.s_free, self.s_d, self.s_e, self.s_t, self.s_pT, self.s_o, self.s_y = (L.sem(n) for n in (
            "q_blocks_ready", "self_scores_done", "self_scores_taken", "self_shifted", "self_exp_ready", "self_turned",
            "self_probsT_ready", "self_read_step", "self_out_ready"))

    def query_blocks(self, b):
        nc, ht = self.L.nc, self.HT
        sel = self.L.env.const("head16" if self.w == 16 else "head8")
        for c in range(KC):
            i = nc.vector.tensor_tensor(self.qd[:, c, :, :], self.qT[:, c, b * P:(b + 1) * P].unsqueeze(1).to_broadcast([P, ht, P]),
                                        sel.unsqueeze(2).to_broadcast([P, ht, P]), ALU.mult)
        i.then_inc(self.s_qd, 1)

    def tensor(self, pe, b):
        nc, G = self.L.nc, self.G

        def scores(g):
            m = b * self.per + g
            if m >= 2:
                pe.wait_ge(self.s_free, m - 1)
            for h in range(G):
                c, j = divmod(g * G + h, self.HT)
                i = nc.tensor.matmul(self.bank_s[m % 2][:, h * P:(h + 1) * P], self.qd[:, c, j, :],
                                     self.kT[:, c, b * P:(b + 1) * P], start=True, stop=True)
            i.then_inc(self.s_s, 1)

        def turn_exp(g):
            m = b * self.per + g
            pe.wait_ge(self.s_e, m + 1)
            if m >= 2:
                pe.wait_ge(self.s_pT, m - 1)
            for h in range(G):
                i = nc.tensor.transpose(self.bank_t[m % 2][:, h * P:(h + 1) * P], self.e[:, m % 2, h, :], self.L.env.const("ident"))
            i.then_inc(self.s_t, 1)

        def read(g):
            m = b * self.per + g
            pe.wait_ge(self.s_pT, m + 1)
            for h in range(G):
                at = (g * G + h) * (self.w + 1)
                i = nc.tensor.matmul(self.bank_o[b][:, at:at + self.w + 1], self.pT[:, m % 2, h * P:(h + 1) * P],
                                     self.vo[:, b, g * G + h, :], start=True, stop=True)
            i.then_inc(self.s_o, 1)

        pe.wait_ge(self.s_qd, b + 1)
        scores(0)
        for g in range(self.per):
            if g + 1 < self.per:
                scores(g + 1)
            turn_exp(g)
            if g:
                read(g - 1)
        read(self.per - 1)

    def scalar(self, act, b):
        nc = self.L.nc

        def copy(m):
            act.wait_ge(self.s_t, m + 1)
            if m >= 2:
                act.wait_ge(self.s_o, m - 1)
            nc.scalar.activation(self.pT[:, m % 2, :], self.bank_t[m % 2][:, :], ACT.Copy).then_inc(self.s_pT, 1)

        for g in range(self.per):
            m = b * self.per + g
            act.wait_ge(self.s_d, m + 1)
            nc.scalar.activation(self.e[:, m % 2, :, :], self.e[:, m % 2, :, :], ACT.Exp).then_inc(self.s_e, 1)
            if g:
                copy(m - 1)
        copy((b + 1) * self.per - 1)

    def vector(self, dve, chain, b):
        nc, G = self.L.nc, self.G
        for g in range(self.per):
            m = b * self.per + g
            dve.wait_ge(self.s_s, m + 1)
            if m >= 2:
                dve.wait_ge(self.s_t, m - 1)
            s = self.e[:, m % 2, :, :]
            nc.vector.scalar_tensor_tensor(out=s, in0=self.bank_s[m % 2][:, :].rearrange("p (h k) -> p h k", h=G),
                                           scalar=self.w ** -0.5, in1=self.mask(b).unsqueeze(1).to_broadcast([P, G, P]),
                                           op0=ALU.mult, op1=ALU.add).then_inc(self.s_free, 1)
            dve.wait_ge(self.s_free, m + 1)
            chain(nc.vector.tensor_reduce(self.mx[:, m % 2, :], s, AX, ALU.max))
            chain(nc.vector.tensor_scalar(self.mx[:, m % 2, :], self.mx[:, m % 2, :], self.LOWEST, None, ALU.max))
            nc.vector.scalar_tensor_tensor(out=s, in0=s, scalar=self.LOWEST,
                                           in1=self.mx[:, m % 2, :].unsqueeze(2).to_broadcast([P, G, P]),
                                           op0=ALU.max, op1=ALU.subtract).then_inc(self.s_d, 1)

    def finish(self, dve, chain, b, y):
        nc = self.L.nc
        dve.wait_ge(self.s_o, (b + 1) * self.per)
        o = self.bank_o[b][:, 0:self.NH * (self.w + 1)].rearrange("p (h e) -> p h e", h=self.NH)
        chain(nc.vector.reciprocal(self.inv[:, :], o[:, :, self.w]))
        return nc.vector.tensor_tensor(y[:, b, :].rearrange("p (h e) -> p h e", h=self.NH), o[:, :, 0:self.w],
                                       self.inv[:, :].unsqueeze(2).to_broadcast([P, self.NH, self.w]), ALU.mult)


L2X = Fields([("Wq", KC * D), ("Wk", KC * D), ("Wv", KC * D), ("Wo", KC * D), ("gate", 32)])


def pack_L2X(i):
    return [tiles(i[f"L2_xattn_W{n}"]) for n in "qkvo"] + [every_row(i["L2_xattn_gate"])]


EXTRA_L2X = {"L2X_mask": lambda i: i["mask_Bx1xSxS_fk0"].reshape(B, P, P).transpose(1, 0, 2).reshape(P, B * P)}


def layer_L2X(env):
    L = Layer(env, "L2X")
    nc, w = env.nc, env.weights("L2X")
    wq, wk, wv = (w(n).rearrange("p (k n) -> p k n", k=KC) for n in ("Wq", "Wk", "Wv"))
    NH, HD, HT = 32, 8, 16
    VW, SCALE = HD + 1, HD ** -0.5
    NS = 5
    bank_s = [L.bank(f"scores{j}") for j in range(NS)]
    bank_t = [L.bank(f"turn{j}") for j in range(2)]
    bank_o = L.bank("read")
    bank_m = bank_s[4]
    head = Head(L, bank_m)
    y = L.sb("y", [P, B, D])
    tail = Tail(L, y, bank_m, bank_t[0], w("Wo"))
    maskt = L.sb("mask", [P, B * P])
    at = SmallAttention(L, HD, bank_s[2:4], bank_t, [bank_o, bank_o], lambda b: maskt[:, b * P:(b + 1) * P])
    q, k = L.sb("q", [P, B, D]), L.sb("k", [P, B, D])
    qr, kr, tmp = L.sb("q_rope", [P, B, D]), L.sb("k_rope", [P, B, D]), L.sb("rope_tmp", [P, B, D])
    cT = L.sb("context_kT", [P, KC, S2])
    cvp = L.sb("context_v_ones", [P, NT, NH * VW + 32 - VW])
    cv = cvp[:, :, 0:NH * VW].rearrange("p t (h e) -> p t h e", e=VW)
    NE, NP = 6, 3
    ex, pT = L.sb("context_exp", [P, NE, 512]), L.sb("context_probsT", [P, NP, 512])
    mx4, mx, nmx = L.sb("max_parts", [P, 2, 4]), L.sb("max", [P, 2]), L.sb("neg_max", [P, 2])
    oT = L.sb("context_readT", [P, 512])
    tg, inv, ya = L.sb("tanh_gate", [P, NH]), L.sb("inv_den", [P, NH]), L.sb("context_out", [P, D])
    names = ("dve_chain", "mask_loaded", "gate_tanh", "q_done", "k_done", "v_done", "qk_copied", "v_copied", "q_rope_ready", "k_rope_ready",
             "q_turned", "k_turned", "q_rope_copied", "k_rope_copied", "ck_done", "ck_copied", "cv_done", "cv_copied", "scores_done",
             "neg_max_ready", "exp_ready", "turned", "copied_by_dve", "copied_by_act", "read_done", "read_taken",
             "readT_copied", "read_turned")
    (s_chain, s_mask, s_tg, s_q, s_k, s_v, s_qkc, s_vc, s_qr, s_kr, s_qt, s_kt, s_qTc, s_kTc, s_ck, s_ckc, s_cv, s_cvc, s_s,
     s_nm, s_e, s_t, s_td, s_ta, s_o, s_taken,
     s_oc, s_ot) = (L.sem(n) for n in names)
    NJ = 8
    env.prefetch(L, "L2A")

    NBLK = NH * 4
    AHEAD = 5

    def wait_copied(eng, n):
        eng.wait_ge(s_ta if n % 2 else s_td, n // 2 + 1)

    with L.block() as block:
        @block.sync
        def _(sp):
            sp.dma_start(maskt[:, :], env.dram["L2X_mask"]).then_inc(s_mask, 16)
            env.issue_prefetch(sp)

        @block.tensor
        def _(pe):
            def context_projections(b):
                for j in range(NJ):
                    c4, c = j // KC, j % KC
                    env.wait_context(pe, b, 4 * c4)
                    if j >= 2:
                        pe.wait_ge(s_ckc, b * NJ + j - 1)
                    for kk in range(KC):
                        i = nc.tensor.matmul(bank_s[j % 2][:, :], wk[:, kk, c * P:(c + 1) * P], env.ctx4(kk, b, c4),
                                             start=(kk == 0), stop=(kk == KC - 1))
                    i.then_inc(s_ck, 1)
                    if j >= 2:
                        pe.wait_ge(s_cvc, b * NJ + j - 1)
                    for u in range(2):
                        for kk in range(KC):
                            i = nc.tensor.matmul(bank_t[j % 2][:, u * D:(u + 1) * D], env.ctx(kk, b, 2 * j + u), wv[:, kk, :],
                                                 start=(kk == 0), stop=(kk == KC - 1))
                    i.then_inc(s_cv, 1)

            def scores(b, m):
                (c, hh), j, n = divmod(m // 4, HT), m % 4, b * NBLK + m
                if m >= NS:
                    pe.wait_ge(s_e, n - NS + 1)
                nc.tensor.matmul(bank_s[m % NS][:, :], at.qd[:, c, hh, :], cT[:, c, j * 512:(j + 1) * 512],
                                 start=True, stop=True).then_inc(s_s, 1)

            def turn_exp(b, m):
                n = b * NBLK + m
                pe.wait_ge(s_e, n + 1)
                if n >= 2:
                    wait_copied(pe, n - 2)
                for u in range(4):
                    i = nc.tensor.transpose(bank_t[n % 2][:, u * P:(u + 1) * P], ex[:, n % NE, u * P:(u + 1) * P], env.const("ident"))
                i.then_inc(s_t, 1)

            def read(b, m):
                h, j, n = m // 4, m % 4, b * NBLK + m
                wait_copied(pe, n)
                lo, at_col = 32 * (h % 4), (h // 4 % 4) * P
                if m % 64 == 0:
                    pe.wait_ge(s_taken, 3 * b + 1 + m // 64)
                for u in range(4):
                    i = nc.tensor.matmul(bank_o[lo:lo + 32, at_col:at_col + P], cvp[:, 4 * j + u, h * VW:h * VW + 32],
                                         pT[:, n % NP, u * P:(u + 1) * P], start=(j == 0 and u == 0), stop=(j == 3 and u == 3))
                i.then_inc(s_o, 1)
                if m % 64 == 63:
                    q = 2 * b + m // 64
                    pe.wait_ge(s_oc, q + 1)
                    for u in range(4):
                        i = nc.tensor.transpose(bank_o[:, u * P:(u + 1) * P], oT[:, u * P:(u + 1) * P], env.const("ident"))
                    i.then_inc(s_ot, 1)

            env.wait_weights(pe, "L2X")
            head.tensor(pe)
            pe.wait_ge(head.s_xT, 1)
            project(L, bank_s[0], wq, head.xT).then_inc(s_q, 1)
            project(L, bank_s[1], wk, head.xT).then_inc(s_k, 1)
            project(L, bank_s[2], wv, head.xT).then_inc(s_v, 1)
            pe.wait_ge(s_qkc, 2)
            context_projections(0)
            turn(L, pe, bank_m, qr, s_qr, 1, s_qt)
            pe.wait_ge(s_qTc, 1)
            turn(L, pe, bank_m, kr, s_kr, 1, s_kt)
            pe.wait_ge(s_kTc, 1)
            pe.wait_ge(s_vc, 1)
            for b in range(B):
                if b:
                    pe.wait_ge(s_e, b * NBLK)
                    wait_copied(pe, b * NBLK - 1)
                    wait_copied(pe, b * NBLK - 2)
                    context_projections(b)
                    pe.wait_ge(s_taken, 3 * b)
                pe.wait_ge(s_cvc, (b + 1) * NJ)
                at.tensor(pe, b)
                pe.wait_ge(s_ckc, (b + 1) * NJ)
                pe.wait_ge(at.s_free, (b + 1) * at.per)
                for m in range(NBLK + AHEAD + 1):
                    if m < NBLK:
                        scores(b, m)
                    if 0 <= m - AHEAD < NBLK:
                        turn_exp(b, m - AHEAD)
                    if m - AHEAD - 1 >= 0:
                        read(b, m - AHEAD - 1)
            tail.tensor(pe)

        @block.gpsimd
        def _(pool):
            head.gpsimd(pool)

        @block.scalar
        def _(act):
            env.wait_weights(act, "L2X")
            nc.scalar.activation(tg[:, :], w("gate"), ACT.Tanh).then_inc(s_tg, 1)
            head.scalar(act)
            act.wait_ge(s_q, 1)
            nc.scalar.activation(q[:, :, :].rearrange("p b n -> p (b n)"), bank_s[0][:, :], ACT.Copy).then_inc(s_qkc, 1)
            act.wait_ge(s_k, 1)
            nc.scalar.activation(k[:, :, :].rearrange("p b n -> p (b n)"), bank_s[1][:, :], ACT.Copy).then_inc(s_qkc, 1)
            for b in range(B):
                for j in range(NJ):
                    c4, c = j // KC, j % KC
                    act.wait_ge(s_ck, b * NJ + j + 1)
                    nc.scalar.activation(cT[:, c, c4 * 512:(c4 + 1) * 512], bank_s[j % 2][:, :], ACT.Copy).then_inc(s_ckc, 1)
                if b == 0:
                    act.wait_ge(s_qt, 1)
                    nc.scalar.activation(at.qT[:, :, :].rearrange("p c t -> p (c t)"), bank_m[:, :], ACT.Copy).then_inc(s_qTc, 1)
                    act.wait_ge(s_kt, 1)
                    nc.scalar.activation(at.kT[:, :, :].rearrange("p c t -> p (c t)"), bank_m[:, :], ACT.Copy).then_inc(s_kTc, 1)
                at.scalar(act, b)

                for m in range(4, NBLK + AHEAD + 2):
                    done, n = m - 4, b * NBLK + m - 4
                    if done < NBLK:
                        if done % 4 == 0:
                            act.wait_ge(s_nm, n // 4 + 1)
                        if n >= NE:
                            act.wait_ge(s_t, n - NE + 1)
                        col = (n // 4) % 2
                        nc.scalar.activation(ex[:, n % NE, :], bank_s[done % NS][:, :], ACT.Exp, bias=nmx[:, col:col + 1],
                                             scale=SCALE).then_inc(s_e, 1)
                    turned, n = m - AHEAD, b * NBLK + m - AHEAD
                    if 0 <= turned < NBLK and n % 2:
                        act.wait_ge(s_t, n + 1)
                        if n >= NP:
                            act.wait_ge(s_o, n - NP + 1)
                        nc.scalar.activation(pT[:, n % NP, :], bank_t[n % 2][:, :], ACT.Copy).then_inc(s_ta, 1)
                    read = m - AHEAD - 1
                    if read >= 0 and read % 64 == 63:
                        act.wait_ge(s_o, b * NBLK + read + 1)
                        nc.scalar.activation(oT[:, :], bank_o[:, :], ACT.Copy).then_inc(s_oc, 1)
            tail.scalar(act)

        @block.vector
        def _(dve):
            chain = Chain(dve, s_chain)

            def rope(dst, src, s_done):
                v = [a[:, :, :].rearrange("p b (h e) -> p (b h) e", e=HD) for a in (dst, src, tmp)]
                cos, sin = (env.const(n).unsqueeze(1).to_broadcast([P, B * NH, HD]) for n in ("cos8", "sin8"))
                half = HD // 2
                nc.vector.tensor_tensor(v[2][:, :, 0:half], v[1][:, :, half:HD], sin[:, :, 0:half], ALU.mult)
                nc.vector.tensor_tensor(v[2][:, :, half:HD], v[1][:, :, 0:half], sin[:, :, half:HD], ALU.mult)
                chain(nc.vector.tensor_tensor(v[0], v[1], cos, ALU.mult))
                nc.vector.tensor_tensor(v[0], v[0], v[2], ALU.add).then_inc(s_done, 1)
                dve.wait_ge(s_done, 1)

            nc.vector.memset(at.vo[:, :, :, HD:VW], 1.0)
            chain(nc.vector.memset(cvp[:, :, :], 1.0))
            head.vector(dve, chain)
            dve.wait_ge(s_v, 1)
            nc.vector.tensor_copy(at.vo[:, :, :, 0:HD], bank_s[2][:, :].rearrange("p (b h e) -> p b h e", b=B, h=NH)).then_inc(s_vc, 1)
            dve.wait_ge(s_qkc, 1)
            rope(qr, q, s_qr)
            dve.wait_ge(s_qkc, 2)
            rope(kr, k, s_kr)
            dve.wait_ge(s_mask, 16)
            for b in range(B):
                for j in range(NJ):
                    dve.wait_ge(s_cv, b * NJ + j + 1)
                    nc.vector.tensor_copy(cv[:, 2 * j:2 * j + 2, :, 0:HD],
                                          bank_t[j % 2][:, :].rearrange("p (t h e) -> p t h e", t=2, h=NH)).then_inc(s_cvc, 1)
                if b == 0:
                    dve.wait_ge(s_qTc, 1)
                at.query_blocks(b)
                at.vector(dve, chain, b)
                at.finish(dve, chain, b, y).then_inc(s_taken, 1)
                dve.wait_ge(s_taken, 3 * b + 1)

                for m in range(NBLK + AHEAD + 2):
                    if m < NBLK:
                        n, u = b * NBLK + m, (b * NBLK + m) // 4 % 2
                        dve.wait_ge(s_s, n + 1)
                        i = nc.vector.tensor_reduce(mx4[:, u, m % 4:m % 4 + 1], bank_s[m % NS][:, :], AX, ALU.max)
                        if m % 4 == 3:
                            chain(i)
                            chain(nc.vector.tensor_reduce(mx[:, u:u + 1], mx4[:, u, :], AX, ALU.max))
                            if n >= 8:
                                dve.wait_ge(s_e, n - 7)
                            nc.vector.tensor_scalar(nmx[:, u:u + 1], mx[:, u:u + 1], -SCALE, None, ALU.mult).then_inc(s_nm, 1)
                    n = b * NBLK + m - AHEAD
                    if 0 <= m - AHEAD < NBLK and n % 2 == 0:
                        dve.wait_ge(s_t, n + 1)
                        if n >= NP:
                            dve.wait_ge(s_o, n - NP + 1)
                        nc.vector.tensor_copy(pT[:, n % NP, :], bank_t[n % 2][:, :]).then_inc(s_td, 1)
                    read = m - AHEAD - 1
                    if read >= 0 and read % 64 == 63:
                        part = read // 64
                        dve.wait_ge(s_ot, 2 * b + part + 1)
                        o = bank_o[:, :].rearrange("p (h e) -> p h e", h=HT)
                        hs = slice(part * HT, (part + 1) * HT)
                        chain(nc.vector.reciprocal(inv[:, hs], o[:, :, HD]))
                        if part == 0 and b == 0:
                            dve.wait_ge(s_tg, 1)
                        chain(nc.vector.tensor_tensor(inv[:, hs], inv[:, hs], tg[:, hs], ALU.mult))
                        yh = y[:, b, part * P:(part + 1) * P]
                        nc.vector.tensor_tensor(ya[:, part * P:(part + 1) * P].rearrange("p (h e) -> p h e", h=HT), o[:, :, 0:HD],
                                                inv[:, hs].unsqueeze(2).to_broadcast([P, HT, HD]), ALU.mult).then_inc(s_taken, 1)
                        dve.wait_ge(s_taken, 3 * b + part + 2)
                        i = nc.vector.tensor_tensor(yh, yh, ya[:, part * P:(part + 1) * P], ALU.add)
                        if part == 0:
                            chain(i)
                        else:
                            i.then_inc(tail.s_y, 1)
                            dve.wait_ge(tail.s_y, b + 1)
            tail.vector(dve, chain)
    L.close()


NK, RH, TOP, EMB = 45, 8, 8, P + D
L2F = Fields([("Wup", KC * HID), ("bup", HC), ("Wdown", HC * P), ("bdown", 1), ("bdown_row", P), ("Wq", 2 * RH * 64),
              ("keys", RH * 2 * NK)])


def pack_L2F(i):
    p = "L2_ffn_"
    keys = np.zeros((P, RH, 2 * NK), np.float32)
    kt = i[p + "keys"].transpose(2, 0, 3, 1)
    for j in range(RH):
        for u in range(2):
            keys[u * 64:(u + 1) * 64, j, u * NK:(u + 1) * NK] = kt[j // 4, 2 * (j % 4) + u]
    return [tiles(i[p + "W_up"].T), per_channel(i[p + "b_up"]), tiles(i[p + "W_down"].T), per_channel(i[p + "b_down"]),
            every_row(i[p + "b_down"]), tiles(i[p + "W_q"].T), keys.reshape(P, RH * 2 * NK)]


EXTRA_L2F = {"L2F_embed": lambda i: np.concatenate([i["L2_ffn_down_embed"], i["L2_ffn_up_embed"]], 1)}


def layer_L2F(env):
    L = Layer(env, "L2F")
    nc, w = env.nc, env.weights("L2F")
    wup = w("Wup").rearrange("p (k n) -> p k n", k=KC)
    bank_x, bank_h, bank_n = L.bank("xT"), L.bank("hT"), L.bank("h")
    bank_p = [L.bank(f"proj{j}") for j in range(2)]
    bank_s = [L.bank(f"sim{j}") for j in range(3)]
    head = Head(L, bank_x)
    g, e = L.sb("up_pre", [P, 2, 512]), L.sb("up_exp", [P, 2, 512])
    h1 = L.sb("up", [P, HC, T])
    hT, hn = L.sb("hT", [P, T]), L.sb("h", [P, B, P])
    qT = L.sb("qT", [P, RH, T])
    sim = L.sb("sim", [P, B, 2, RH, NK])
    v8, i8, f8 = L.sb("top_values", [P, B, 2, RH, TOP]), L.sb("top_index", [P, B, 2, RH, TOP], U32), L.sb("top_index_f", [P, B, 2, RH, TOP])
    pairs = L.sb("pair_scores", [P, B, RH, TOP, TOP])
    s8, pk, pf = L.sb("pair_top", [P, B, RH, TOP]), L.sb("pair_pos", [P, B, RH, TOP], U32), L.sb("pair_pos_f", [P, B, RH, TOP])
    pa, pb = L.sb("pair_x", [P, B, RH, TOP]), L.sb("pair_y", [P, B, RH, TOP])
    eq = L.sb("equal", [P, RH, TOP, TOP])
    ix, iy = L.sb("index_x", [P, B, RH, TOP]), L.sb("index_y", [P, B, RH, TOP])
    idx = L.sb("expert", [P, B, RH, TOP], U32)
    soft, ssum = L.sb("softmax", [P, B, RH, TOP]), L.sb("softmax_sum", [P, B, RH])
    NR = 4
    rows = L.sb("rows", [P, NR, TOP, EMB])
    junk, zz = L.sb("products", [P, P]), L.sb("z", [P, 2, TOP])
    ze, wt = L.sb("z_exp", [P, 2, TOP]), L.sb("expert_weight", [P, 2, TOP])
    acc = L.sb("acc", [P, B, D])
    names = ("dve_chain", "up_done", "up_pre_ready", "up_exp_ready", "up_ready", "hT_done", "hT_ready", "h_done", "q_done",
             "q_copied", "sim_done", "sim_copied", "shifted", "softmax_exp", "experts_ready", "z_ready", "z_exp_ready", "rows_used")
    (s_chain, s_up, s_pre, s_ue, s_h1, s_h, s_hT, s_hn, s_q, s_qc, s_sim, s_simc, s_sh, s_se, s_idx, s_z, s_ze,
     s_used) = (L.sem(n) for n in names)
    s_rows = [L.sem(f"rows_gathered{r}") for r in range(NR)]
    JOBS = HC // 2
    chunks = [(b, h) for b in range(B) for h in range(RH)]
    env.prefetch(L, "L3X")

    with L.block() as block:
        @block.sync
        def _(sp):
            env.issue_prefetch(sp)

        @block.tensor
        def _(pe):
            env.wait_weights(pe, "L2F")
            head.tensor(pe)
            pe.wait_ge(head.s_xT, 1)
            for j in range(JOBS):
                if j >= 2:
                    pe.wait_ge(s_pre, j - 1)
                for m in range(2):
                    at = (2 * j + m) * P
                    for k in range(KC):
                        i = nc.tensor.matmul(bank_p[j % 2][:, m * T:(m + 1) * T], wup[:, k, at:at + P], head.xT[:, k, :],
                                             start=(k == 0), stop=(k == KC - 1))
                i.then_inc(s_up, 1)
            pe.wait_ge(s_h1, JOBS)
            for m in range(HC):
                i = nc.tensor.matmul(bank_h[:, 0:T], w("Wdown")[:, m * P:(m + 1) * P], h1[:, m, :], start=(m == 0), stop=(m == HC - 1))
            i.then_inc(s_h, 1)
            for b in range(B):
                for m in range(HC):
                    i = nc.tensor.matmul(bank_n[:, b * P:(b + 1) * P], h1[:, m, b * P:(b + 1) * P], w("Wdown")[:, m * P:(m + 1) * P],
                                         start=(m == 0), stop=(m == HC - 1))
            i.then_inc(s_hn, 1)
            pe.wait_ge(s_hT, 1)
            for j in range(RH // 2):
                if j >= 2:
                    pe.wait_ge(s_qc, j - 1)
                for u in range(2):
                    n = 2 * j + u
                    i = nc.tensor.matmul(bank_p[j % 2][:, u * T:(u + 1) * T], w("Wq")[:, n * P:(n + 1) * P], hT[:, :],
                                         start=True, stop=True)
                i.then_inc(s_q, 1)
            pe.wait_ge(s_qc, RH // 2)
            for n in range(2 * B):
                b, half = divmod(n, 2)
                if n >= 3:
                    pe.wait_ge(s_simc, n - 2)
                for u in range(4):
                    j = half * 4 + u
                    i = nc.tensor.matmul(bank_s[n % 3][:, u * 2 * NK:(u + 1) * 2 * NK], qT[:, j, b * P:(b + 1) * P],
                                         w("keys")[:, j * 2 * NK:(j + 1) * 2 * NK], start=True, stop=True)
                i.then_inc(s_sim, 1)

        @block.gpsimd
        def _(pool):
            head.gpsimd(pool)
            for n, (b, h) in enumerate(chunks):
                if h == 0:
                    pool.wait_ge(s_idx, b + 1)
                if n >= NR:
                    pool.wait_ge(s_used, n - NR + 1)
                for k in range(TOP):
                    pool.indirect_dma_start(out=rows[:, n % NR, k, :], out_offset=None, in_=env.dram["L2F_embed"],
                                            in_offset=bass.IndirectOffsetOnAxis(idx[:, b, h, k:k + 1], axis=0)).then_inc(s_rows[n % NR], 16)

        @block.scalar
        def _(act):
            head.scalar(act)
            env.wait_weights(act, "L2F")
            for j in range(JOBS):
                act.wait_ge(s_up, j + 1)
                if j >= 2:
                    act.wait_ge(s_h1, j - 1)
                for m in range(2):
                    n = 2 * j + m
                    i = nc.scalar.activation(g[:, j % 2, m * T:(m + 1) * T], bank_p[j % 2][:, m * T:(m + 1) * T], ACT.Identity,
                                             bias=w("bup")[:, n:n + 1])
                i.then_inc(s_pre, 1)
                act.wait_ge(s_pre, j + 1)
                nc.scalar.activation(e[:, j % 2, :], g[:, j % 2, :], ACT.Exp, scale=-1.0).then_inc(s_ue, 1)
            act.wait_ge(s_h, 1)
            nc.scalar.activation(hT[:, :], bank_h[:, 0:T], ACT.Identity, bias=w("bdown")).then_inc(s_hT, 1)
            for j in range(RH // 2):
                act.wait_ge(s_q, j + 1)
                nc.scalar.activation(qT[:, 2 * j:2 * j + 2, :].rearrange("p j t -> p (j t)"), bank_p[j % 2][:, :], ACT.Copy).then_inc(s_qc, 1)
            for n in range(2 * B):
                b, half = divmod(n, 2)
                act.wait_ge(s_sim, n + 1)
                nc.scalar.activation(sim[:, b, half, :, :].rearrange("p h k -> p (h k)"), bank_s[n % 3][:, 0:RH * NK],
                                     ACT.Copy).then_inc(s_simc, 1)
            for b in range(B):
                act.wait_ge(s_sh, b + 1)
                nc.scalar.activation(soft[:, b, :, :], soft[:, b, :, :], ACT.Exp).then_inc(s_se, 1)
            for n in range(len(chunks)):
                act.wait_ge(s_z, n + 1)
                nc.scalar.activation(ze[:, n % 2, :], zz[:, n % 2, :], ACT.Exp, scale=-1.0).then_inc(s_ze, 1)

        @block.vector
        def _(dve):
            chain = Chain(dve, s_chain)
            chain(nc.vector.memset(acc[:, :, :], 0.0))
            head.vector(dve, chain)
            for j in range(JOBS):
                dve.wait_ge(s_ue, j + 1)
                chain(nc.vector.tensor_scalar(e[:, j % 2, :], e[:, j % 2, :], 1.0, None, ALU.add))
                chain(nc.vector.reciprocal(e[:, j % 2, :], e[:, j % 2, :]))
                nc.vector.tensor_tensor(h1[:, 2 * j:2 * j + 2, :].rearrange("p m t -> p (m t)"), g[:, j % 2, :], e[:, j % 2, :],
                                        ALU.mult).then_inc(s_h1, 1)
            dve.wait_ge(s_hn, 1)
            env.wait_weights(dve, "L2F")
            chain(nc.vector.tensor_tensor(hn[:, :, :], bank_n[:, 0:B * P].rearrange("p (b n) -> p b n", b=B),
                                          w("bdown_row").unsqueeze(1).to_broadcast([P, B, P]), ALU.add))

            def choose(b):
                for half in range(2):
                    dve.wait_ge(s_simc, 2 * b + half + 1)
                    for h in range(RH):
                        i = nc.vector.max(v8[:, b, half, h, :], sim[:, b, half, h, :])
                chain(i)
                for half in range(2):
                    for h in range(RH):
                        i = nc.vector.max_index(i8[:, b, half, h, :], v8[:, b, half, h, :], sim[:, b, half, h, :])
                chain(i)
                nc.vector.tensor_copy(f8[:, b, :, :, :], i8[:, b, :, :, :])
                chain(nc.vector.tensor_tensor(pairs[:, b, :, :, :], v8[:, b, 0, :, :].unsqueeze(3).to_broadcast([P, RH, TOP, TOP]),
                                              v8[:, b, 1, :, :].unsqueeze(2).to_broadcast([P, RH, TOP, TOP]), ALU.add))
                for h in range(RH):
                    i = nc.vector.max(s8[:, b, h, :], pairs[:, b, h, :, :].rearrange("p x y -> p (x y)"))
                chain(i)
                for h in range(RH):
                    i = nc.vector.max_index(pk[:, b, h, :], s8[:, b, h, :], pairs[:, b, h, :, :].rearrange("p x y -> p (x y)"))
                chain(i)
                nc.vector.tensor_tensor(soft[:, b, :, :], s8[:, b, :, :], s8[:, b, :, 0:1].to_broadcast([P, RH, TOP]),
                                        ALU.subtract).then_inc(s_sh, 1)
                chain(nc.vector.tensor_copy(pf[:, b, :, :], pk[:, b, :, :]))
                chain(nc.vector.tensor_scalar(pa[:, b, :, :], pf[:, b, :, :], 1.0 / TOP, 0.5 / TOP - 0.5, ALU.mult, ALU.add))
                chain(nc.vector.tensor_scalar(pa[:, b, :, :], pa[:, b, :, :], ROUND, ROUND, ALU.add, ALU.subtract))
                chain(nc.vector.scalar_tensor_tensor(out=pb[:, b, :, :], in0=pa[:, b, :, :], scalar=-float(TOP), in1=pf[:, b, :, :],
                                                     op0=ALU.mult, op1=ALU.add))
                for half, (pos, dst) in enumerate(((pa, ix), (pb, iy))):
                    for h in range(RH):
                        i = nc.vector.tensor_tensor(eq[:, h, :, :], pos[:, b, h, :].unsqueeze(2).to_broadcast([P, TOP, TOP]),
                                                    env.const("eight").unsqueeze(1).to_broadcast([P, TOP, TOP]), ALU.is_equal)
                    chain(i)
                    chain(nc.vector.tensor_tensor(eq[:, :, :, :], eq[:, :, :, :],
                                                  f8[:, b, half, :, :].unsqueeze(2).to_broadcast([P, RH, TOP, TOP]), ALU.mult))
                    chain(nc.vector.tensor_reduce(dst[:, b, :, :], eq[:, :, :, :], AX, ALU.add))
                nc.vector.scalar_tensor_tensor(out=idx[:, b, :, :], in0=ix[:, b, :, :], scalar=float(NK), in1=iy[:, b, :, :],
                                               op0=ALU.mult, op1=ALU.add).then_inc(s_idx, 1)
                dve.wait_ge(s_se, b + 1)
                chain(nc.vector.tensor_reduce(ssum[:, b, :], soft[:, b, :, :], AX, ALU.add))
                chain(nc.vector.reciprocal(ssum[:, b, :], ssum[:, b, :]))
                chain(nc.vector.tensor_tensor(soft[:, b, :, :], soft[:, b, :, :], ssum[:, b, :].unsqueeze(2).to_broadcast([P, RH, TOP]),
                                              ALU.mult))

            def products(n):
                b, h = chunks[n]
                dve.wait_ge(s_rows[n % NR], 16 * TOP * (n // NR + 1))
                if n >= 2:
                    dve.wait_ge(s_ze, n - 1)
                for k in range(TOP):
                    i = nc.vector.tensor_tensor_reduce(out=junk[:, :], in0=rows[:, n % NR, k, 0:P], in1=hn[:, b, :], scale=1.0, scalar=0.0,
                                                       op0=ALU.mult, op1=ALU.add, accum_out=zz[:, n % 2, k:k + 1])
                    chain(i)
                nc.vector.tensor_tensor(zz[:, n % 2, :], zz[:, n % 2, :], soft[:, b, h, :], ALU.mult).then_inc(s_z, 1)

            def weighted_sum(n):
                b, h = chunks[n]
                dve.wait_ge(s_ze, n + 1)
                chain(nc.vector.tensor_scalar(ze[:, n % 2, :], ze[:, n % 2, :], 1.0, None, ALU.add))
                chain(nc.vector.reciprocal(ze[:, n % 2, :], ze[:, n % 2, :]))
                dve.wait_ge(s_z, n + 1)
                chain(nc.vector.tensor_tensor(wt[:, n % 2, :], zz[:, n % 2, :], ze[:, n % 2, :], ALU.mult))
                for k in range(TOP):
                    i = nc.vector.scalar_tensor_tensor(out=acc[:, b, :], in0=rows[:, n % NR, k, P:EMB], scalar=wt[:, n % 2, k:k + 1],
                                                       in1=acc[:, b, :], op0=ALU.mult, op1=ALU.add)
                    if k < TOP - 1:
                        chain(i)
                i.then_inc(s_used, 1)
                dve.wait_ge(s_used, n + 1)

            choose(0)
            choose(1)
            products(0)
            for n in range(len(chunks)):
                if n + 1 < len(chunks):
                    products(n + 1)
                weighted_sum(n)
            chain(nc.vector.tensor_tensor(env.x[:, :, :], env.x[:, :, :], acc[:, :, :], ALU.add))
    L.close()


NH2, LAT, ROT = 16, 64, 32
L2A = Fields([("Wa", KC * 3 * LAT), ("norm_q", LAT), ("norm_kv", LAT), ("Wqb", NH2 * P), ("Wqs", NH2 * LAT),
              ("Wkn", NH2 * LAT), ("Wvb", NH2 * LAT), ("Wo", 8 * D)])


def pack_L2A(i):
    p = "L2_attn_"
    kva = i[p + "wkv_a"]
    wa = np.concatenate([i[p + "wq_a"], kva[:, :LAT], kva[:, LAT::2], kva[:, LAT + 1::2]], 1)
    qb = i[p + "wq_b"].reshape(LAT, NH2, 2 * LAT)
    even, odd = qb[:, :, LAT::2], qb[:, :, LAT + 1::2]
    kvb = i[p + "wkv_b"].reshape(LAT, NH2, 2 * LAT)
    return [tiles(wa), every_row(i[p + "q_a_norm_w"]), every_row(i[p + "kv_a_norm_w"]),
            full(np.concatenate([qb[:, :, :LAT], even, odd], 2).reshape(LAT, NH2 * P)),
            full(np.concatenate([odd, even], 2).reshape(LAT, NH2 * LAT)),
            full(kvb[:, :, :LAT].reshape(LAT, NH2 * LAT)), full(kvb[:, :, LAT:].reshape(LAT, NH2 * LAT)),
            tiles(i[p + "wo"])]


def layer_L2A(env):
    L = Layer(env, "L2A")
    nc, w = env.nc, env.weights("L2A")
    wa = w("Wa").rearrange("p (k n) -> p k n", k=KC)
    SCALE, G = P ** -0.5, 4
    bank_x, bank_a, bank_v, bank_o = L.bank("xT"), L.bank("latent"), L.bank("v"), L.bank("out")
    bank_p = [L.bank(f"proj{j}") for j in range(2)]
    bank_s = [L.bank(f"scores{j}") for j in range(2)]
    head = Head(L, bank_x)
    la, sq = L.sb("latent", [P, B, 3 * LAT]), L.sb("squares", [P, B, 2, LAT])
    nq, nk = L.sb("q_latent", [P, B, LAT]), L.sb("kv_latent_and_rope", [P, B, P])
    rt = L.sb("rope_tmp", [P, B, LAT])
    ms = L.sb("mean_square", [P, 2, B])
    inv_q, inv_k = InvSqrt(L, "q_latent"), InvSqrt(L, "kv_latent")
    lT = L.sb("latentT", [P, 2, T])
    qT, kT = L.sb("qT", [P, NH2, T]), L.sb("kT", [P, NH2, T])
    qs = L.sb("q_rope_tmp", [P, 2, 2, T])
    v = L.sb("v", [P, B, NH2 * LAT])
    ex, pT = L.sb("exp", [P, 2, G, P]), L.sb("probsT", [P, 2, G * P])
    pn = L.sb("probs", [P, 2, G, P])
    mx, nmx, rsum, rinv = (L.sb(n, [P, 2, G]) for n in ("max", "neg_max", "row_sum", "inv_sum"))
    oT = L.sb("readT", [P, NH2 // 2, T])
    names = ("dve_chain", "latent_done", "latent_copied", "latents_normed", "latents_turned", "latentT_ready", "rope_keys_spread",
             "v_done", "v_copied", "k_done", "k_copied", "q_done", "q_swapped_done", "q_ready", "q_parts", "scores_done",
             "neg_max_ready", "exp_ready", "probs_ready", "probs_turned", "probsT_ready", "read_done", "read_copied", "out_done")
    (s_chain, s_la, s_lac, s_n, s_nt, s_lT, s_kr, s_v, s_vc, s_k, s_kc, s_q, s_qs, s_qr, s_qp, s_s, s_nm, s_e, s_pn, s_t, s_pT,
     s_o, s_oc, s_out) = (L.sem(n) for n in names)
    NU = NH2 // G * B
    units = [(b, g) for b in range(B) for g in range(NH2 // G)]
    NJ = NH2 // 2
    env.prefetch(L, "L2F")

    with L.block() as block:
        @block.sync
        def _(sp):
            env.issue_prefetch(sp)

        @block.tensor
        def _(pe):
            env.wait_weights(pe, "L2A")
            head.tensor(pe)
            pe.wait_ge(head.s_xT, 1)
            project(L, bank_a, wa, head.xT).then_inc(s_la, 1)
            pe.wait_ge(s_n, 1)
            for b in range(B):
                nc.tensor.transpose(bank_x[0:LAT, b * P:(b + 1) * P], nq[:, b, :], env.const("ident"))
                i = nc.tensor.transpose(bank_x[:, T + b * P:T + (b + 1) * P], nk[:, b, :], env.const("ident"))
            i.then_inc(s_nt, 1)
            pe.wait_ge(s_lT, 2)
            for j in range(NJ):
                if j >= 2:
                    pe.wait_ge(s_qp, 2 * (j - 1))
                for u in range(2):
                    h = 2 * j + u
                    i = nc.tensor.matmul(bank_p[j % 2][:, u * T:(u + 1) * T], w("Wqb")[0:LAT, h * P:(h + 1) * P], lT[0:LAT, 0, :],
                                         start=True, stop=True)
                i.then_inc(s_q, 1)
                for u in range(2):
                    h = 2 * j + u
                    i = nc.tensor.matmul(bank_s[j % 2][LAT:P, u * T:(u + 1) * T], w("Wqs")[0:LAT, h * LAT:(h + 1) * LAT],
                                         lT[0:LAT, 0, :], start=True, stop=True)
                i.then_inc(s_qs, 1)
                if j >= 1:
                    pe.wait_ge(s_kc, j)
                for u in range(2):
                    h = 2 * j + u
                    i = nc.tensor.matmul(bank_o[0:LAT, u * T:(u + 1) * T], w("Wkn")[0:LAT, h * LAT:(h + 1) * LAT],
                                         lT[0:LAT, 1, :], start=True, stop=True)
                i.then_inc(s_k, 1)
            for j in range(2 * B):
                b, half = divmod(j, 2)
                bank = bank_v if j % 2 else bank_a
                if j >= 2:
                    pe.wait_ge(s_vc, j - 1)
                nc.tensor.matmul(bank[:, :], lT[0:LAT, 1, b * P:(b + 1) * P], w("Wvb")[0:LAT, half * 512:(half + 1) * 512],
                                 start=True, stop=True).then_inc(s_v, 1)
            pe.wait_ge(s_qr, 1)
            pe.wait_ge(s_kc, NJ)
            pe.wait_ge(s_kr, 1)
            pe.wait_ge(s_vc, 2 * B)

            def scores(n):
                b, g = units[n]
                if n >= 2:
                    pe.wait_ge(s_e, n - 1)
                for u in range(G):
                    h = g * G + u
                    i = nc.tensor.matmul(bank_s[n % 2][:, u * P:(u + 1) * P], qT[:, h, b * P:(b + 1) * P],
                                         kT[:, h, b * P:(b + 1) * P], start=True, stop=True)
                i.then_inc(s_s, 1)

            def turn_probs(n):
                pe.wait_ge(s_pn, n + 1)
                if n >= 2:
                    pe.wait_ge(s_pT, n - 1)
                for u in range(G):
                    i = nc.tensor.transpose(bank_p[n % 2][:, u * P:(u + 1) * P], pn[:, n % 2, u, :], env.const("ident"))
                i.then_inc(s_t, 1)

            def read(n):
                b, g = units[n]
                pe.wait_ge(s_pT, n + 1)
                if n:
                    pe.wait_ge(s_oc, n)
                for u in range(G):
                    h, lo = g * G + u, (u % 2) * LAT
                    i = nc.tensor.matmul(bank_x[lo:lo + LAT, (u // 2) * P:(u // 2 + 1) * P], v[:, b, h * LAT:(h + 1) * LAT],
                                         pT[:, n % 2, u * P:(u + 1) * P], start=True, stop=True)
                i.then_inc(s_o, 1)

            scores(0)
            for n in range(NU):
                if n + 1 < NU:
                    scores(n + 1)
                turn_probs(n)
                if n:
                    read(n - 1)
            read(NU - 1)
            pe.wait_ge(s_oc, NU)
            for b in range(B):
                for j in range(NH2 // 2):
                    i = nc.tensor.matmul(bank_o[:, b * D:(b + 1) * D], oT[:, j, b * P:(b + 1) * P], w("Wo")[:, j * D:(j + 1) * D],
                                         start=(j == 0), stop=(j == NH2 // 2 - 1))
            i.then_inc(s_out, 1)

        @block.gpsimd
        def _(pool):
            head.gpsimd(pool)
            inv_q.gpsimd(pool)
            inv_k.gpsimd(pool)

        @block.scalar
        def _(act):
            head.scalar(act)
            act.wait_ge(s_la, 1)
            nc.scalar.activation(la[:, :, :].rearrange("p b n -> p (b n)"), bank_a[:, 0:B * 3 * LAT], ACT.Copy).then_inc(s_lac, 1)
            act.wait_ge(s_nt, 1)
            nc.scalar.activation(lT[0:LAT, 0, :], bank_x[0:LAT, 0:T], ACT.Copy).then_inc(s_lT, 1)
            nc.scalar.activation(lT[:, 1, :], bank_x[:, T:2 * T], ACT.Copy).then_inc(s_lT, 1)
            for j in range(NJ):
                act.wait_ge(s_k, j + 1)
                nc.scalar.activation(kT[0:LAT, 2 * j:2 * j + 2, :].rearrange("p h t -> p (h t)"), bank_o[0:LAT, :],
                                     ACT.Copy).then_inc(s_kc, 1)
            act.wait_ge(s_lT, 2)
            nc.scalar.activation(kT[LAT:P, :, :], lT[LAT:P, 1, :].unsqueeze(1).to_broadcast([LAT, NH2, T]), ACT.Copy).then_inc(s_kr, 1)
            for j in range(2 * B):
                b, half = divmod(j, 2)
                act.wait_ge(s_v, j + 1)
                nc.scalar.activation(v[:, b, half * 512:(half + 1) * 512], (bank_v if j % 2 else bank_a)[:, :], ACT.Copy).then_inc(s_vc, 1)

            def copy(n):
                act.wait_ge(s_t, n + 1)
                if n >= 2:
                    act.wait_ge(s_o, n - 1)
                nc.scalar.activation(pT[:, n % 2, :], bank_p[n % 2][:, :], ACT.Copy).then_inc(s_pT, 1)

            for n in range(NU):
                act.wait_ge(s_nm, n + 1)
                if n >= 2:
                    act.wait_ge(s_pn, n - 1)
                for u in range(G):
                    i = nc.scalar.activation(ex[:, n % 2, u, :], bank_s[n % 2][:, u * P:(u + 1) * P], ACT.Exp,
                                             bias=nmx[:, n % 2, u:u + 1], scale=SCALE, accum_out=rsum[:, n % 2, u:u + 1])
                i.then_inc(s_e, 1)
                if n:
                    copy(n - 1)
            copy(NU - 1)

        @block.vector
        def _(dve):
            chain = Chain(dve, s_chain)
            head.vector(dve, chain)
            dve.wait_ge(s_lac, 1)
            pair = la[:, :, 0:2 * LAT].rearrange("p b (m n) -> p b m n", m=2)
            chain(nc.vector.tensor_tensor(sq[:, :, :, :], pair, pair, ALU.mult))
            chain(nc.vector.tensor_reduce(ms[:, :, :], sq[:, :, :, :].rearrange("p b m n -> p m b n"), AX, ALU.add))
            chain(nc.vector.tensor_scalar(ms[:, :, :], ms[:, :, :], 1.0 / LAT, None, ALU.mult))
            kp = la[:, :, 2 * LAT:3 * LAT]
            cos, sin = (env.const(n).unsqueeze(1).to_broadcast([P, B, LAT]) for n in ("cos_tok", "sin_tok"))
            nc.vector.tensor_tensor(rt[:, :, 0:ROT], kp[:, :, ROT:LAT], sin[:, :, 0:ROT], ALU.mult)
            nc.vector.tensor_tensor(rt[:, :, ROT:LAT], kp[:, :, 0:ROT], sin[:, :, ROT:LAT], ALU.mult)
            chain(nc.vector.tensor_tensor(nk[:, :, LAT:P], kp, cos, ALU.mult))
            chain(nc.vector.tensor_tensor(nk[:, :, LAT:P], nk[:, :, LAT:P], rt[:, :, :], ALU.add))
            inv_q.vector(dve, ms[:, 0, :], 1e-6)
            inv_k.vector(dve, ms[:, 1, :], 1e-6)
            env.wait_weights(dve, "L2A")
            for b in range(B):
                nc.vector.scalar_tensor_tensor(out=nq[:, b, :], in0=la[:, b, 0:LAT], scalar=inv_q.out[:, b:b + 1],
                                               in1=w("norm_q"), op0=ALU.mult, op1=ALU.mult)
                i = nc.vector.scalar_tensor_tensor(out=nk[:, b, 0:LAT], in0=la[:, b, LAT:2 * LAT], scalar=inv_k.out[:, b:b + 1],
                                                   in1=w("norm_kv"), op0=ALU.mult, op1=ALU.mult)
            i.then_inc(s_n, 1)
            cos_r = env.const("cos_rows").unsqueeze(1).to_broadcast([P, 2 * B, P])
            sin_r = env.const("sin_rows")[LAT:P, :].unsqueeze(1).to_broadcast([LAT, 2 * B, P])
            for j in range(NJ):
                dve.wait_ge(s_q, j + 1)
                nc.vector.tensor_tensor(qT[:, 2 * j:2 * j + 2, :].rearrange("p h (b t) -> p (h b) t", b=B),
                                        bank_p[j % 2][:, :].rearrange("p (n t) -> p n t", t=P), cos_r, ALU.mult).then_inc(s_qp, 1)
                dve.wait_ge(s_qs, j + 1)
                t = qs[LAT:P, j % 2, :, :]
                nc.vector.tensor_tensor(t.rearrange("p h (b t) -> p (h b) t", b=B),
                                        bank_s[j % 2][LAT:P, :].rearrange("p (n t) -> p n t", t=P), sin_r, ALU.mult).then_inc(s_qp, 1)
                dve.wait_ge(s_qp, 2 * j + 2)
                rot = qT[LAT:P, 2 * j:2 * j + 2, :]
                i = nc.vector.tensor_tensor(rot, rot, t, ALU.add)
            i.then_inc(s_qr, 1)

            def maxima(n):
                dve.wait_ge(s_s, n + 1)
                chain(nc.vector.tensor_reduce(mx[:, n % 2, :], bank_s[n % 2][:, :].rearrange("p (h t) -> p h t", h=G), AX, ALU.max))
                if n >= 2:
                    dve.wait_ge(s_e, n - 1)
                nc.vector.tensor_scalar(nmx[:, n % 2, :], mx[:, n % 2, :], -SCALE, None, ALU.mult).then_inc(s_nm, 1)

            def normalise(n):
                dve.wait_ge(s_e, n + 1)
                chain(nc.vector.reciprocal(rinv[:, n % 2, :], rsum[:, n % 2, :]))
                if n >= 2:
                    dve.wait_ge(s_t, n - 1)
                nc.vector.tensor_tensor(pn[:, n % 2, :, :], ex[:, n % 2, :, :],
                                        rinv[:, n % 2, :].unsqueeze(2).to_broadcast([P, G, P]), ALU.mult).then_inc(s_pn, 1)

            def copy_read(n):
                b, g = units[n]
                dve.wait_ge(s_o, n + 1)
                nc.vector.tensor_copy(oT[:, 2 * g:2 * g + 2, b * P:(b + 1) * P],
                                      bank_x[:, 0:2 * P].rearrange("p (j t) -> p j t", j=2)).then_inc(s_oc, 1)

            maxima(0)
            for n in range(NU):
                if n + 1 < NU:
                    maxima(n + 1)
                normalise(n)
                if n:
                    copy_read(n - 1)
            copy_read(NU - 1)
            dve.wait_ge(s_out, 1)
            x = env.x[:, :, :].rearrange("p b d -> p (b d)")
            chain(nc.vector.tensor_tensor(x, x, bank_o[:, :], ALU.add))
    L.close()


FD = 64
L3X = Fields([("Wq", KC * D), ("Wk", KC * D), ("Wv", KC * D), ("Wo", KC * D), ("Wqf", 8 * FD), ("Wkf", 8 * FD),
              ("bq", KC), ("bk", KC), ("bv", D), ("bo", D)])


def pack_L3X(i):
    p = "L3_xattn_"
    return [tiles(i[f"{p}W{n}"].T) for n in "qkvo"] + [block_diag(i[f"{p}W{n}f"].T, 8) for n in "qk"] + \
        [per_channel(i[p + "bq"]), per_channel(i[p + "bk"]), every_row(i[p + "bv"]), every_row(i[p + "bo"])]


EXTRA_L3X = {"L3X_mask": lambda i: i["mask_BxS2_ff1"].reshape(B * NT, P).T}


def layer_L3X(env):
    L = Layer(env, "L3X")
    nc, w = env.nc, env.weights("L3X")
    wq, wk, wv = (w(n).rearrange("p (k n) -> p k n", k=KC) for n in ("Wq", "Wk", "Wv"))
    NH, VW, NPAIR = 16, 17, 8
    bank_x = L.bank("xT")
    bank_k = L.bank("k")
    bank_f = [L.bank(f"features{j}") for j in range(3)]
    bank_v = L.bank("v")
    bank_s = [L.bank(f"summary{b}") for b in range(B)]
    head = Head(L, bank_x)
    y = L.sb("y", [P, B, D])
    tail = Tail(L, y, bank_x, bank_k, w("Wo"), bias=w("bo"))
    mask = L.sb("mask", [P, B * NT])
    qT, qf = L.sb("qT", [P, KC, T]), L.sb("q_features", [P, NPAIR, T])
    kT = L.sb("kT", [P, 2, KC, 512])
    NB = 3
    kf, vo = L.sb("k_features", [P, NB, KC, 512]), L.sb("v_ones", [P, NB, NH, VW])
    kvm = L.sb("kv_blocks", [P, B, NPAIR, 2 * VW])
    z = L.sb("z", [P, NH])
    names = ("dve_chain", "mask_loaded", "q_done", "q_copied", "qf_done", "qf_copied", "k_done", "k_copied", "features_done",
             "features_ready", "v_done", "v_ready", "summary_step", "kv_blocks_ready", "attended")
    s_chain, s_mask, s_q, s_qc, s_qf, s_qfc, s_k, s_kc, s_f, s_fc, s_v, s_vc, s_sum, s_kvm, s_att = (L.sem(n) for n in names)
    steps = [(b, t) for b in range(B) for t in range(NT)]
    env.prefetch(L, "L3A")

    with L.block() as block:
        @block.sync
        def _(sp):
            sp.dma_start(mask[:, :], env.dram["L3X_mask"]).then_inc(s_mask, 16)
            env.issue_prefetch(sp)

        @block.tensor
        def _(pe):
            def keys(n):
                b, q = divmod(n, 4)
                env.wait_context(pe, b, 4 * q)
                for c in range(KC):
                    if 2 * n + c >= 1:
                        pe.wait_ge(s_kc, 2 * n + c)
                    for k in range(KC):
                        i = nc.tensor.matmul(bank_k[:, :], wk[:, k, c * P:(c + 1) * P], env.ctx4(k, b, q),
                                             start=(k == 0), stop=(k == KC - 1))
                    i.then_inc(s_k, 1)

            def features(n):
                b, t = steps[n]
                if t % 4 == 0:
                    pe.wait_ge(s_kc, 2 * (n // 4 + 1))
                for c in range(KC):
                    m = 2 * n + c
                    if m >= 3:
                        pe.wait_ge(s_fc, m - 2)
                    nc.tensor.matmul(bank_f[m % 3][:, :], kT[:, (n // 4) % 2, c, (t % 4) * P:(t % 4 + 1) * P], w("Wkf"),
                                     start=True, stop=True).then_inc(s_f, 1)
                if n >= 1:
                    pe.wait_ge(s_vc, n)
                for k in range(KC):
                    i = nc.tensor.matmul(bank_v[:, 0:D], env.ctx(k, b, t), wv[:, k, :], start=(k == 0), stop=(k == KC - 1))
                i.then_inc(s_v, 1)

            def summary(n):
                b, t = steps[n]
                pe.wait_ge(s_fc, 2 * n + 2)
                pe.wait_ge(s_vc, n + 1)
                for j in range(NPAIR):
                    c, at = j // 4, (j % 4) * P
                    i = nc.tensor.matmul(bank_s[b][:, j * 2 * VW:(j + 1) * 2 * VW], kf[:, n % NB, c, at:at + P],
                                         vo[:, n % NB, 2 * j:2 * j + 2, :].rearrange("p h e -> p (h e)"),
                                         start=(t == 0 and j == 0), stop=(t == NT - 1), skip_group_check=True)
                i.then_inc(s_sum, 1)

            env.wait_weights(pe, "L3X")
            head.tensor(pe)
            pe.wait_ge(head.s_xT, 1)
            project_T(L, bank_f[0], wq, head.xT).then_inc(s_q, 1)
            pe.wait_ge(s_qc, 1)
            for j in range(NPAIR // 2):
                if j >= 1:
                    pe.wait_ge(s_qfc, j)
                for u in range(2):
                    n = 2 * j + u
                    i = nc.tensor.matmul(bank_f[0][:, u * T:(u + 1) * T], w("Wqf")[:, (n % 4) * P:(n % 4 + 1) * P],
                                         qT[:, n // 4, :], start=True, stop=True)
                i.then_inc(s_qf, 1)
            keys(0)
            pe.wait_ge(s_qfc, NPAIR // 2)
            for n in range(len(steps)):
                features(n)
                if n % 4 == 0 and n // 4 + 1 < len(steps) // 4:
                    keys(n // 4 + 1)
                if n:
                    summary(n - 1)
            summary(len(steps) - 1)
            for b in range(B):
                pe.wait_ge(s_kvm, b + 1)
                for j in range(NPAIR):
                    i = nc.tensor.matmul(bank_s[b][:, j * 2 * VW:(j + 1) * 2 * VW], qf[:, j, b * P:(b + 1) * P], kvm[:, b, j, :],
                                         start=True, stop=True)
                i.then_inc(s_att, 1)
            tail.tensor(pe)

        @block.gpsimd
        def _(pool):
            head.gpsimd(pool)

        @block.scalar
        def _(act):
            env.wait_weights(act, "L3X")
            head.scalar(act)
            act.wait_ge(s_q, 1)
            for c in range(KC):
                i = nc.scalar.activation(qT[:, c, :], bank_f[0][:, c * T:(c + 1) * T], ACT.Identity, bias=w("bq")[:, c:c + 1])
            i.then_inc(s_qc, 1)
            for j in range(NPAIR // 2):
                act.wait_ge(s_qf, j + 1)
                nc.scalar.activation(qf[:, 2 * j:2 * j + 2, :].rearrange("p j t -> p (j t)"), bank_f[0][:, :], ACT.Relu).then_inc(s_qfc, 1)
            for n in range(len(steps) // 4):
                for c in range(KC):
                    act.wait_ge(s_k, 2 * n + c + 1)
                    if n >= 2:
                        act.wait_ge(s_f, 8 * (n - 1))
                    nc.scalar.activation(kT[:, n % 2, c, :], bank_k[:, :], ACT.Identity, bias=w("bk")[:, c:c + 1]).then_inc(s_kc, 1)
            tail.scalar(act)

        @block.vector
        def _(dve):
            chain = Chain(dve, s_chain)
            nc.vector.memset(vo[:, :, :, 16:17], 1.0)
            head.vector(dve, chain)
            env.wait_weights(dve, "L3X")
            dve.wait_ge(s_mask, 16)
            bv = w("bv").rearrange("p (h e) -> p h e", h=NH)

            def blocks(b):
                dve.wait_ge(s_sum, NT * (b + 1))
                nc.vector.tensor_tensor(kvm[:, b, :, :], bank_s[b][:, 0:NPAIR * 2 * VW].rearrange("p (j e) -> p j e", j=NPAIR),
                                        env.const("pair64").unsqueeze(1).to_broadcast([P, NPAIR, 2 * VW]), ALU.mult).then_inc(s_kvm, 1)

            for n in range(len(steps)):
                for c in range(KC):
                    dve.wait_ge(s_f, 2 * n + c + 1)
                    if n >= NB:
                        dve.wait_ge(s_sum, n - NB + 1)
                    nc.vector.tensor_scalar(kf[:, n % NB, c, :], bank_f[(2 * n + c) % 3][:, :], 0.0, mask[:, n:n + 1], ALU.max,
                                            ALU.mult).then_inc(s_fc, 1)
                dve.wait_ge(s_v, n + 1)
                nc.vector.tensor_tensor(vo[:, n % NB, :, 0:16], bank_v[:, 0:D].rearrange("p (h e) -> p h e", h=NH), bv,
                                        ALU.add).then_inc(s_vc, 1)
                if n == NT + 2:
                    blocks(0)
            blocks(1)
            for b in range(B):
                dve.wait_ge(s_att, b + 1)
                o = bank_s[b][:, 0:NH * VW].rearrange("p (h e) -> p h e", h=NH)
                chain(nc.vector.tensor_scalar(z[:, :], o[:, :, 16], 1e-8, None, ALU.add))
                chain(nc.vector.reciprocal(z[:, :], z[:, :]))
                nc.vector.tensor_tensor(y[:, b, :].rearrange("p (h e) -> p h e", h=NH), o[:, :, 0:16],
                                        z[:, :].unsqueeze(2).to_broadcast([P, NH, 16]), ALU.mult).then_inc(tail.s_y, 1)
                dve.wait_ge(tail.s_y, b + 1)
            tail.vector(dve, chain)
    L.close()


L3A = Fields([("Wq", KC * D), ("Wk", KC * D), ("Wv", KC * D), ("Wo", KC * D)])


def pack_L3A(i):
    return [tiles(i[f"L3_attn_W{n}"].T) for n in "qkvo"]


def layer_L3A(env):
    L = Layer(env, "L3A")
    nc, w = env.nc, env.weights("L3A")
    wq, wk, wv = (w(n).rearrange("p (k n) -> p k n", k=KC) for n in ("Wq", "Wk", "Wv"))
    bank_x, bank_v = L.bank("xT"), L.bank("v")
    bank_s, bank_t, bank_o = ([L.bank(f"{n}{j}") for j in range(2)] for n in ("scores", "turn", "read"))
    head = Head(L, bank_x)
    y = L.sb("y", [P, B, D])
    tail = Tail(L, y, bank_x, bank_v, w("Wo"))
    at = SmallAttention(L, 16, bank_s, bank_t, bank_o, lambda b: env.const("causal"))
    s_chain, s_q, s_k, s_v, s_kc, s_vc = (L.sem(n) for n in ("dve_chain", "q_done", "k_done", "v_done", "k_copied", "v_copied"))
    env.prefetch(L, "L3F")

    with L.block() as block:
        @block.sync
        def _(sp):
            env.issue_prefetch(sp)

        @block.tensor
        def _(pe):
            env.wait_weights(pe, "L3A")
            head.tensor(pe)
            pe.wait_ge(head.s_xT, 1)
            project_T(L, bank_t[0], wq, head.xT).then_inc(s_q, 1)
            project_T(L, bank_t[1], wk, head.xT).then_inc(s_k, 1)
            project(L, bank_v, wv, head.xT).then_inc(s_v, 1)
            pe.wait_ge(s_kc, 1)
            for b in range(B):
                if b == 0:
                    pe.wait_ge(s_vc, 1)
                at.tensor(pe, b)
            tail.tensor(pe)

        @block.gpsimd
        def _(pool):
            head.gpsimd(pool)

        @block.scalar
        def _(act):
            head.scalar(act)
            act.wait_ge(s_k, 1)
            nc.scalar.activation(at.kT[:, :, :].rearrange("p c t -> p (c t)"), bank_t[1][:, :], ACT.Copy).then_inc(s_kc, 1)
            for b in range(B):
                at.scalar(act, b)
            tail.scalar(act)

        @block.vector
        def _(dve):
            chain = Chain(dve, s_chain)
            nc.vector.memset(at.vo[:, :, :, 16:17], 1.0)
            head.vector(dve, chain)
            dve.wait_ge(s_q, 1)
            chain(nc.vector.tensor_copy(at.qT[:, :, :].rearrange("p c t -> p (c t)"), bank_t[0][:, :]))
            at.query_blocks(0)
            dve.wait_ge(s_v, 1)
            nc.vector.tensor_copy(at.vo[:, :, :, 0:16], bank_v[:, :].rearrange("p (b h e) -> p b h e", b=B, h=16)).then_inc(s_vc, 1)
            for b in range(B):
                at.vector(dve, chain, b)
                if b == 0:
                    dve.wait_ge(at.s_s, at.per)
                    at.query_blocks(1)
                at.finish(dve, chain, b, y).then_inc(tail.s_y, 1)
            tail.vector(dve, chain)
    L.close()


NEXP, FE, EG, NGROUP = 64, 96, 8, 8
KEEP_GROUPS, KEEP = 4, 6
CAP = 2 * (T * KEEP // NEXP)
PER = 4
HJ = PER * FE
NJOB = NEXP // PER
JOBW = 2 * KC * HJ + (HJ // P) * D
L3F = Fields([("gate_w", KC * NEXP), ("bias", NEXP), ("s_gate", KC * FE), ("s_up", KC * FE), ("s_down", D)])


def pack_L3F(i):
    p = "L3_ffn_"
    return [tiles(i[p + "gate_w"]), every_row(i[p + "bias"]), tiles(i[p + "ws_gate"]), tiles(i[p + "ws_up"]),
            full(i[p + "ws_down"])]


def expert_jobs(i):
    p = "L3_ffn_"
    gu = [i[p + n].reshape(NJOB, PER, KC, P, FE).transpose(0, 3, 2, 1, 4).reshape(NJOB, P, KC * HJ) for n in ("w_gate", "w_up")]
    down = i[p + "w_down"].reshape(NJOB, HJ // P, P, D).transpose(0, 2, 1, 3).reshape(NJOB, P, (HJ // P) * D)
    return np.concatenate(gu + [down], 2)


EXTRA_L3F = {"L3F_experts": expert_jobs}


def layer_L3F(env):
    L = Layer(env, "L3F")
    nc, w = env.nc, env.weights("L3F")
    wr = w("gate_w").rearrange("p (k n) -> p k n", k=KC)
    bank_x, bank_r, bank_y = L.bank("xT_and_turn1"), L.bank("router_and_turn0"), L.bank("y")
    bank_g, bank_u = ([L.bank(f"{n}{j}") for j in range(2)] for n in ("gate", "up"))
    bank_t = [bank_r, bank_x]
    head = Head(L, bank_x)
    NR = 5
    ring = L.sb("expert_weights", [P, NR, JOBW])
    sc, sb, t64 = L.sb("scores", [P, B, NEXP]), L.sb("biased", [P, B, NEXP]), L.sb("masked", [P, B, NEXP])
    m8 = L.sb("group_top", [P, B, NGROUP, 8])
    gs, gr, t8 = L.sb("group_scores", [P, B, NGROUP]), L.sb("group_mask", [P, B, NGROUP]), L.sb("top8", [P, B, 8])
    sel, comb, tot = L.sb("chosen", [P, B, NEXP]), L.sb("combine", [P, B, NEXP + 1]), L.sb("weight_sum", [P, B])
    NB = 3
    e, a, c2, h = (L.sb(n, [P, NB, HJ]) for n in ("tanh", "silu", "weighted_up", "hidden"))
    hT = L.sb("hiddenT", [P, 2, HJ])
    s_w = [L.sem(f"experts_loaded{r}") for r in range(NR)]
    names = ("dve_chain", "router_done", "router_exp", "chosen_ready", "ranks_done", "gate_done", "up_done", "tanh_ready", "gate_used",
             "up_used", "hidden_ready", "turned", "hiddenT_ready", "y_step")
    (s_chain, s_r, s_re, s_sel, s_rank, s_g, s_u, s_e, s_gu, s_uu, s_h, s_t, s_hT, s_y) = (L.sem(n) for n in names)
    units = [(j, b) for j in range(-1, NJOB) for b in range(B)]
    NU = len(units)
    env.prefetch(L, None)

    def width(n):
        return FE if units[n][0] < 0 else HJ

    with L.block() as block:
        @block.sync
        def _(sp):
            env.issue_prefetch(sp)
            for j in range(NJOB):
                if j >= NR:
                    sp.wait_ge(s_y, (j - NR + 1) * B + B)
                sp.dma_start(ring[:, j % NR, :], env.dram["L3F_experts"][j]).then_inc(s_w[j % NR], 16)

        @block.tensor
        def _(pe):
            def weights(j):
                if j < 0:
                    return tuple(w(n).rearrange("p (k n) -> p k n", k=KC) for n in ("s_gate", "s_up")) + \
                        (w("s_down")[0:FE, :].unsqueeze(1),)
                s = ring[:, j % NR, :]
                return tuple(s[:, m * KC * HJ:(m + 1) * KC * HJ].rearrange("p (k n) -> p k n", k=KC) for m in range(2)) + \
                    (s[:, 2 * KC * HJ:].rearrange("p (m d) -> p m d", d=D),)

            def up(n):
                j, b = units[n]
                if j >= 0 and b == 0:
                    pe.wait_ge(s_w[j % NR], 16 * (j // NR + 1))
                wg, wu, _ = weights(j)
                for wt, bank, s, used in ((wg, bank_g, s_g, s_gu), (wu, bank_u, s_u, s_uu)):
                    if n >= 2:
                        pe.wait_ge(used, n - 1)
                    for k in range(KC):
                        i = nc.tensor.matmul(bank[n % 2][:, 0:width(n)], head.xT[:, k, b * P:(b + 1) * P], wt[:, k, :],
                                             start=(k == 0), stop=(k == KC - 1))
                    i.then_inc(s, 1)

            def turn_hidden(n):
                pe.wait_ge(s_h, n + 1)
                if n >= 2:
                    pe.wait_ge(s_hT, n - 1)
                if units[n][0] < 0:
                    i = nc.tensor.transpose(bank_t[n % 2][0:FE, 0:P], h[:, n % NB, 0:FE], env.const("ident"))
                else:
                    for m in range(HJ // P):
                        i = nc.tensor.transpose(bank_t[n % 2][:, m * P:(m + 1) * P], h[:, n % NB, m * P:(m + 1) * P], env.const("ident"))
                i.then_inc(s_t, 1)

            def down(n):
                j, b = units[n]
                pe.wait_ge(s_hT, n + 1)
                wd = weights(j)[2]
                rows, tiles_n = (FE, 1) if j < 0 else (P, HJ // P)
                for m in range(tiles_n):
                    i = nc.tensor.matmul(bank_y[:, b * D:(b + 1) * D], hT[0:rows, n % 2, m * P:(m + 1) * P], wd[:, m, :],
                                         start=(n == 0), stop=(j == NJOB - 1 and m == tiles_n - 1), skip_group_check=True)
                i.then_inc(s_y, 1)

            env.wait_weights(pe, "L3F")
            head.tensor(pe)
            pe.wait_ge(head.s_xT, 1)
            project(L, bank_r, wr, head.xT).then_inc(s_r, 1)
            up(0)
            up(1)
            pe.wait_ge(s_sel, 1)
            for b in range(B):
                o = bank_r[:, b * NEXP:(b + 1) * NEXP]
                i = nc.tensor.matmul(o, env.const("before"), sel[:, b, :], start=True, stop=(b == 0))
                if b:
                    i = nc.tensor.matmul(o, env.const("ones"), sel[:, 0, :], start=False, stop=True)
            i.then_inc(s_rank, 1)
            pe.wait_ge(s_h, 1)
            for n in range(NU):
                turn_hidden(n)
                if n + 2 < NU:
                    up(n + 2)
                down(n)

        @block.gpsimd
        def _(pool):
            head.gpsimd(pool)

        @block.scalar
        def _(act):
            head.scalar(act)
            act.wait_ge(s_r, 1)
            nc.scalar.activation(sc[:, :, :].rearrange("p b n -> p (b n)"), bank_r[:, 0:B * NEXP], ACT.Exp, scale=-1.0).then_inc(s_re, 1)

            def tanhs(n):
                act.wait_ge(s_g, n + 1)
                if n >= NB:
                    act.wait_ge(s_gu, n - NB + 1)
                nc.scalar.activation(e[:, n % NB, 0:width(n)], bank_g[n % 2][:, 0:width(n)], ACT.Tanh, scale=0.5).then_inc(s_e, 1)

            tanhs(0)
            tanhs(1)
            for n in range(NU):
                act.wait_ge(s_t, n + 1)
                if n >= 2:
                    act.wait_ge(s_y, n - 1)
                rows, cols = (FE, P) if units[n][0] < 0 else (P, HJ)
                nc.scalar.activation(hT[0:rows, n % 2, 0:cols], bank_t[n % 2][0:rows, 0:cols], ACT.Copy).then_inc(s_hT, 1)
                if n + 2 < NU:
                    tanhs(n + 2)

        @block.vector
        def _(dve):
            chain = Chain(dve, s_chain)
            head.vector(dve, chain)
            dve.wait_ge(s_re, 1)
            chain(nc.vector.tensor_scalar(sc[:, :, :], sc[:, :, :], 1.0, None, ALU.add))
            chain(nc.vector.reciprocal(sc[:, :, :], sc[:, :, :]))
            env.wait_weights(dve, "L3F")
            chain(nc.vector.tensor_tensor(sb[:, :, :], sc[:, :, :], w("bias").unsqueeze(1).to_broadcast([P, B, NEXP]), ALU.add))
            for b in range(B):
                for g in range(NGROUP):
                    i = nc.vector.max(m8[:, b, g, :], sb[:, b, g * EG:(g + 1) * EG])
            chain(i)
            chain(nc.vector.tensor_tensor(gs[:, :, :], m8[:, :, :, 0], m8[:, :, :, 1], ALU.add))

            def choose(dst, src, count, taken):
                for b in range(B):
                    i = nc.vector.max(t8[:, b, :], src[:, b, :])
                chain(i)
                chain(nc.vector.memset(t8[:, :, count:8], -taken))
                for b in range(B):
                    i = nc.vector.match_replace(out=dst[:, b, :], in_to_replace=t8[:, b, :], in_values=src[:, b, :], imm_value=taken)
                chain(i)
                return nc.vector.tensor_scalar(dst[:, :, :], dst[:, :, :], taken / 2, None, ALU.is_lt)

            chain(choose(gr, gs, KEEP_GROUPS, 4 * NEG_LARGE))
            g4 = gr[:, :, :].rearrange("p b g -> p (b g)").unsqueeze(2).to_broadcast([P, B * NGROUP, EG])
            tv = t64[:, :, :].rearrange("p b (g n) -> p (b g) n", g=NGROUP)
            chain(nc.vector.tensor_tensor(tv, sb[:, :, :].rearrange("p b (g n) -> p (b g) n", g=NGROUP), g4, ALU.mult))
            chain(nc.vector.tensor_scalar(gr[:, :, :], gr[:, :, :], -1.0, -NEG_LARGE, ALU.add, ALU.mult))
            chain(nc.vector.tensor_tensor(tv, tv, g4, ALU.add))
            choose(sel, t64, KEEP, 4 * NEG_LARGE).then_inc(s_sel, 1)
            dve.wait_ge(s_sel, 1)
            cb = comb[:, :, 0:NEXP]
            chain(nc.vector.tensor_tensor(cb, sc[:, :, :], sel[:, :, :], ALU.mult))
            chain(nc.vector.tensor_reduce(tot[:, :], cb, AX, ALU.add))
            chain(nc.vector.reciprocal(tot[:, :], tot[:, :]))
            for b in range(B):
                i = nc.vector.tensor_scalar(comb[:, b, 0:NEXP], comb[:, b, 0:NEXP], tot[:, b:b + 1], 2.5 / 2, ALU.mult, ALU.mult)
            chain(i)
            dve.wait_ge(s_rank, 1)
            rank = bank_r[:, 0:B * NEXP].rearrange("p (b n) -> p b n", b=B)
            chain(nc.vector.scalar_tensor_tensor(out=cb, in0=rank, scalar=float(CAP), in1=cb, op0=ALU.is_lt, op1=ALU.mult))
            for n in range(NU):
                j, b = units[n]
                s, wd = n % NB, width(n)
                dve.wait_ge(s_e, n + 1)
                if n >= NB:
                    dve.wait_ge(s_t, n - NB + 1)
                nc.vector.scalar_tensor_tensor(out=a[:, s, 0:wd], in0=e[:, s, 0:wd], scalar=1.0, in1=bank_g[n % 2][:, 0:wd],
                                               op0=ALU.add, op1=ALU.mult).then_inc(s_gu, 1)
                dve.wait_ge(s_u, n + 1)
                if j < 0:
                    nc.vector.tensor_scalar(c2[:, s, 0:wd], bank_u[n % 2][:, 0:wd], 0.5, None, ALU.mult).then_inc(s_uu, 1)
                else:
                    nc.vector.tensor_tensor(c2[:, s, :].rearrange("p (x f) -> p x f", f=FE),
                                            bank_u[n % 2][:, 0:HJ].rearrange("p (x f) -> p x f", f=FE),
                                            comb[:, b, j * PER:(j + 1) * PER].unsqueeze(2).to_broadcast([P, PER, FE]),
                                            ALU.mult).then_inc(s_uu, 1)
                dve.wait_ge(s_gu, n + 1)
                dve.wait_ge(s_uu, n + 1)
                nc.vector.tensor_tensor(h[:, s, 0:wd], a[:, s, 0:wd], c2[:, s, 0:wd], ALU.mult).then_inc(s_h, 1)
            dve.wait_ge(s_y, NU)
            x = env.x[:, :, :].rearrange("p b d -> p (b d)")
            chain(nc.vector.tensor_tensor(x, x, bank_y[:, :], ALU.add))
    L.close()


PACKED = {"L0X": (L0X, pack_L0X), "L0A": (L0A, pack_L0A), "L0F": (L0F, pack_L0F), "L1X": (L1X, pack_L1X),
          "L1A": (L1A, pack_L1A), "L1F": (L1F, pack_L1F), "L2X": (L2X, pack_L2X), "L2A": (L2A, pack_L2A),
          "L2F": (L2F, pack_L2F), "L3X": (L3X, pack_L3X), "L3A": (L3A, pack_L3A), "L3F": (L3F, pack_L3F)}
EXTRA = {"L1X": EXTRA_L1X, "L1A": EXTRA_L1A, "L2X": EXTRA_L2X, "L2F": EXTRA_L2F, "L3X": EXTRA_L3X, "L3F": EXTRA_L3F}
LAYERS = {"L0X": layer_L0X, "L0A": layer_L0A, "L0F": layer_L0F, "L1X": layer_L1X, "L1A": layer_L1A, "L1F": layer_L1F,
          "L2X": layer_L2X, "L2A": layer_L2A, "L2F": layer_L2F, "L3X": layer_L3X, "L3A": layer_L3A, "L3F": layer_L3F}


ORDER = ["L0X", "L0A", "L0F", "L1X", "L1A", "L1F", "L2X", "L2A", "L2F", "L3X", "L3A", "L3F"]
SLOT = 30 * 256


class Env:

    def __init__(self, nc, stack, dram, const_fields):
        self.nc, self.stack, self.dram, self.cf = nc, stack, dram, const_fields
        self.x = stack.enter_context(nc.sbuf_tensor("x", [P, B, D], F32))
        self.ctxT = stack.enter_context(nc.sbuf_tensor("ctxT", [P, B, 4, KC, S2 // 4], F32))
        self.consts = stack.enter_context(nc.sbuf_tensor("consts", [P, const_fields.n], F32))
        self.slots = [stack.enter_context(nc.sbuf_tensor(f"slot{j}", [P, SLOT], F32)) for j in range(2)]
        self.s_start = stack.enter_context(nc.semaphore("x_and_consts_loaded"))
        self.s_ctx = [stack.enter_context(nc.semaphore(f"context_loaded{j}")) for j in range(B * 4)]
        self.s_w = {n: stack.enter_context(nc.semaphore(f"weights_{n}_loaded")) for n in self.order if n in PACKED}
        self.s_out = stack.enter_context(nc.semaphore("out_stored"))
        self.next = None

    order = ORDER

    def const(self, name):
        return self.cf.view(self.consts, name)

    def ctx(self, k, b, t):
        q, r = t // 4, t % 4
        return self.ctxT[:, b, q, k, r * P:(r + 1) * P]

    def ctx4(self, k, b, q):
        return self.ctxT[:, b, q, k, :]

    def wait_context(self, eng, b, t):
        if t % 4 == 0:
            eng.wait_ge(self.s_ctx[b * 4 + t // 4], 16)

    def slot(self, name):
        return self.slots[self.order.index(name) % 2]

    def weights(self, name):
        f = PACKED[name][0]
        return lambda field: f.view(self.slot(name), field)

    def wait_weights(self, eng, name):
        eng.wait_ge(self.s_w[name], 16)

    def load_weights(self, sp, name):
        n = PACKED[name][0].n
        assert n <= SLOT, (name, n)
        sp.dma_start(self.slot(name)[:, 0:n], self.dram[name]).then_inc(self.s_w[name], 16)

    def prefetch(self, L, name):
        i = self.order.index(L.name) + 1
        self.next = self.order[i] if i < len(self.order) else None

    def issue_prefetch(self, sp):
        if self.next in PACKED:
            self.load_weights(sp, self.next)


def build(nc, dram, out):
    cf = Fields([(n, a.shape[1]) for n, a in constants().items()])
    with ExitStack() as stack:
        env = Env(nc, stack, dram, cf)
        with nc.Block("load") as block:
            @block.sync
            def _(sp):
                sp.dma_start(env.x[:, :, :], dram["x"].rearrange("b p d -> p b d")).then_inc(env.s_start, 16)
                sp.dma_start(env.consts[:, :], dram["consts"]).then_inc(env.s_start, 16)
                if env.order[0] in PACKED:
                    env.load_weights(sp, env.order[0])
                for j in range(B * 4):
                    sp.dma_start(env.ctxT[:, j // 4, j % 4, :, :],
                                 dram["ctxT"][j].rearrange("p (k t) -> p k t", k=KC)).then_inc(env.s_ctx[j], 16)
                sp.wait_ge(env.s_start, 32)
        for name in env.order:
            LAYERS[name](env)
        with nc.Block("store") as block:
            @block.sync
            def _(sp):
                sp.dma_start(out.rearrange("b p d -> p b d"), env.x[:, :, :]).then_inc(env.s_out, 16)
                sp.wait_ge(env.s_out, 16)
                for j in range(B * 4):
                    sp.wait_ge(env.s_ctx[j], 16)


def kernel(**inputs):
    import concourse.bacc as _bacc
    from concourse import mybir as _mybir
    from concourse.bass_utils import run_bass_kernel_spmd as _run

    i = {k: np.asarray(v) for k, v in inputs.items()}
    arrays = {"x": i["x"], "consts": np.ascontiguousarray(np.concatenate(list(constants().values()), 1))}
    arrays["ctxT"] = np.ascontiguousarray(
        i["ctx_2048"].reshape(B, 4, S2 // 4, KC, P).transpose(0, 1, 4, 3, 2).reshape(B * 4, P, KC * (S2 // 4)))
    for name in ORDER:
        if name in PACKED:
            arrays[name] = np.ascontiguousarray(np.concatenate(PACKED[name][1](i), 1))
        for extra, make in EXTRA.get(name, {}).items():
            arrays[extra] = np.ascontiguousarray(make(i))
    nc = _bacc.Bacc("TRN2", target_bir_lowering=False, num_devices=1)
    arrays = {f"in_{k}_dram": v for k, v in arrays.items()}
    dram = {k[3:-5]: nc.dram_tensor(k, v.shape, _mybir.dt.from_np(v.dtype), kind="ExternalInput").ap()
            for k, v in arrays.items()}
    out = nc.dram_tensor("out_0_dram", (B, P, D), F32, kind="ExternalOutput").ap()
    build(nc, dram, out)
    r = _run(nc, [arrays], core_ids=[0])
    return r.results[0]["out_0_dram"]
```
